# Optimizing a Trainium2 kernel written in Bass

```python
import numpy as np
import jax
import jax.numpy as jnp

def _softmax(x, axis=-1):
    return jax.nn.softmax(x, axis=axis)

def _gelu(x):
    return jax.nn.gelu(x, approximate=True)

def _silu(x):
    return jax.nn.silu(x)

def _sigmoid(x):
    return jax.nn.sigmoid(x)

def _layernorm(x, axis=-1, eps=1e-05):
    m = jnp.mean(x, axis=axis, keepdims=True)
    v = jnp.var(x, axis=axis, keepdims=True)
    return (x - m) / jnp.sqrt(v + eps)

def _scatter_add(tgt, idx, src, axis=0):
    return tgt.at[idx].add(src)

def _segment_sum(src, seg, n):
    return jax.ops.segment_sum(src, seg, n)
kernel_name = 'mk_gnn_resnorm_d4_gnn_r32_ffe78d'

def setup_inputs(seed: int=0):
    np.random.seed(seed)
    _w = jnp.asarray

    def _rec_inputs():
        import jax
        import jax.numpy as jnp
        _gk = jax.random.key(seed)
        x = -0.000202 + 1 * jax.random.normal(jax.random.fold_in(_gk, 1), (3125, 128), jnp.float32)
        _s = jax.random.randint(jax.random.fold_in(_gk, 2), (25000,), 0, 3125, jnp.int32)
        _d = jax.random.randint(jax.random.fold_in(_gk, 3), (25000,), 0, 3125, jnp.int32)
        _loop = jnp.arange(3125, dtype=jnp.int32)
        src = jnp.concatenate([_s, _d, _loop])
        dst = jnp.concatenate([_d, _s, _loop])
        _o = jnp.argsort(dst, stable=True)
        src = src[_o]
        dst = dst[_o]
        edge_attr_128 = -5.16925e-05 + 1.00005 * jax.random.normal(jax.random.fold_in(_gk, 12), (53125, 128), jnp.float32)
        edge_attr_64 = 0.000196303 + 1.00016 * jax.random.normal(jax.random.fold_in(_gk, 13), (53125, 64), jnp.float32)
        return (x, src, dst, edge_attr_128, edge_attr_64)
    x, src, dst, edge_attr_128, edge_attr_64 = _rec_inputs()

    def _L0_gnn_setup():
        import jax, jax.numpy as jnp
        import numpy as np
        N, E = (50000, 12500)
        NODE_DIM, EDGE_DIM = (128, 64)
        MSG_IN = 2 * NODE_DIM + EDGE_DIM
        key = jax.random.key(seed)
        ks = jax.random.split(key, 12)
        h = jax.random.normal(ks[0], (N, NODE_DIM), dtype=jnp.float32)
        edge_index = jax.random.randint(ks[1], (2, E), 0, N, dtype=jnp.int64)
        e = jax.random.normal(ks[2], (E, EDGE_DIM), dtype=jnp.float32)

        def lin(k, fan_in, fan_out):
            bound = 1.0 / np.sqrt(fan_in)
            k1, k2 = jax.random.split(k)
            w = jax.random.uniform(k1, (fan_in, fan_out), minval=-bound, maxval=bound, dtype=jnp.float32)
            b = jax.random.uniform(k2, (fan_out,), minval=-bound, maxval=bound, dtype=jnp.float32)
            return (w, b)
        w1, b1 = lin(ks[3], MSG_IN, NODE_DIM)
        w2, b2 = lin(ks[4], NODE_DIM, NODE_DIM)
        wg, bg = lin(ks[5], MSG_IN, NODE_DIM)
        wu, bu = lin(ks[6], 2 * NODE_DIM, NODE_DIM)
        return {'h': h, 'edge_index': edge_index, 'e': e, 'w1': w1, 'b1': b1, 'w2': w2, 'b2': b2, 'wg': wg, 'bg': bg, 'wu': wu, 'bu': bu}
    _L0_gnn_all = _L0_gnn_setup()
    _L0_gnn_in = {k: v for k, v in _L0_gnn_all.items() if k in ('w1', 'b1', 'w2', 'b2', 'wg', 'bg', 'wu', 'bu')}
    del _L0_gnn_all

    def _L1_gnn_setup():
        import jax, jax.numpy as jnp
        import numpy as np
        N_NODES = 3125
        N_EDGES = 50000
        D_IN = 128
        D_OUT = 128
        key = jax.random.key(seed)
        k1, k2, k3, k4, k5 = jax.random.split(key, 5)
        feat = jax.random.normal(k1, (N_NODES, D_IN), dtype=jnp.float32)
        W_neigh = jax.random.normal(k2, (D_IN, D_OUT), dtype=jnp.float32) * (1.0 / np.sqrt(D_IN))
        W_self = jax.random.normal(k3, (D_IN, D_OUT), dtype=jnp.float32) * (1.0 / np.sqrt(D_IN))
        b_self = jnp.zeros((D_OUT,), dtype=jnp.float32)
        src = jax.random.randint(k4, (N_EDGES,), 0, N_NODES, dtype=jnp.int32)
        dst = jnp.sort(jax.random.randint(k5, (N_EDGES,), 0, N_NODES, dtype=jnp.int32))
        return {'feat': feat, 'W_neigh': W_neigh, 'W_self': W_self, 'b_self': b_self, 'src': src, 'dst': dst}
    _L1_gnn_all = _L1_gnn_setup()
    _L1_gnn_in = {k: v for k, v in _L1_gnn_all.items() if k in ('W_neigh', 'W_self', 'b_self')}
    del _L1_gnn_all

    def _L2_gnn_setup():
        import jax, jax.numpy as jnp
        import numpy as np
        N, E = (50000, 25000)
        F_IN, HID, SENT = (128, 128, 128)
        NEG_SLOPE = 0.2

        def _glorot(key, shape):
            fan_in, fan_out = (shape[0], shape[-1])
            lim = float(np.sqrt(6.0 / (fan_in + fan_out)))
            return jax.random.uniform(key, shape, jnp.float32, -lim, lim)

        def _gat_layer(x, src, dst, edge_attr, W, att_s, att_d, We, att_e, b):
            n = x.shape[0]
            deg = jax.ops.segment_sum(jnp.ones(src.shape[0], x.dtype), dst, num_segments=n)
            loop_attr = jax.ops.segment_sum(edge_attr, dst, num_segments=n) / jnp.maximum(deg, 1.0)[:, None]
            loops = jnp.arange(n, dtype=src.dtype)
            src = jnp.concatenate([src, loops])
            dst = jnp.concatenate([dst, loops])
            ea = jnp.concatenate([edge_attr, loop_attr], axis=0)
            h = x @ W
            a_s = h @ att_s
            a_d = h @ att_d
            a_e = ea @ We @ att_e
            alpha = jax.nn.leaky_relu(a_s[src] + a_d[dst] + a_e, NEG_SLOPE)
            m = jax.ops.segment_max(alpha, dst, num_segments=n)
            ex = jnp.exp(alpha - m[dst])
            w = ex / jax.ops.segment_sum(ex, dst, num_segments=n)[dst]
            return jax.ops.segment_sum(w[:, None] * h[src], dst, num_segments=n) + b
        key = jax.random.key(seed)
        ks = jax.random.split(key, 16)
        x = jax.random.normal(ks[0], (N, F_IN), jnp.float32)
        edge_index = jax.random.randint(ks[1], (2, E), 0, N, jnp.int64)
        edge_attr = jax.random.normal(ks[2], (E, SENT), jnp.float32)
        params = {'W1': _glorot(ks[3], (F_IN, HID)), 'a1s': _glorot(ks[4], (HID,)), 'a1d': _glorot(ks[5], (HID,)), 'We1': _glorot(ks[6], (SENT, HID)), 'ae1': _glorot(ks[7], (HID,)), 'b1': jnp.zeros((HID,), jnp.float32), 'W2': _glorot(ks[8], (HID, HID)), 'a2s': _glorot(ks[9], (HID,)), 'a2d': _glorot(ks[10], (HID,)), 'We2': _glorot(ks[11], (SENT, HID)), 'ae2': _glorot(ks[12], (HID,)), 'b2': jnp.zeros((HID,), jnp.float32)}
        return {'x': x, 'edge_index': edge_index, 'edge_attr': edge_attr, **params}
    _L2_gnn_all = _L2_gnn_setup()
    _L2_gnn_in = {k: v for k, v in _L2_gnn_all.items() if k in ('W1', 'a1s', 'a1d', 'We1', 'ae1', 'b1', 'W2', 'a2s', 'a2d', 'We2', 'ae2', 'b2')}
    del _L2_gnn_all

    def _L3_gnn_setup():
        import jax, jax.numpy as jnp
        import numpy as np
        N = 50000
        E = 18750
        D = 128
        LN_EPS = 1e-05

        def _sage_layer(x, src, dst, W_l, b_l, W_r, gamma, beta):
            n = x.shape[0]
            msg = x[src]
            summed = jax.ops.segment_sum(msg, dst, num_segments=n)
            cnt = jax.ops.segment_sum(jnp.ones_like(dst, dtype=x.dtype), dst, num_segments=n)
            agg = summed / jnp.maximum(cnt, 1.0)[:, None]
            out = agg @ W_l.T + b_l + x @ W_r.T
            mu = jnp.mean(out, axis=-1, keepdims=True)
            var = jnp.var(out, axis=-1, keepdims=True)
            out = (out - mu) * jax.lax.rsqrt(var + LN_EPS) * gamma + beta
            return jax.nn.relu(out)
        key = jax.random.key(seed)
        ks = jax.random.split(key, 12)
        s = 1.0 / np.sqrt(D)
        inp = {'x': jax.random.normal(ks[0], (N, D), jnp.float32), 'edge_index': jax.random.randint(ks[1], (2, E), 0, N, dtype=jnp.int64)}
        for i in range(2):
            inp[f'W_l{i}'] = jax.random.normal(ks[2 + 5 * i], (D, D), jnp.float32) * s
            inp[f'b_l{i}'] = jnp.zeros((D,), jnp.float32)
            inp[f'W_r{i}'] = jax.random.normal(ks[3 + 5 * i], (D, D), jnp.float32) * s
            inp[f'gamma{i}'] = jnp.ones((D,), jnp.float32)
            inp[f'beta{i}'] = jnp.zeros((D,), jnp.float32)
        return inp
    _L3_gnn_all = _L3_gnn_setup()
    _L3_gnn_in = {k: v for k, v in _L3_gnn_all.items() if k in ('W_l0', 'b_l0', 'W_r0', 'gamma0', 'beta0', 'W_l1', 'b_l1', 'W_r1', 'gamma1', 'beta1')}
    del _L3_gnn_all
    return {'x': x, 'src': src, 'dst': dst, 'edge_attr_128': edge_attr_128, 'edge_attr_64': edge_attr_64, 'L0_gnn_w1': _L0_gnn_in['w1'], 'L0_gnn_b1': _L0_gnn_in['b1'], 'L0_gnn_w2': _L0_gnn_in['w2'], 'L0_gnn_b2': _L0_gnn_in['b2'], 'L0_gnn_wg': _L0_gnn_in['wg'], 'L0_gnn_bg': _L0_gnn_in['bg'], 'L0_gnn_wu': _L0_gnn_in['wu'], 'L0_gnn_bu': _L0_gnn_in['bu'], 'L1_gnn_W_neigh': _L1_gnn_in['W_neigh'], 'L1_gnn_W_self': _L1_gnn_in['W_self'], 'L1_gnn_b_self': _L1_gnn_in['b_self'], 'L2_gnn_W1': _L2_gnn_in['W1'], 'L2_gnn_a1s': _L2_gnn_in['a1s'], 'L2_gnn_a1d': _L2_gnn_in['a1d'], 'L2_gnn_We1': _L2_gnn_in['We1'], 'L2_gnn_ae1': _L2_gnn_in['ae1'], 'L2_gnn_b1': _L2_gnn_in['b1'], 'L2_gnn_W2': _L2_gnn_in['W2'], 'L2_gnn_a2s': _L2_gnn_in['a2s'], 'L2_gnn_a2d': _L2_gnn_in['a2d'], 'L2_gnn_We2': _L2_gnn_in['We2'], 'L2_gnn_ae2': _L2_gnn_in['ae2'], 'L2_gnn_b2': _L2_gnn_in['b2'], 'L3_gnn_W_l0': _L3_gnn_in['W_l0'], 'L3_gnn_b_l0': _L3_gnn_in['b_l0'], 'L3_gnn_W_r0': _L3_gnn_in['W_r0'], 'L3_gnn_gamma0': _L3_gnn_in['gamma0'], 'L3_gnn_beta0': _L3_gnn_in['beta0'], 'L3_gnn_W_l1': _L3_gnn_in['W_l1'], 'L3_gnn_b_l1': _L3_gnn_in['b_l1'], 'L3_gnn_W_r1': _L3_gnn_in['W_r1'], 'L3_gnn_gamma1': _L3_gnn_in['gamma1'], 'L3_gnn_beta1': _L3_gnn_in['beta1']}

def reference(x, src, dst, edge_attr_128, edge_attr_64, L0_gnn_w1, L0_gnn_b1, L0_gnn_w2, L0_gnn_b2, L0_gnn_wg, L0_gnn_bg, L0_gnn_wu, L0_gnn_bu, L1_gnn_W_neigh, L1_gnn_W_self, L1_gnn_b_self, L2_gnn_W1, L2_gnn_a1s, L2_gnn_a1d, L2_gnn_We1, L2_gnn_ae1, L2_gnn_b1, L2_gnn_W2, L2_gnn_a2s, L2_gnn_a2d, L2_gnn_We2, L2_gnn_ae2, L2_gnn_b2, L3_gnn_W_l0, L3_gnn_b_l0, L3_gnn_W_r0, L3_gnn_gamma0, L3_gnn_beta0, L3_gnn_W_l1, L3_gnn_b_l1, L3_gnn_W_r1, L3_gnn_gamma1, L3_gnn_beta1):
    import jax
    import jax.numpy as jnp

    def _L0_gnn_ref(h, edge_index, e, w1, b1, w2, b2, wg, bg, wu, bu):
        import jax, jax.numpy as jnp
        import numpy as np
        N, E = (50000, 12500)
        NODE_DIM, EDGE_DIM = (128, 64)
        MSG_IN = 2 * NODE_DIM + EDGE_DIM
        src, dst = (edge_index[0], edge_index[1])
        msg_in = jnp.concatenate([h[src], h[dst], e], axis=-1)
        messages = jax.nn.silu(msg_in @ w1 + b1) @ w2 + b2
        gates = jax.nn.sigmoid(msg_in @ wg + bg)
        messages = messages * gates
        n = h.shape[0]
        agg = jax.ops.segment_sum(messages, dst, num_segments=n)
        deg = jax.ops.segment_sum(jnp.ones((dst.shape[0],), h.dtype), dst, num_segments=n)
        agg = agg / jnp.maximum(deg, 1.0)[:, None]
        h_new = jax.nn.silu(jnp.concatenate([h, agg], axis=-1) @ wu + bu)
        return h_new

    def _L1_gnn_ref(feat, W_neigh, W_self, b_self, src, dst):
        import jax, jax.numpy as jnp
        import numpy as np
        N_NODES = 3125
        N_EDGES = 50000
        D_IN = 128
        D_OUT = 128
        "SAGE 'mean' aggregation: h = fc_self(feat) + fc_neigh(mean_{u in N(v)} feat_u).\n            in_feats == out_feats -> lin_before_mp is False: aggregate raw features first.\n            In-degrees are clamped to min 1.0 as in set_graph_data."
        n = feat.shape[0]
        deg = jax.ops.segment_sum(jnp.ones_like(dst, dtype=feat.dtype), dst, num_segments=n)
        deg = jnp.maximum(deg, 1.0)
        agg = jax.ops.segment_sum(feat[src], dst, num_segments=n)
        h_neigh = agg / deg[:, None] @ W_neigh
        h_self = feat @ W_self + b_self
        return h_self + h_neigh

    def _L2_gnn_ref(x, edge_index, edge_attr, W1, a1s, a1d, We1, ae1, b1, W2, a2s, a2d, We2, ae2, b2):
        import jax, jax.numpy as jnp
        import numpy as np
        N, E = (50000, 25000)
        F_IN, HID, SENT = (128, 128, 128)
        NEG_SLOPE = 0.2

        def _glorot(key, shape):
            fan_in, fan_out = (shape[0], shape[-1])
            lim = float(np.sqrt(6.0 / (fan_in + fan_out)))
            return jax.random.uniform(key, shape, jnp.float32, -lim, lim)

        def _gat_layer(x, src, dst, edge_attr, W, att_s, att_d, We, att_e, b):
            n = x.shape[0]
            deg = jax.ops.segment_sum(jnp.ones(src.shape[0], x.dtype), dst, num_segments=n)
            loop_attr = jax.ops.segment_sum(edge_attr, dst, num_segments=n) / jnp.maximum(deg, 1.0)[:, None]
            loops = jnp.arange(n, dtype=src.dtype)
            src = jnp.concatenate([src, loops])
            dst = jnp.concatenate([dst, loops])
            ea = jnp.concatenate([edge_attr, loop_attr], axis=0)
            h = x @ W
            a_s = h @ att_s
            a_d = h @ att_d
            a_e = ea @ We @ att_e
            alpha = jax.nn.leaky_relu(a_s[src] + a_d[dst] + a_e, NEG_SLOPE)
            m = jax.ops.segment_max(alpha, dst, num_segments=n)
            ex = jnp.exp(alpha - m[dst])
            w = ex / jax.ops.segment_sum(ex, dst, num_segments=n)[dst]
            return jax.ops.segment_sum(w[:, None] * h[src], dst, num_segments=n) + b
        src, dst = (edge_index[0], edge_index[1])
        h = _gat_layer(x, src, dst, edge_attr, W1, a1s, a1d, We1, ae1, b1)
        h = jax.nn.relu(h)
        return _gat_layer(h, src, dst, edge_attr, W2, a2s, a2d, We2, ae2, b2)

    def _L3_gnn_ref(x, edge_index, W_l0, b_l0, W_r0, gamma0, beta0, W_l1, b_l1, W_r1, gamma1, beta1):
        import jax, jax.numpy as jnp
        import numpy as np
        N = 50000
        E = 18750
        D = 128
        LN_EPS = 1e-05

        def _sage_layer(x, src, dst, W_l, b_l, W_r, gamma, beta):
            n = x.shape[0]
            msg = x[src]
            summed = jax.ops.segment_sum(msg, dst, num_segments=n)
            cnt = jax.ops.segment_sum(jnp.ones_like(dst, dtype=x.dtype), dst, num_segments=n)
            agg = summed / jnp.maximum(cnt, 1.0)[:, None]
            out = agg @ W_l.T + b_l + x @ W_r.T
            mu = jnp.mean(out, axis=-1, keepdims=True)
            var = jnp.var(out, axis=-1, keepdims=True)
            out = (out - mu) * jax.lax.rsqrt(var + LN_EPS) * gamma + beta
            return jax.nn.relu(out)
        src, dst = (edge_index[0], edge_index[1])
        x = _sage_layer(x, src, dst, W_l0, b_l0, W_r0, gamma0, beta0)
        x = _sage_layer(x, src, dst, W_l1, b_l1, W_r1, gamma1, beta1)
        return x
    edge_index = jnp.stack([src, dst])
    x = _layernorm(x + _L0_gnn_ref(x, edge_index, edge_attr_64, L0_gnn_w1, L0_gnn_b1, L0_gnn_w2, L0_gnn_b2, L0_gnn_wg, L0_gnn_bg, L0_gnn_wu, L0_gnn_bu), axis=-1)
    x = _layernorm(x + _L1_gnn_ref(x, L1_gnn_W_neigh, L1_gnn_W_self, L1_gnn_b_self, src, dst), axis=-1)
    x = _layernorm(x + _L2_gnn_ref(x, edge_index, edge_attr_128, L2_gnn_W1, L2_gnn_a1s, L2_gnn_a1d, L2_gnn_We1, L2_gnn_ae1, L2_gnn_b1, L2_gnn_W2, L2_gnn_a2s, L2_gnn_a2d, L2_gnn_We2, L2_gnn_ae2, L2_gnn_b2), axis=-1)
    x = _layernorm(x + _L3_gnn_ref(x, edge_index, L3_gnn_W_l0, L3_gnn_b_l0, L3_gnn_W_r0, L3_gnn_gamma0, L3_gnn_beta0, L3_gnn_W_l1, L3_gnn_b_l1, L3_gnn_W_r1, L3_gnn_gamma1, L3_gnn_beta1), axis=-1)
    return x

_drawn_inputs = setup_inputs


def setup_inputs(seed=0):
    import zlib

    import numpy as np

    out = dict(_drawn_inputs(seed))
    spreads = {'L1_gnn_b_self': (0.0, 0.1),
     'L2_gnn_b1': (0.0, 0.1),
     'L2_gnn_b2': (0.0, 0.1),
     'L3_gnn_b_l0': (0.0, 0.1),
     'L3_gnn_gamma0': (1.0, 0.2),
     'L3_gnn_beta0': (0.0, 0.1),
     'L3_gnn_b_l1': (0.0, 0.1),
     'L3_gnn_gamma1': (1.0, 0.2),
     'L3_gnn_beta1': (0.0, 0.1)}
    factors = {'edge_attr_64': 8.0,
     'L0_gnn_w1': 4.618,
     'L0_gnn_b1': 8.0,
     'L0_gnn_w2': 3.802,
     'L0_gnn_b2': 5.828,
     'L0_gnn_wg': 8.0,
     'L0_gnn_bg': 28.765,
     'L2_gnn_a1d': 3.039,
     'L2_gnn_a2s': 3.28,
     'L2_gnn_a2d': 64.0,
     'L0_gnn_bu': 3.094,
     'L2_gnn_We1': 2.807}
    for name, (base, spread) in spreads.items():
        noise = np.random.default_rng([zlib.crc32(name.encode()), seed]).standard_normal(out[name].shape)
        drawn = base * np.exp(spread * noise) if base else spread * noise
        out[name] = jnp.asarray(drawn.astype(out[name].dtype))
    for name, factor in factors.items():
        out[name] = (out[name] * factor).astype(out[name].dtype)
    return out
```

```python
from contextlib import ExitStack, contextmanager

import concourse.bass as bass
from concourse import mybir

ALU = mybir.AluOpType
ACT = mybir.ActivationFunctionType
AX = mybir.AxisListType.X
F32 = mybir.dt.float32
BF16 = mybir.dt.bfloat16
I32 = mybir.dt.int32

P = 128
J = 8
BE = P * J
UN = 2
PAIRS = J // 2
TICKS = UN * PAIRS
CREDIT = 8
BIG = 1.0e38
EPS = 1e-5
SLOPE = 0.2


def build_program(nc, a, out):
    N, D = a["x"].shape
    E = a["src"].shape[0]
    DE = a["edge_attr_64"].shape[1]
    assert D == P and DE == P // 2
    NB = -(-E // BE)
    NB += NB % UN
    TAIL = E - (NB - 1) * BE
    TP, TR = TAIL // J, TAIL % J
    assert 0 < TAIL <= BE and TR > 0
    NT = -(-(N + P) // P)
    NODES = NT * P
    FT, FR = N // P, N % P
    ITERS = NB // UN
    STEPS = NB * PAIRS
    HI = NT

    ctx = ExitStack()

    def sb(name, shape, dt=F32):
        return ctx.enter_context(nc.sbuf_tensor(name, shape, dt))

    def sem(name):
        return ctx.enter_context(nc.semaphore(name))

    kept_sem = sem

    @contextmanager
    def phase(name):
        with ExitStack() as c:
            used = []

            def local_sb(n, shape, dt=F32):
                return c.enter_context(nc.sbuf_tensor(f"{name}_{n}", shape, dt))

            def local_sem(n):
                used.append(c.enter_context(nc.semaphore(f"{name}_{n}")))
                return used[-1]

            yield local_sb, local_sem
            with nc.Block() as block:
                @block.sync
                def _(sp):
                    for s in used:
                        sp.sem_clear(s)

    def dram(name, shape, dt=F32):
        return nc.dram_tensor(name, shape, dt).ap()

    bank = [ctx.enter_context(nc.psum_tensor(f"bank{i}", [P, 512], F32)) for i in range(8)]
    ident = sb("ident", [P, P])
    ones = sb("ones", [1, P])
    iota0 = sb("iota0", [P, P])
    part0 = sb("part0", [P, 1])
    iota = sb("iota", [P, P])
    part = sb("part", [P, 1])
    base0 = sb("base0", [1, NB], I32)
    base = sb("base", [1, NB], I32)
    rounds = sb("rounds", [1, 1], I32)
    src_idx = sb("src_idx", [P, NB, J], I32)
    rel = sb("rel", [P, NB, J])
    x_sb = sb("x_sb", [P, NT, P])
    cur = sb("cur", [P, NT, P])
    h_sb = sb("h_sb", [P, NT, P])
    y_sb = sb("y_sb", [P, NT, P])
    w1_sb = sb("w1_sb", [P, NT, P])
    acc = sb("acc", [P, NODES])
    aux_acc = sb("aux_acc", [3, NODES])
    rdeg = sb("rdeg", [P, NT])
    has = sb("has", [P, NT])
    ae_loop = sb("ae_loop", [P, NT, 2])
    ae_tab = sb("ae_tab", [P, NB, J, 2])
    w_tab = sb("w_tab", [P, NB, J, 2])
    pen_f = sb("pen_f", [NB, BE])
    pen_b = sb("pen_b", [NB, BE])
    last = sb("last", [NB, BE])
    pass_f = sb("pass_f", [NB, 1])
    pass_b = sb("pass_b", [NB, 1])
    wide_w = sb("wide_w", [P, 4 * P])
    wide_b = sb("wide_b", [1, 4 * P])

    settled = sem("settled")
    p_tab = dram("p_tab", [NODES, 2 * P])
    q_tab = dram("q_tab", [NODES, 2 * P])
    rel_rows = dram("rel_rows", [NB, BE])
    id_rows = dram("id_rows", [NB, 4, BE], BF16)
    tables = [dram(f"table{i}", [NODES, P]) for i in range(5)]

    def steps_of(engine, *sems):
        for s in sems:
            engine.sem_inc(s, CREDIT)

    def done(engine, s, n):
        engine.wait_ge(s, n + CREDIT)

    def settle(engine):
        engine.sem_inc(settled, 1)

    def row(v):
        return v.rearrange("(a n) -> a n", a=1)

    def spread(v, n=P):
        return row(v).broadcast_to([n, v.shape[0]])

    def by_tile(t):
        return t.rearrange("(t p) d -> p t d", p=P)

    def flat(t):
        return t.rearrange("p a b -> p (a b)")

    def prologue():
        with phase("pro") as (tmp, sem):
            dst_i = tmp("dst_i", [P, NB, J], I32)
            dst_f = tmp("dst_f", [P, NB, J])
            src_s = tmp("src_s", [NB, BE], I32)
            dst_s = tmp("dst_s", [NB, BE], I32)
            prev_s = tmp("prev_s", [NB, BE], I32)
            next_s = tmp("next_s", [NB, BE], I32)
            ids_i = tmp("ids_i", [NB, 4, BE], I32)
            ids_b = tmp("ids_b", [NB, 4, BE], BF16)
            dst_sf = tmp("dst_sf", [NB, BE])
            rel_s = tmp("rel_s", [NB, BE])
            same = tmp("same", [NB, BE])
            base_b = tmp("base_b", [P, NB])
            mrel = tmp("mrel", [P, 1])
            mrel1 = tmp("mrel1", [1, 1])
            mrel_i = tmp("mrel_i", [1, 1], I32)
            mrel_q = tmp("mrel_q", [1, 1], I32)
            filled, loaded, consts = sem("filled"), sem("loaded"), sem("consts")
            v, t, stored = sem("v"), sem("t"), sem("stored")
            NL = 2 * 3 + 2 * 2 + 3 + 2 + 2

            with nc.Block() as block:
                @block.gpsimd
                def _(pool):
                    pool.memset(ident[:, :], 0.0).then_inc(consts, 1)
                    pool.memset(ones[:, :], 1.0).then_inc(consts, 1)
                    pool.wait_ge(consts, 2)
                    pool.affine_select(out=ident[:, :], in_=ident[:, :], compare_op=ALU.not_equal,
                                       fill=1.0, base=0, pattern=[[-1, P]],
                                       channel_multiplier=1).then_inc(consts, 1)
                    pool.iota(iota0[:, :], pattern=[[1, P]], base=0, channel_multiplier=0,
                              allow_small_or_imprecise_dtypes=True).then_inc(consts, 1)
                    pool.iota(part0[:, :], pattern=[[0, 1]], base=0, channel_multiplier=1,
                              allow_small_or_imprecise_dtypes=True).then_inc(consts, 1)

                @block.sync
                def _(sp):
                    sp.wait_ge(filled, 7)
                    full = (NB - 1) * BE
                    for dst_t, name in ((src_idx, "src"), (dst_i, "dst")):
                        sp.dma_start(dst_t[:, 0:NB - 1, :],
                                     a[name][0:full].rearrange("(b p j) -> p b j", p=P, j=J)).then_inc(loaded, 16)
                        sp.dma_start(dst_t[0:TP, NB - 1, :],
                                     a[name][full:full + TP * J].rearrange("(p j) -> p j", j=J)).then_inc(loaded, 16)
                        sp.dma_start(dst_t[TP:TP + 1, NB - 1, 0:TR],
                                     a[name][full + TP * J:E].rearrange("(p j) -> p j", p=1)).then_inc(loaded, 16)
                    for dst_t, name in ((src_s, "src"), (dst_s, "dst")):
                        sp.dma_start(dst_t[0:NB - 1, :],
                                     a[name][0:full].rearrange("(b e) -> b e", e=BE)).then_inc(loaded, 16)
                        sp.dma_start(dst_t[NB - 1:NB, 0:TAIL],
                                     a[name][full:E].rearrange("(b e) -> b e", b=1)).then_inc(loaded, 16)
                    sp.dma_start(prev_s[0:1, 1:BE], a["dst"][0:BE - 1].rearrange("(b e) -> b e", b=1)).then_inc(loaded, 16)
                    sp.dma_start(prev_s[1:NB - 1, :],
                                 a["dst"][BE - 1:full - 1].rearrange("(b e) -> b e", e=BE)).then_inc(loaded, 16)
                    sp.dma_start(prev_s[NB - 1:NB, 0:TAIL + 1],
                                 a["dst"][full - 1:E].rearrange("(b e) -> b e", b=1)).then_inc(loaded, 16)
                    sp.dma_start(next_s[0:NB - 1, :],
                                 a["dst"][1:full + 1].rearrange("(b e) -> b e", e=BE)).then_inc(loaded, 16)
                    sp.dma_start(next_s[NB - 1:NB, 0:TAIL - 1],
                                 a["dst"][full + 1:E].rearrange("(b e) -> b e", b=1)).then_inc(loaded, 16)
                    sp.dma_start(x_sb[:, 0:FT, :], by_tile(a["x"][0:FT * P, :])).then_inc(loaded, 16)
                    sp.dma_start(x_sb[0:FR, FT, :], a["x"][FT * P:N, :]).then_inc(loaded, 16)
                    sp.wait_ge(v, 13)
                    sp.dma_start(rel_rows, rel_s[:, :]).then_inc(stored, 16)
                    sp.dma_start(id_rows, ids_b[:, :, :]).then_inc(stored, 16)
                    sp.wait_ge(stored, 32)

                @block.vector
                def _(dve):
                    dve.memset(src_idx[:, NB - 1, :], 0).then_inc(filled, 1)
                    dve.memset(dst_i[:, NB - 1, :], N).then_inc(filled, 1)
                    dve.memset(src_s[:, :], 0).then_inc(filled, 1)
                    dve.memset(dst_s[:, :], N).then_inc(filled, 1)
                    dve.memset(prev_s[:, :], N).then_inc(filled, 1)
                    dve.memset(next_s[:, :], N).then_inc(filled, 1)
                    dve.memset(x_sb[:, FT:NT, :], 0.0).then_inc(filled, 1)
                    dve.wait_ge(loaded, 16 * NL)
                    dve.memset(prev_s[0:1, 0:1], -1).then_inc(v, 1)
                    dve.tensor_copy(dst_f[:, :, :], dst_i[:, :, :]).then_inc(v, 1)
                    dve.tensor_copy(dst_sf[:, :], dst_s[:, :]).then_inc(v, 1)
                    dve.wait_ge(v, 3)
                    dve.tensor_tensor(same[:, :], dst_s[:, :], prev_s[:, :], ALU.is_equal).then_inc(v, 1)
                    dve.wait_ge(v, 4)
                    dve.tensor_scalar(pen_f[:, :], same[:, :], -1.0, BIG, ALU.add, ALU.mult).then_inc(v, 1)
                    dve.tensor_tensor(last[:, :], dst_s[:, :], next_s[:, :], ALU.not_equal).then_inc(v, 1)
                    dve.wait_ge(v, 6)
                    dve.tensor_scalar(pen_b[:, :], last[:, :], -BIG, None, ALU.mult).then_inc(v, 1)
                    dve.tensor_tensor(rel_s[:, :], dst_sf[:, :], dst_sf[:, 0:1].broadcast_to([NB, BE]), ALU.subtract).then_inc(v, 1)
                    for k, s in ((0, src_s), (2, dst_s)):
                        dve.tensor_scalar(ids_i[:, k, :], s[:, :], P - 1, None, ALU.bitwise_and).then_inc(v, 1)
                        dve.tensor_scalar(ids_i[:, k + 1, :], s[:, :], 7, None, ALU.logical_shift_right).then_inc(v, 1)
                    dve.wait_ge(v, 12)
                    dve.tensor_copy(ids_b[:, :, :], ids_i[:, :, :]).then_inc(v, 1)
                    dve.tensor_reduce(pass_f[:, :], pen_f[:, :], AX, ALU.min).then_inc(v, 1)
                    dve.tensor_reduce(pass_b[:, :], pen_b[:, :], AX, ALU.min).then_inc(v, 1)
                    dve.wait_ge(t, 1)
                    dve.tensor_copy(base_b[:, :], bank[0][:, 0:NB]).then_inc(v, 1)
                    dve.tensor_copy(base0[:, :], dst_f[0:1, :, 0]).then_inc(v, 1)
                    dve.wait_ge(v, 17)
                    dve.tensor_tensor(rel[:, :, :], dst_f[:, :, :],
                                      base_b[:, :].rearrange("p (b j) -> p b j", j=1).broadcast_to([P, NB, J]),
                                      ALU.subtract).then_inc(v, 1)
                    dve.wait_ge(v, 18)
                    dve.tensor_reduce(mrel[:, :], flat(rel[:, :, :]), AX, ALU.max).then_inc(v, 1)
                    dve.wait_ge(t, 2)
                    dve.tensor_reduce(mrel1[:, :], bank[1][0:1, 0:P], AX, ALU.max).then_inc(v, 1)
                    dve.wait_ge(v, 20)
                    dve.tensor_copy(mrel_i[:, :], mrel1[:, :]).then_inc(v, 1)
                    dve.wait_ge(v, 21)
                    dve.tensor_scalar(mrel_q[:, :], mrel_i[:, :], 7, None, ALU.logical_shift_right).then_inc(v, 1)
                    dve.wait_ge(v, 22)
                    dve.tensor_scalar(rounds[:, :], mrel_q[:, :], 1, None, ALU.add).then_inc(v, 1)

                @block.tensor
                def _(pe):
                    pe.wait_ge(consts, 5)
                    pe.wait_ge(v, 2)
                    pe.matmul(bank[0][:, 0:NB], ones[0:1, :], dst_f[0:1, :, 0], start=True, stop=True).then_inc(t, 1)
                    pe.wait_ge(v, 19)
                    pe.transpose(bank[1][0:1, 0:P], mrel[:, :], ident[:, :]).then_inc(t, 1)

    def start_windows(dve, windows):
        dve.tensor_copy(iota[:, :], iota0[:, :]).then_inc(windows, 1)
        dve.tensor_copy(part[:, :], part0[:, :]).then_inc(windows, 1)
        dve.tensor_copy(base[:, :], base0[:, :]).then_inc(windows, 1)

    def next_windows(dve, windows):
        dve.tensor_scalar(iota[:, :], iota[:, :], float(P), None, ALU.add).then_inc(windows, 1)
        dve.tensor_scalar(part[:, :], part[:, :], float(P), None, ALU.add).then_inc(windows, 1)
        dve.tensor_scalar(base[:, :], base[:, :], P, N, ALU.add, ALU.min).then_inc(windows, 1)

    def lagged(i, lag, where):
        j = i - lag
        if (where == "first" and j < 0) or (where == "tail" and j >= 0):
            return None
        return j % TICKS, (-1 if j < 0 else 0)


    def node_loop(name, x_from, loads, width, bias=False, turn=(), agg=False, dest=None, stores=None):
        with phase(name) as (sb, sem):
            xs, gs = sb("xs", [P, 2, P]), sb("gs", [P, 2, P]) if agg else None
            xT = sb("xT", [P, 2, P])
            zs = sb("zs", [P, 2, width]) if (agg or stores) else None
            weights, turned_w = sem("weights"), sem("turned_w")
            staged, turned, xT_ready = sem("staged"), sem("turned"), sem("xT_ready")
            made, z_ready, y_ready = sem("made"), sem("z_ready"), sem("y_ready")
            stored = [sem(f"stored{u}") for u in range(2)] if stores else []
            HALF = NT // 2
            with nc.Block() as block:
                @block.sync
                def _(sp):
                    for to, frm in loads:
                        sp.dma_start(to, frm).then_inc(weights, 16)
                    if stores:
                        with sp.Fori(0, HALF) as it:
                            for u in range(2):
                                done(sp, z_ready, it * 2 + u + 1)
                                settle(sp)
                                for table, col in stores:
                                    w = table.shape[1]
                                    sp.dma_start(table[bass.ds(it * (2 * P) + u * P, P), :],
                                                 zs[:, u, col:col + w]).then_inc(stored[u], 16)
                        for u in range(2):
                            sp.wait_ge(stored[u], 16 * len(stores) * HALF)

                @block.gpsimd
                def _(pool):
                    steps_of(pool, staged)
                    with pool.Fori(0, HALF) as it:
                        for u in range(2):
                            t = it * 2 + u
                            done(pool, turned, t - 1)
                            if agg:
                                done(pool, made, t - 1)
                                pool.tensor_copy(gs[:, u, :], acc[:, bass.ds(it * (2 * P) + u * P, P)])
                            pool.tensor_copy(xs[:, u, :], flat(x_from[:, bass.ds(t, 1), :])).then_inc(staged, 1)

                @block.tensor
                def _(pe):
                    steps_of(pe, turned, made)
                    pe.wait_ge(weights, 16 * len(loads))
                    for n, k in enumerate(turn):
                        pe.transpose(bank[6 + n][:, 0:P], wide_w[:, k * P:(k + 1) * P], ident[:, :]).then_inc(turned_w, 1)
                    if turn:
                        pe.wait_ge(turned_w, 2 * len(turn))

                    def transpose(t, u):
                        done(pe, staged, t + 1)
                        done(pe, xT_ready, t - 1)
                        pe.transpose(bank[u][:, 0:P], xs[:, u, :], ident[:, :]).then_inc(turned, 1)

                    def product(t, u):
                        done(pe, xT_ready, t + 1)
                        done(pe, z_ready, t - 1)
                        z = bank[2 + u]
                        mm = pe.matmul(z[:, 0:width], xT[:, u, :], wide_w[:, 0:width], start=True, stop=not bias)
                        if bias:
                            nb = min(width, 2 * P)
                            mm = pe.matmul(z[:, 0:nb], ones[0:1, :], wide_b[0:1, 0:nb], start=False, stop=True)
                        if agg:
                            done(pe, y_ready, t - 1)
                            mm = pe.matmul(bank[4 + u][:, 0:P], gs[:, u, :], wide_w[:, P:2 * P], start=True, stop=True)
                        mm.then_inc(made, 1)

                    for u in range(2):
                        transpose(u, u)
                    with pe.Fori(0, HALF - 1) as it:
                        for u in range(2):
                            product(it * 2 + u, u)
                            transpose(it * 2 + (u + 2), u)
                    for u in range(2):
                        product(NT - 2 + u, u)

                @block.scalar
                def _(act):
                    steps_of(act, xT_ready, z_ready)

                    def copy_xT(t, u):
                        done(act, turned, t + 1)
                        done(act, made, t - 1)
                        act.copy(xT[:, u, :], bank[u][:, 0:P]).then_inc(xT_ready, 1)

                    def copy_z(t, u, it):
                        done(act, made, t + 1)
                        if agg:
                            done(act, y_ready, t - 1)
                            to = zs[:, u, :]
                        elif stores:
                            if it is not None:
                                act.wait_ge(stored[u], it * (16 * len(stores)))
                            to = zs[:, u, :]
                        else:
                            to = flat(dest[:, bass.ds(t, 1), :])
                        act.copy(to, bank[2 + u][:, 0:width]).then_inc(z_ready, 1)

                    for u in range(2):
                        copy_xT(u, u)
                    for u in range(2):
                        copy_z(u, u, None)
                        copy_xT(u + 2, u)
                    with act.Fori(1, HALF - 1) as it:
                        for u in range(2):
                            copy_z(it * 2 + u, u, it)
                            copy_xT(it * 2 + (u + 2), u)
                    for u in range(2):
                        copy_z(NT - 2 + u, u, HALF - 1)

                @block.vector
                def _(dve):
                    steps_of(dve, y_ready)
                    for n, k in enumerate(turn):
                        dve.wait_ge(turned_w, len(turn))
                        dve.tensor_copy(wide_w[:, k * P:(k + 1) * P], bank[6 + n][:, 0:P]).then_inc(turned_w, 1)
                    if agg:
                        with dve.Fori(0, HALF) as it:
                            for u in range(2):
                                t = it * 2 + u
                                done(dve, z_ready, t + 1)
                                dve.scalar_tensor_tensor(out=flat(dest[:, bass.ds(t, 1), :]), in0=bank[4 + u][:, 0:P],
                                                         scalar=rdeg[:, bass.ds(t, 1)], in1=zs[:, u, :],
                                                         op0=ALU.mult, op1=ALU.add).then_inc(y_ready, 1)

    def chain(engine, s):
        count = [0]

        def link(ins):
            ins.then_inc(s, 1)
            count[0] += 1
            engine.wait_ge(s, count[0])
        return link

    def norm_steps(sb, sem):
        stats, mean, dif = sb("stats", [P, NT, 6]), sb("mean", [P, NT]), sb("dif", [P, NT])
        var, rstd = sb("var", [P, NT]), sb("rstd", [P, NT])
        counted, var_ready, rstd_ready = sem("counted"), sem("var_ready"), sem("rstd_ready")
        norms = [0]

        def wide(v):
            return v[:, :].rearrange("p (t d) -> p t d", d=1).broadcast_to([P, NT, P])

        def steps(dve, link, x, y):
            with dve.Fori(0, NT // 2) as it:
                for u in range(2):
                    dve.bn_stats(flat(stats[:, bass.ds(it * 2 + u, 1), :]), flat(x[:, bass.ds(it * 2 + u, 1), :])).then_inc(counted, 1)
            norms[0] += 1
            dve.wait_ge(counted, norms[0] * NT)
            link(dve.tensor_tensor(mean[:, :], stats[:, :, 1], stats[:, :, 4], ALU.add))
            link(dve.tensor_tensor(dif[:, :], stats[:, :, 1], stats[:, :, 4], ALU.subtract))
            link(dve.tensor_tensor(var[:, :], stats[:, :, 2], stats[:, :, 5], ALU.add))
            link(dve.tensor_scalar(mean[:, :], mean[:, :], 0.5, None, ALU.mult))
            link(dve.tensor_tensor(dif[:, :], dif[:, :], dif[:, :], ALU.mult))
            link(dve.tensor_scalar(dif[:, :], dif[:, :], 0.25, EPS, ALU.mult, ALU.add))
            link(dve.scalar_tensor_tensor(out=var[:, :], in0=var[:, :], scalar=1.0 / P, in1=dif[:, :],
                                          op0=ALU.mult, op1=ALU.add))
            dve.sem_inc(var_ready, 1)
            dve.wait_ge(rstd_ready, norms[0])
            link(dve.reciprocal(rstd[:, :], dif[:, :]))
            link(dve.tensor_tensor(dif[:, :], rstd[:, :], rstd[:, :], ALU.mult))
            link(dve.tensor_tensor(dif[:, :], dif[:, :], var[:, :], ALU.mult))
            link(dve.tensor_scalar(dif[:, :], dif[:, :], -0.5, 1.5, ALU.mult, ALU.add))
            link(dve.tensor_tensor(rstd[:, :], rstd[:, :], dif[:, :], ALU.mult))
            link(dve.tensor_tensor(x[:, :, :], x[:, :, :], wide(mean), ALU.subtract))
            link(dve.tensor_tensor(y[:, :, :], x[:, :, :], wide(rstd), ALU.mult))

        def root(act, n):
            act.wait_ge(var_ready, n + 1)
            act.activation(dif[:, :], var[:, :], ACT.Sqrt).then_inc(rstd_ready, 1)

        return steps, root

    def over_chunks(v):
        return v[:, :].rearrange("p (a n) -> p a n", a=1).broadcast_to([P, J, P])

    def over_nodes(b):
        return rel[:, bass.ds(b, 1), :].rearrange("p b (j n) -> p (b j) n", n=1).broadcast_to([P, J, P])

    def add_window(dve, seg, b, n, added, k):
        settle(dve)
        start = dve.value_load(base[0:1, bass.ds(b, 1)], min_val=0, max_val=N)
        to = acc[:, bass.ds(start, P)]
        done(dve, added, n)
        ins = dve.tensor_tensor(to, to, seg[:, 0:P], ALU.add)
        if k:
            to = aux_acc[0:k, bass.ds(start, P)]
            ins = dve.tensor_tensor(to, to, seg[0:k, P:2 * P], ALU.add)
        ins.then_inc(added, 1)

    def gated_pass():
        with phase("gated") as (sb, sem):
            we, w2 = sb("we", [P, 2, 2 * P]), sb("w2", [P, P])
            b2 = sb("b2", [1, P])
            we_g, ae_row = sb("we_g", [P, 2, P]), sb("ae_row", [1, 2, P])
            ae_w = sb("ae_w", [P, 2, P])
            ae_c, we_T, aecol = sb("ae_c", [P, 2]), sb("we_T", [P, 2, P]), sb("aecol", [P, 2])
            idx = sb("idx", [P, UN, J], I32)
            ea64, ea128 = sb("ea64", [P, UN, J, DE]), sb("ea128", [P, UN, J, P])
            relr, qwin = sb("relr", [P, UN, BE]), sb("qwin", [P, UN, 2 * P])
            hotT, hot = sb("hotT", [P, UN, J, P]), sb("hot", [P, UN, J, P])
            rows = sb("rows", [P, TICKS, 2, 2 * P])
            eaT = sb("eaT", [P, 2, P])
            pre, sig = sb("pre", [P, 2, 2, 2 * P]), sb("sig", [P, 4, 2, 2 * P])
            silu, siluT, msg = sb("silu", [P, 2, 2, P]), sb("siluT", [P, 2, 2, P]), sb("msg", [P, 2, 2, P])
            junk, aux = sb("junk", [P, 2, 4, P]), sb("aux", [P, UN, J, 3])

            loaded, consts, ready = sem("loaded"), sem("consts"), sem("ready")
            idx_in = [sem(f"idx_in{u}") for u in range(UN)]
            ea64_in = [sem(f"ea64_in{u}") for u in range(UN)]
            ea128_in = [sem(f"ea128_in{u}") for u in range(UN)]
            relr_in = [sem(f"relr_in{u}") for u in range(UN)]
            qwin_in = [sem(f"qwin_in{u}") for u in range(UN)]
            rows_in = [kept_sem(f"gated_rows_in{i}") for i in range(TICKS)]
            windows = sem("windows")
            ea_turned, made, s_turned, m_made, summed = sem("ea_turned"), sem("pre_made"), sem("s_turned"), sem("m_made"), sem("summed")
            eaT_ready, sig_ready, sT_ready = sem("eaT_ready"), sem("sig_ready"), sem("sT_ready")
            pre_ready, silu_ready, msg_ready = sem("pre_ready"), sem("silu_ready"), sem("msg_ready")
            ae_ready, hot_ready, hotT_ready, added, ae_kept = sem("ae_ready"), sem("hot_ready"), sem("hotT_ready"), sem("added"), sem("ae_kept")
            PRE = [bank[0], bank[1]]
            SEG = [bank[2], bank[3]]
            EAT, ST, M = bank[4], bank[5], bank[6]

            def q_of(rr, it, i):
                return rr * STEPS + it * TICKS + i

            def edges_in(engine, s, rr, it, u, where):
                if u < UN - 1:
                    engine.wait_ge(s[u], (rr * ITERS + it + 1) * 16)
                else:
                    engine.wait_ge(s[u], (rr * (ITERS + 1) + it + (2 if where == "last" else 1)) * 16)

            with nc.Block() as block:
                @block.sync
                def _(sp):
                    for half in range(2):
                        rows_h = slice(half * DE, (half + 1) * DE)
                        if half == 0:
                            sp.wait_ge(ready, 4)
                        sp.dma_start(we[rows_h, half, 0:P], a["L0_gnn_w1"][2 * P:2 * P + DE, :]).then_inc(loaded, 16)
                        sp.dma_start(we[rows_h, half, P:2 * P], a["L0_gnn_wg"][2 * P:2 * P + DE, :]).then_inc(loaded, 16)
                    sp.dma_start(w2[:, :], a["L0_gnn_w2"]).then_inc(loaded, 16)
                    sp.dma_start(b2[:, :], row(a["L0_gnn_b2"])).then_inc(loaded, 16)
                    for k in range(2):
                        sp.dma_start(we_g[:, k, :], a[f"L2_gnn_We{k + 1}"]).then_inc(loaded, 16)
                        sp.dma_start(ae_c[:, k:k + 1], a[f"L2_gnn_ae{k + 1}"].rearrange("(p a) -> p a", a=1)).then_inc(loaded, 16)
                    R = sp.value_load(rounds[0:1, 0:1], min_val=1, max_val=NT)

                    def load_batch(rr, it, u, tail):
                        b = it * UN + u
                        n = rr * NB + b
                        q = n * PAIRS
                        done(sp, pre_ready, q - 4)
                        settle(sp)
                        sp.dma_start(idx[:, u, :], flat(src_idx[:, bass.ds(b, 1), :])).then_inc(idx_in[u], 16)
                        done(sp, ea_turned, q - 4)
                        settle(sp)
                        done(sp, ae_ready, q - 4)
                        settle(sp)
                        if not tail:
                            sp.dma_start(ea64[:, u, :, :], a["edge_attr_64"][bass.ds(b * BE, BE), :]
                                         .rearrange("(p j) d -> p j d", j=J)).then_inc(ea64_in[u], 16)
                            sp.dma_start(ea128[:, u, :, :], a["edge_attr_128"][bass.ds(b * BE, BE), :]
                                         .rearrange("(p j) d -> p j d", j=J)).then_inc(ea128_in[u], 16)
                        else:
                            for buf, name, s in ((ea64, "edge_attr_64", ea64_in), (ea128, "edge_attr_128", ea128_in)):
                                e0 = (NB - 1) * BE
                                sp.dma_start(buf[0:TP, u, :, :], a[name][e0:e0 + TP * J, :]
                                             .rearrange("(p j) d -> p j d", j=J)).then_inc(s[u], 16)
                                sp.dma_start(buf[TP:TP + 1, u, 0:TR, :], a[name][e0 + TP * J:E, :]
                                             .rearrange("(p j) d -> p j d", p=1)).then_inc(s[u], 16)
                        done(sp, hotT_ready, n - 1)
                        settle(sp)
                        sp.dma_start(relr[:, u, :], rel_rows[bass.ds(b, 1), :].broadcast_to([P, BE])).then_inc(relr_in[u], 16)
                        done(sp, made, q - 4)
                        settle(sp)
                        start = sp.value_load(base[0:1, bass.ds(b, 1)], min_val=0, max_val=N)
                        sp.dma_start(qwin[:, u, :], q_tab[bass.ds(start, P), :]).then_inc(qwin_in[u], 16)

                    with sp.Fori(0, R) as rr:
                        sp.wait_ge(windows, rr * 3 + 3)
                        settle(sp)
                        with sp.Fori(0, ITERS - 1) as it:
                            for u in range(UN):
                                load_batch(rr, it, u, False)
                        for u in range(UN):
                            load_batch(rr, ITERS - 1, u, u == UN - 1)

                @block.gpsimd
                def _(pool):
                    R = pool.value_load(rounds[0:1, 0:1], min_val=1, max_val=NT)
                    with pool.Fori(0, R) as rr:
                        with pool.Fori(0, ITERS) as it:
                            for u in range(UN):
                                pool.wait_ge(idx_in[u], (rr * ITERS + it + 1) * 16)
                                for k in range(PAIRS):
                                    i = u * PAIRS + k
                                    done(pool, pre_ready, q_of(rr, it, i) - TICKS + 1)
                                    settle(pool)
                                    for c in range(2):
                                        j = 2 * k + c
                                        pool.indirect_dma_start(out=rows[:, i, c, :], out_offset=None, in_=p_tab,
                                                                in_offset=bass.IndirectOffsetOnAxis(ap=idx[:, u, j:j + 1], axis=0)
                                                                ).then_inc(rows_in[i], 16)

                @block.tensor
                def _(pe):
                    steps_of(pe, ea_turned, made, s_turned, m_made, summed)
                    pe.wait_ge(loaded, 16 * 10)
                    for k in range(2):
                        pe.transpose(bank[k][:, 0:P], we_g[:, k, :], ident[:, :]).then_inc(consts, 1)
                    pe.wait_ge(consts, 4)
                    for k in range(2):
                        pe.matmul(bank[2][0:1, k * P:(k + 1) * P], ae_c[:, k:k + 1], we_T[:, k, :], start=True, stop=True).then_inc(consts, 1)
                    pe.wait_ge(consts, 7)
                    pe.matmul(bank[3][:, 0:2 * P], ones[0:1, :], flat(ae_row[0:1, :, :]), start=True, stop=True).then_inc(consts, 1)
                    pe.wait_ge(ready, 4)
                    R = pe.value_load(rounds[0:1, 0:1], min_val=1, max_val=NT)

                    def tick(rr, it, i, where):
                        if (w := lagged(i, 0, where)):
                            m, back = w
                            q, u, k = q_of(rr, it + back, m), m // PAIRS, m % PAIRS
                            if k == 0:
                                edges_in(pe, ea64_in, rr, it, u, where)
                            done(pe, eaT_ready, q)
                            pe.transpose(EAT[:, 0:P], ea64[:, u, 2 * k:2 * k + 2, :].rearrange("p j d -> p (j d)"),
                                         ident[:, :]).then_inc(ea_turned, 1)
                        if (w := lagged(i, 2, where)):
                            m, back = w
                            q, u, k = q_of(rr, it + back, m), m // PAIRS, m % PAIRS
                            done(pe, eaT_ready, q + 1)
                            done(pe, hotT_ready, rr * NB + (it + back) * UN + u + 1)
                            pe.wait_ge(qwin_in[u], (rr * ITERS + it + back + 1) * 16)
                            done(pe, pre_ready, q - 1)
                            for c in range(2):
                                to = PRE[m % 2][:, c * 2 * P:(c + 1) * 2 * P]
                                pe.matmul(to, hotT[:, u, 2 * k + c, :], qwin[:, u, :], start=True, stop=False)
                                mm = pe.matmul(to, eaT[:, m % 2, :], we[:, c, :], start=False, stop=True)
                            mm.then_inc(made, 1)
                        if (w := lagged(i, 4, where)):
                            m, back = w
                            q = q_of(rr, it + back, m)
                            done(pe, silu_ready, q + 1)
                            done(pe, sT_ready, q)
                            for c in range(2):
                                mm = pe.transpose(ST[:, c * P:(c + 1) * P], silu[:, m % 2, c, :], ident[:, :])
                            mm.then_inc(s_turned, 1)
                        if (w := lagged(i, 5, where)):
                            m, back = w
                            q = q_of(rr, it + back, m)
                            done(pe, sT_ready, q + 1)
                            done(pe, msg_ready, q)
                            for c in range(2):
                                to = M[:, c * P:(c + 1) * P]
                                pe.matmul(to, ones[0:1, :], b2[0:1, :], start=True, stop=False)
                                mm = pe.matmul(to, siluT[:, m % 2, c, :], w2[:, :], start=False, stop=True)
                            mm.then_inc(m_made, 1)
                        if (w := lagged(i, 6, where)):
                            m, back = w
                            q, u, k = q_of(rr, it + back, m), m // PAIRS, m % PAIRS
                            b = rr * NB + (it + back) * UN + u
                            done(pe, msg_ready, q + 1)
                            done(pe, ae_ready, q + 1)
                            if k == 0:
                                done(pe, hot_ready, b + 1)
                                done(pe, added, b - 1)
                            for c in range(2):
                                j = 2 * k + c
                                pe.matmul(SEG[u][:, 0:P], msg[:, m % 2, c, :], hot[:, u, j, :],
                                          start=(j == 0), stop=(j == J - 1), skip_group_check=True)
                                mm = pe.matmul(SEG[u][0:3, P:2 * P], aux[:, u, j, :], hot[:, u, j, :],
                                               start=False, stop=(j == J - 1), skip_group_check=True)
                            mm.then_inc(summed, 1)

                    with pe.Fori(0, R) as rr:
                        for i in range(TICKS):
                            tick(rr, 0, i, "first")
                        with pe.Fori(1, ITERS - 1) as it:
                            for i in range(TICKS):
                                tick(rr, it, i, "body")
                        for i in range(TICKS):
                            tick(rr, ITERS - 1, i, "last")
                        for i in range(6):
                            tick(rr, ITERS, i, "tail")

                @block.scalar
                def _(act):
                    steps_of(act, eaT_ready, sig_ready, sT_ready)
                    R = act.value_load(rounds[0:1, 0:1], min_val=1, max_val=NT)

                    def tick(rr, it, i, where):
                        if (w := lagged(i, 0, where)):
                            m, back = w
                            q = q_of(rr, it + back, m)
                            done(act, ea_turned, q + 1)
                            done(act, made, q - 1)
                            act.copy(eaT[:, m % 2, :], EAT[:, 0:P]).then_inc(eaT_ready, 1)
                        if (w := lagged(i, 2, where)):
                            m, back = w
                            q = q_of(rr, it + back, m)
                            done(act, pre_ready, q + 1)
                            done(act, msg_ready, q - 3)
                            act.activation(flat(sig[:, m % 4, :, :]), flat(pre[:, m % 2, :, :]), ACT.Sigmoid).then_inc(sig_ready, 1)
                        if (w := lagged(i, 4, where)):
                            m, back = w
                            q = q_of(rr, it + back, m)
                            done(act, s_turned, q + 1)
                            done(act, m_made, q - 1)
                            act.copy(flat(siluT[:, m % 2, :, :]), ST[:, 0:2 * P]).then_inc(sT_ready, 1)

                    with act.Fori(0, R) as rr:
                        for i in range(TICKS):
                            tick(rr, 0, i, "first")
                        with act.Fori(1, ITERS) as it:
                            for i in range(TICKS):
                                tick(rr, it, i, "body")
                        for i in range(4):
                            tick(rr, ITERS, i, "tail")

                @block.vector
                def _(dve):
                    steps_of(dve, pre_ready, silu_ready, msg_ready, ae_ready, hot_ready, hotT_ready, added, ae_kept)
                    dve.memset(we[:, :, :], 0.0).then_inc(ready, 1)
                    dve.memset(acc[:, :], 0.0).then_inc(ready, 1)
                    dve.memset(aux_acc[:, :], 0.0).then_inc(ready, 1)
                    dve.memset(aux[:, :, :, :], 1.0).then_inc(ready, 1)
                    dve.wait_ge(consts, 2)
                    dve.tensor_copy(we_T[:, 0, :], bank[0][:, 0:P]).then_inc(consts, 1)
                    dve.tensor_copy(we_T[:, 1, :], bank[1][:, 0:P]).then_inc(consts, 1)
                    dve.wait_ge(consts, 6)
                    dve.tensor_copy(flat(ae_row[0:1, :, :]), bank[2][0:1, 0:2 * P]).then_inc(consts, 1)
                    dve.wait_ge(consts, 8)
                    dve.tensor_copy(flat(ae_w[:, :, :]), bank[3][:, 0:2 * P]).then_inc(consts, 1)
                    start_windows(dve, windows)
                    dve.wait_ge(consts, 9)
                    dve.wait_ge(windows, 3)
                    R = dve.value_load(rounds[0:1, 0:1], min_val=1, max_val=NT)

                    def tick(rr, it, i, where):
                        if (w := lagged(i, 0, where)):
                            m, back = w
                            q, u, k = q_of(rr, it + back, m), m // PAIRS, m % PAIRS
                            b = it * UN + u
                            if k == 0:
                                dve.wait_ge(relr_in[u], (rr * ITERS + it + 1) * 16)
                                done(dve, made, q - 4)
                                dve.tensor_scalar(hotT[:, u, :, :], relr[:, u, :].rearrange("n (p j) -> n j p", j=J),
                                                  part[:, 0:1], None, ALU.is_equal).then_inc(hotT_ready, 1)
                                edges_in(dve, ea128_in, rr, it, u, where)
                            done(dve, summed, q - 7)
                            done(dve, ae_ready, q - 1)
                            for c in range(2):
                                for l in range(2):
                                    j = 2 * k + c
                                    ins = dve.tensor_tensor_reduce(out=junk[:, m % 2, 2 * c + l, :], in0=ea128[:, u, j, :],
                                                                   in1=ae_w[:, l, :], scale=1.0, scalar=0.0,
                                                                   op0=ALU.mult, op1=ALU.add,
                                                                   accum_out=aux[:, u, j, 1 + l:2 + l])
                            ins.then_inc(ae_ready, 1)
                            if k == PAIRS - 1:
                                done(dve, ae_ready, q + 1)
                                dve.tensor_copy(ae_tab[:, bass.ds(b, 1), :, :].rearrange("p b j l -> p (b j) l"),
                                                aux[:, u, :, 1:3]).then_inc(ae_kept, 1)
                        if (w := lagged(i, 2, where)):
                            m, back = w
                            q = q_of(rr, it + back, m)
                            done(dve, made, q + 1)
                            dve.wait_ge(rows_in[m], (rr * ITERS + it + back + 1) * 32)
                            done(dve, sig_ready, q - 1)
                            done(dve, silu_ready, q - 1)
                            dve.tensor_tensor(flat(pre[:, m % 2, :, :]), PRE[m % 2][:, :], flat(rows[:, m, :, :]),
                                              ALU.add).then_inc(pre_ready, 1)
                        if (w := lagged(i, 3, where)):
                            m, back = w
                            q = q_of(rr, it + back, m)
                            done(dve, sig_ready, q + 1)
                            done(dve, s_turned, q - 1)
                            dve.tensor_tensor(silu[:, m % 2, :, :], pre[:, m % 2, :, 0:P], sig[:, m % 4, :, 0:P],
                                              ALU.mult).then_inc(silu_ready, 1)
                        if (w := lagged(i, 4, where)) and w[0] % PAIRS == 0:
                            m, back = w
                            q, u = q_of(rr, it + back, m), m // PAIRS
                            b = (it + back) * UN + u
                            done(dve, summed, q - 4)
                            dve.tensor_tensor(hot[:, u, :, :], over_chunks(iota), over_nodes(b), ALU.is_equal).then_inc(hot_ready, 1)
                        if (w := lagged(i, 5, where)):
                            m, back = w
                            q = q_of(rr, it + back, m)
                            done(dve, m_made, q + 1)
                            done(dve, summed, q - 1)
                            dve.tensor_tensor(msg[:, m % 2, :, :], M[:, 0:2 * P].rearrange("p (c d) -> p c d", c=2),
                                              sig[:, m % 4, :, P:2 * P], ALU.mult).then_inc(msg_ready, 1)
                        if (w := lagged(i, 7, where)) and w[0] % PAIRS == PAIRS - 1:
                            m, back = w
                            q, u = q_of(rr, it + back, m), m // PAIRS
                            b = (it + back) * UN + u
                            done(dve, summed, q + 1)
                            add_window(dve, SEG[u], b, rr * NB + b, added, 3)

                    with dve.Fori(0, R) as rr:
                        dve.wait_ge(windows, rr * 3 + 3)
                        for i in range(TICKS):
                            tick(rr, 0, i, "first")
                        with dve.Fori(1, ITERS - 1) as it:
                            for i in range(TICKS):
                                tick(rr, it, i, "body")
                        for i in range(TICKS):
                            tick(rr, ITERS - 1, i, "last")
                        for i in range(7):
                            tick(rr, ITERS, i, "tail")
                        done(dve, hot_ready, (rr + 1) * NB)
                        next_windows(dve, windows)

    def edge_pass(name, table, weighted):
        with phase(name) as (sb, sem):
            idx, hot = sb("idx", [P, UN, J], I32), sb("hot", [P, UN, J, P])
            rows = sb("rows", [P, TICKS, 2, P])
            aux = sb("aux", [P, UN, J, 2])
            scaled = sb("scaled", [P, 4, 2, P])
            idx_in = [sem(f"idx_in{u}") for u in range(UN)]
            rows_in = [kept_sem(f"{name}_rows_in{i}") for i in range(TICKS)]
            windows, ready = sem("windows"), sem("ready")
            hot_ready, added, summed, scaled_ready, aux_ready = sem("hot_ready"), sem("added"), sem("summed"), sem("scaled_ready"), sem("aux_ready")
            used = scaled_ready if weighted else summed
            SEG = [bank[0], bank[1]]

            with nc.Block() as block:
                @block.sync
                def _(sp):
                    R = sp.value_load(rounds[0:1, 0:1], min_val=1, max_val=NT)
                    with sp.Fori(0, R) as rr:
                        with sp.Fori(0, ITERS) as it:
                            for u in range(UN):
                                done(sp, used, rr * STEPS + it * TICKS + u * PAIRS - PAIRS)
                                settle(sp)
                                sp.dma_start(idx[:, u, :], flat(src_idx[:, bass.ds(it * UN + u, 1), :])).then_inc(idx_in[u], 16)

                @block.gpsimd
                def _(pool):
                    R = pool.value_load(rounds[0:1, 0:1], min_val=1, max_val=NT)
                    with pool.Fori(0, R) as rr:
                        with pool.Fori(0, ITERS) as it:
                            for u in range(UN):
                                pool.wait_ge(idx_in[u], (rr * ITERS + it + 1) * 16)
                                for k in range(PAIRS):
                                    i = u * PAIRS + k
                                    done(pool, used, rr * STEPS + it * TICKS + i - TICKS + 1)
                                    settle(pool)
                                    for c in range(2):
                                        j = 2 * k + c
                                        pool.indirect_dma_start(out=rows[:, i, c, :], out_offset=None, in_=table,
                                                                in_offset=bass.IndirectOffsetOnAxis(ap=idx[:, u, j:j + 1], axis=0)
                                                                ).then_inc(rows_in[i], 16)

                if weighted:
                    @block.scalar
                    def _(act):
                        steps_of(act, scaled_ready)
                        R = act.value_load(rounds[0:1, 0:1], min_val=1, max_val=NT)
                        with act.Fori(0, R) as rr:
                            with act.Fori(0, ITERS) as it:
                                for i in range(TICKS):
                                    u, k = i // PAIRS, i % PAIRS
                                    q = rr * STEPS + it * TICKS + i
                                    if k == 0:
                                        done(act, aux_ready, rr * NB + it * UN + u + 1)
                                    act.wait_ge(rows_in[i], (rr * ITERS + it + 1) * 32)
                                    done(act, summed, q - 3)
                                    for c in range(2):
                                        ins = act.activation(scaled[:, i % 4, c, :], rows[:, i, c, :], ACT.Copy,
                                                             scale=aux[:, u, 2 * k + c, 0:1])
                                    ins.then_inc(scaled_ready, 1)

                @block.tensor
                def _(pe):
                    steps_of(pe, summed)
                    R = pe.value_load(rounds[0:1, 0:1], min_val=1, max_val=NT)
                    with pe.Fori(0, R) as rr:
                        with pe.Fori(0, ITERS) as it:
                            for i in range(TICKS):
                                u, k = i // PAIRS, i % PAIRS
                                q = rr * STEPS + it * TICKS + i
                                n = rr * NB + it * UN + u
                                if k == 0:
                                    done(pe, hot_ready, n + 1)
                                    done(pe, added, n - 1)
                                if weighted:
                                    done(pe, scaled_ready, q + 1)
                                else:
                                    pe.wait_ge(rows_in[i], (rr * ITERS + it + 1) * 32)
                                for c in range(2):
                                    j = 2 * k + c
                                    lhsT = scaled[:, i % 4, c, :] if weighted else rows[:, i, c, :]
                                    mm = pe.matmul(SEG[u][:, 0:P], lhsT, hot[:, u, j, :], start=(j == 0),
                                                   stop=(j == J - 1), skip_group_check=True)
                                    if weighted:
                                        mm = pe.matmul(SEG[u][0:2, P:2 * P], aux[:, u, j, :], hot[:, u, j, :],
                                                       start=False, stop=(j == J - 1), skip_group_check=True)
                                mm.then_inc(summed, 1)

                @block.vector
                def _(dve):
                    steps_of(dve, hot_ready, added, aux_ready)
                    dve.memset(acc[:, :], 0.0).then_inc(ready, 1)
                    dve.memset(aux_acc[:, :], 0.0).then_inc(ready, 1)
                    start_windows(dve, windows)
                    dve.wait_ge(ready, 2)
                    R = dve.value_load(rounds[0:1, 0:1], min_val=1, max_val=NT)

                    def onehots(rr, it, u):
                        b, n = it * UN + u, rr * NB + it * UN + u
                        done(dve, summed, n * PAIRS - PAIRS)
                        if weighted:
                            dve.tensor_copy(aux[:, u, :, :], w_tab[:, bass.ds(b, 1), :, :].rearrange("p b j l -> p (b j) l")).then_inc(aux_ready, 1)
                        dve.tensor_tensor(hot[:, u, :, :], over_chunks(iota), over_nodes(b), ALU.is_equal).then_inc(hot_ready, 1)

                    def add(rr, b, u):
                        n = rr * NB + b
                        done(dve, summed, n * PAIRS + PAIRS)
                        add_window(dve, SEG[u], b, n, added, 2 if weighted else 0)

                    with dve.Fori(0, R) as rr:
                        dve.wait_ge(windows, rr * 3 + 3)
                        onehots(rr, 0, 0)
                        onehots(rr, 0, 1)
                        with dve.Fori(1, ITERS) as it:
                            for u in range(UN):
                                add(rr, it * UN - UN + u, u)
                                onehots(rr, it, u)
                        for u in range(UN):
                            add(rr, NB - UN + u, u)
                        done(dve, hot_ready, rr * NB + NB)
                        next_windows(dve, windows)

    def turn_aux(pe, k, s):
        for t in range(NT):
            mm = pe.transpose(bank[7][:, t * k:(t + 1) * k], aux_acc[0:k, t * P:(t + 1) * P], ident[0:k, 0:k])
        mm.then_inc(s, 1)

    def aux_nodes(k):
        return bank[7][:, 0:NT * k].rearrange("p (t k) -> p t k", k=k)

    def degrees():
        with phase("degrees") as (sb, sem):
            turned, v = sem("turned"), sem("v")
            cnt = sb("cnt", [P, NT])
            with nc.Block() as block:
                @block.tensor
                def _(pe):
                    turn_aux(pe, 3, turned)

                @block.vector
                def _(dve):
                    link = chain(dve, v)
                    dve.wait_ge(turned, 1)
                    link(dve.tensor_scalar(cnt[:, :], aux_nodes(3)[:, :, 0], 1.0, None, ALU.max))
                    link(dve.tensor_scalar(has[:, :], aux_nodes(3)[:, :, 0], 1.0, None, ALU.min))
                    link(dve.reciprocal(rdeg[:, :], cnt[:, :]))
                    link(dve.tensor_tensor(ae_loop[:, :, :], aux_nodes(3)[:, :, 1:3],
                                           rdeg[:, :].rearrange("p (t k) -> p t k", k=1).broadcast_to([P, NT, 2]), ALU.mult))

    def over_tiles(v):
        return v[:, :].rearrange("p (a d) -> p a d", a=1).broadcast_to([P, NT, P])

    def over_features(v):
        return v[:, :].rearrange("p (t d) -> p t d", d=1).broadcast_to([P, NT, P])

    def finish_layer(name, gate=False, affine=None, residual=True, outer=False, store=None):
        with phase(name) as (sb, sem):
            norm, root = norm_steps(sb, sem)
            gb = sb("gb", [P, 2, P])
            loaded, v, sig, fin, stored = sem("loaded"), sem("v"), sem("sig"), sem("fin"), sem("stored")
            result = x_sb if residual else cur
            with nc.Block() as block:
                @block.sync
                def _(sp):
                    if affine:
                        for k in range(2):
                            sp.dma_start(gb[:, k, :], spread(a[affine[k]])).then_inc(loaded, 16)
                    sp.wait_ge(fin, 1)
                    if outer:
                        sp.dma_start(by_tile(out[0:FT * P, :]), result[:, 0:FT, :]).then_inc(stored, 16)
                        sp.dma_start(out[FT * P:N, :], result[0:FR, FT, :]).then_inc(stored, 16)
                        sp.wait_ge(stored, 32)
                    else:
                        if store is not None:
                            sp.dma_start(by_tile(store), result[:, :, :]).then_inc(stored, 16)
                            sp.wait_ge(stored, 16)

                @block.scalar
                def _(act):
                    if gate:
                        act.activation(flat(w1_sb[:, :, :]), flat(y_sb[:, :, :]), ACT.Sigmoid).then_inc(sig, 1)
                    for n in range((affine is not None) + residual):
                        root(act, n)

                @block.vector
                def _(dve):
                    link = chain(dve, v)
                    if gate:
                        dve.wait_ge(sig, 1)
                        link(dve.tensor_tensor(y_sb[:, :, :], y_sb[:, :, :], w1_sb[:, :, :], ALU.mult))
                    if affine:
                        norm(dve, link, y_sb, y_sb)
                        dve.wait_ge(loaded, 32)
                        link(dve.tensor_tensor(y_sb[:, :, :], y_sb[:, :, :], over_tiles(gb[:, 0, :]), ALU.mult))
                        link(dve.tensor_tensor(y_sb[:, :, :], y_sb[:, :, :], over_tiles(gb[:, 1, :]), ALU.add))
                        link(dve.tensor_scalar((y_sb if residual else cur)[:, :, :], y_sb[:, :, :], 0.0, None, ALU.max))
                    if residual:
                        link(dve.tensor_tensor(y_sb[:, :, :], y_sb[:, :, :], x_sb[:, :, :], ALU.add))
                        norm(dve, link, y_sb, x_sb)
                    dve.sem_inc(fin, 1)

    def attend(l, table, a_s, a_d):
        ROWS = 2
        with phase(f"attend{l}") as (sb, sem):
            att = sb("att", [P, 2, P])
            res = sb("res", [P, NT])
            tabs = sb("tabs", [P, 2, P], BF16)
            hik, hi_off = sb("hik", [P, 1]), sb("hi_off", [P, 2])
            pick = sb("pick", [P, 2 * P - 1], BF16)
            ids = sb("ids", [P, ROWS, 4, BE], BF16)
            hot_lo, found = sb("hot_lo", [P, 2, BE], BF16), sb("found", [P, 2, BE], BF16)
            ae_s, alpha = sb("ae_s", [NB, BE]), sb("alpha", [NB, BE])
            run, seg_max, ex, ml = sb("run", [NB, BE]), sb("seg_max", [NB, BE]), sb("ex", [NB, BE]), sb("ml", [NB, BE])
            pass_row, end_row, carry_row = sb("pass_row", [1, NB]), sb("end_row", [1, NB]), sb("carry_row", [1, NB + 1])
            carry = sb("carry", [NB, 1])
            loaded, stored, v, t, consts = sem("loaded"), sem("stored"), sem("v"), sem("t"), sem("consts")
            scanned, carried, shifted, weighed = sem("scanned"), sem("carried"), sem("shifted"), sem("weighed")
            ids_in = [sem(f"ids_in{i}") for i in range(ROWS)]
            hot_ready, found_ready, looked, picked = sem("hot_ready"), sem("found_ready"), sem("looked"), sem("picked")
            SIDES = 2
            BODY = TICKS // SIDES
            TURNS = NB // BODY
            assert NB % BODY == 0
            OUT = [bank[4], bank[5]]
            HALF = BE // 2

            def step_of(i):
                return i // SIDES, i % SIDES

            with nc.Block() as block:
                @block.sync
                def _(sp):
                    sp.dma_start(by_tile(table), h_sb[:, :, :]).then_inc(stored, 16)
                    for k, side in enumerate("sd"):
                        sp.dma_start(att[:, k, :], spread(a[f"L2_gnn_a{l}{side}"])).then_inc(loaded, 16)
                    with sp.Fori(0, TURNS) as it:
                        for bb in range(BODY):
                            done(sp, found_ready, (it * BODY + bb - ROWS + 1) * SIDES)
                            settle(sp)
                            sp.dma_start(ids[:, bb % ROWS, :, :], id_rows[bass.ds(it * BODY + bb, 1), :, :]
                                         .rearrange("b k e -> b (k e)").broadcast_to([P, 4 * BE])).then_inc(ids_in[bb % ROWS], 16)
                    sp.wait_ge(stored, 16)

                @block.tensor
                def _(pe):
                    steps_of(pe, looked, picked)
                    for j in range(J):
                        to = bank[6 + j // PAIRS][0:NB, (j % PAIRS) * P:(j % PAIRS + 1) * P]
                        mm = pe.transpose(to, ae_tab[:, :, j, l - 1], ident[:, :])
                    mm.then_inc(t, 1)
                    pe.wait_ge(consts, 1)
                    pe.matmul(OUT[0][:, :], pick[:, 0:P], found[:, 0, 0:HALF], start=True, stop=False, skip_group_check=True)
                    pe.matmul(OUT[1][:, :], pick[:, 0:P], found[:, 0, 0:HALF], start=True, stop=False, skip_group_check=True)

                    def tick(it, i, where):
                        if (w := lagged(i, 0, where)):
                            m, back = w
                            s = (it + back) * TICKS + m
                            done(pe, hot_ready, s + 1)
                            done(pe, found_ready, s - 1)
                            for h in range(2):
                                mm = pe.matmul(bank[2 * (m % 2) + h][:, :], tabs[:, m % SIDES, :],
                                               hot_lo[:, m % 2, h * HALF:(h + 1) * HALF], start=True, stop=True)
                            mm.then_inc(looked, 1)
                        if (w := lagged(i, 1, where)):
                            m, back = w
                            s = (it + back) * TICKS + m
                            b = (it + back) * BODY + m // SIDES
                            done(pe, found_ready, s + 1)
                            for h in range(2):
                                mm = pe.matmul(OUT[h][:, :], pick[:, bass.ds(b * (-1) + (P - 1), P)],
                                               found[:, m % 2, h * HALF:(h + 1) * HALF], start=False, stop=where == "tail",
                                               skip_group_check=True)
                            mm.then_inc(picked, 1)

                    for i in range(TICKS):
                        tick(0, i, "first")
                    with pe.Fori(1, TURNS) as it:
                        for i in range(TICKS):
                            tick(it, i, "body")
                    tick(TURNS, 0, "tail")
                    for n, (end, through) in enumerate(((run[:, BE - 1:BE], pass_f), (seg_max[:, 0:1], pass_b))):
                        pe.wait_ge(scanned, n + 1)
                        pe.transpose(bank[0][0:1, 0:NB], end, ident[0:NB, 0:NB])
                        pe.transpose(bank[0][0:1, P:P + NB], through[:, :], ident[0:NB, 0:NB]).then_inc(t, 1)
                        pe.wait_ge(carried, n + 1)
                        pe.transpose(bank[0][0:NB, 2 * P:2 * P + 1], carry_row[0:1, n:n + NB], ident[0:1, 0:1]).then_inc(t, 1)
                    for n, frm in enumerate((ml, ex)):
                        pe.wait_ge(weighed, n + 1)
                        for j in range(J):
                            mm = pe.transpose(bank[2 + n][:, j * NB:(j + 1) * NB], frm[:, j:BE:J], ident[0:NB, 0:NB])
                        mm.then_inc(t, 1)

                @block.scalar
                def _(act):
                    act.wait_ge(shifted, 1)
                    act.activation(ex[:, :], run[:, :], ACT.Exp).then_inc(weighed, 1)

                @block.vector
                def _(dve):
                    steps_of(dve, hot_ready, found_ready)
                    link = chain(dve, v)
                    dve.wait_ge(loaded, 32)
                    link(dve.memset(tabs[:, :, :], 0.0))
                    link(dve.memset(found[:, :, :], 0.0))
                    link(dve.memset(pick[:, :], 0.0))
                    link(dve.memset(pick[:, P - 1:P], 1.0))
                    for k, av in enumerate((a_s, a_d)):
                        link(dve.tensor_tensor(w1_sb[:, :, :], h_sb[:, :, :], over_tiles(att[:, k, :]), ALU.mult))
                        link(dve.tensor_reduce(av[:, :], w1_sb[:, :, :], AX, ALU.add))
                        link(dve.tensor_copy(tabs[:, k, 0:NT], av[:, :]))
                        link(dve.tensor_tensor(res[:, :], av[:, :], tabs[:, k, 0:NT], ALU.subtract))
                        link(dve.tensor_copy(tabs[:, k, NT:2 * NT], res[:, :]))
                        link(dve.tensor_tensor(res[:, :], res[:, :], tabs[:, k, NT:2 * NT], ALU.subtract))
                        link(dve.tensor_copy(tabs[:, k, 2 * NT:3 * NT], res[:, :]))
                    for n in range(2):
                        link(dve.tensor_scalar(hi_off[:, n:n + 1], part0[:, :], float((n + 1) * NT), -float(NT), ALU.is_ge, ALU.mult))
                    link(dve.tensor_tensor(hik[:, :], part0[:, :], hi_off[:, 0:1], ALU.add))
                    link(dve.tensor_tensor(hik[:, :], hik[:, :], hi_off[:, 1:2], ALU.add))
                    dve.wait_ge(t, 1)
                    for h in range(2):
                        link(dve.tensor_copy(ae_s[:, :].rearrange("b (p j) -> b j p", j=J)[:, h * PAIRS:(h + 1) * PAIRS, :],
                                             bank[6 + h][0:NB, :].rearrange("b (j p) -> b j p", p=P)))
                    dve.sem_inc(consts, 1)

                    def tick(it, i, where):
                        if (w := lagged(i, 0, where)):
                            m, back = w
                            s = (it + back) * TICKS + m
                            bb, side = step_of(m)
                            if side == 0:
                                dve.wait_ge(ids_in[bb % ROWS], (it * (BODY // ROWS) + (bb // ROWS + 1)) * 16)
                            done(dve, looked, s - 1)
                            dve.tensor_scalar(hot_lo[:, m % 2, :], ids[:, bb % ROWS, 2 * side, :], part0[:, 0:1], None,
                                              ALU.is_equal).then_inc(hot_ready, 1)
                        if (w := lagged(i, 1, where)):
                            m, back = w
                            s = (it + back) * TICKS + m
                            bb, side = step_of(m)
                            done(dve, looked, s + 1)
                            done(dve, picked, s - 1)
                            for h in range(2):
                                ins = dve.scalar_tensor_tensor(out=found[:, m % 2, h * HALF:(h + 1) * HALF],
                                                               in0=ids[:, bb % ROWS, 2 * side + 1, h * HALF:(h + 1) * HALF],
                                                               scalar=hik[:, 0:1], in1=bank[2 * (m % 2) + h][:, :],
                                                               op0=ALU.is_equal, op1=ALU.mult)
                            ins.then_inc(found_ready, 1)

                    for i in range(TICKS):
                        tick(0, i, "first")
                    with dve.Fori(1, TURNS) as it:
                        for i in range(TICKS):
                            tick(it, i, "body")
                    tick(TURNS, 0, "tail")
                    done(dve, picked, NB * SIDES)
                    for h in range(2):
                        cols = slice(h * HALF, (h + 1) * HALF)
                        link(dve.tensor_tensor(alpha[:, cols], ae_s[:, cols], OUT[h][0:NB, :], ALU.add))
                    link(dve.scalar_tensor_tensor(out=alpha[:, :], in0=alpha[:, :], scalar=SLOPE, in1=alpha[:, :], op0=ALU.mult, op1=ALU.max))
                    link(dve.tensor_tensor_scan(run[:, :], pen_f[:, :], alpha[:, :], -BIG, ALU.add, ALU.max))
                    dve.sem_inc(scanned, 1)
                    dve.wait_ge(t, 2)
                    link(dve.tensor_copy(end_row[:, :], bank[0][0:1, 0:NB]))
                    link(dve.tensor_copy(pass_row[:, :], bank[0][0:1, P:P + NB]))
                    link(dve.memset(carry_row[:, :], -BIG))
                    link(dve.tensor_tensor_scan(carry_row[:, 1:NB + 1], pass_row[:, :], end_row[:, :], -BIG, ALU.add, ALU.max))
                    dve.sem_inc(carried, 1)
                    dve.wait_ge(t, 3)
                    link(dve.tensor_copy(carry[:, :], bank[0][0:NB, 2 * P:2 * P + 1]))
                    link(dve.tensor_tensor_scan(run[:, :], pen_f[:, :], alpha[:, :], carry[:, 0:1], ALU.add, ALU.max))
                    rev = slice(None, None, -1)
                    link(dve.tensor_tensor_scan(seg_max[:, rev], pen_b[:, rev], run[:, rev], -BIG, ALU.add, ALU.max))
                    dve.sem_inc(scanned, 1)
                    dve.wait_ge(t, 4)
                    link(dve.tensor_copy(end_row[:, :], bank[0][0:1, 0:NB]))
                    link(dve.tensor_copy(pass_row[:, :], bank[0][0:1, P:P + NB]))
                    link(dve.memset(carry_row[:, :], -BIG))
                    link(dve.tensor_tensor_scan(carry_row[:, 0:NB][:, rev], pass_row[:, rev], end_row[:, rev], -BIG, ALU.add, ALU.max))
                    dve.sem_inc(carried, 1)
                    dve.wait_ge(t, 5)
                    link(dve.tensor_copy(carry[:, :], bank[0][0:NB, 2 * P:2 * P + 1]))
                    link(dve.tensor_tensor_scan(seg_max[:, rev], pen_b[:, rev], run[:, rev], carry[:, 0:1], ALU.add, ALU.max))
                    link(dve.tensor_tensor(ml[:, :], seg_max[:, :], last[:, :], ALU.mult))
                    dve.sem_inc(weighed, 1)
                    link(dve.tensor_tensor(run[:, :], alpha[:, :], seg_max[:, :], ALU.subtract))
                    dve.sem_inc(shifted, 1)
                    for n in range(2):
                        dve.wait_ge(t, 6 + n)
                        dve.tensor_copy(w_tab[:, :, :, 1 - n], bank[2 + n][:, 0:NB * J].rearrange("p (j b) -> p b j", b=NB)).then_inc(consts, 1)

    def settle_attention(l, a_s, a_d):
        with phase(f"gat{l}") as (sb, sem):
            m, al, M = sb("m", [P, NT]), sb("al", [P, NT]), sb("M", [P, NT])
            both = sb("both", [P, 2, NT])
            den, bias = sb("den", [P, NT]), sb("bias", [P, P])
            gs = sb("gs", [P, 2, P])
            loaded, v, turned, exp_ready, ready = sem("loaded"), sem("v"), sem("turned"), sem("exp_ready"), sem("ready")
            staged, flipped, copied = sem("staged"), sem("flipped"), sem("copied")
            with nc.Block() as block:
                @block.sync
                def _(sp):
                    sp.dma_start(bias[:, :], spread(a[f"L2_gnn_b{l}"])).then_inc(loaded, 16)

                @block.gpsimd
                def _(pool):
                    steps_of(pool, staged)
                    with pool.Fori(0, NT // 2) as it:
                        for u in range(2):
                            done(pool, flipped, it * 2 + (u - 1))
                            pool.tensor_copy(gs[:, u, :], acc[:, bass.ds(it * (2 * P) + u * P, P)]).then_inc(staged, 1)

                @block.tensor
                def _(pe):
                    steps_of(pe, flipped)
                    turn_aux(pe, 2, turned)
                    with pe.Fori(0, NT // 2) as it:
                        for u in range(2):
                            done(pe, staged, it * 2 + (u + 1))
                            done(pe, copied, it * 2 + (u - 1))
                            pe.transpose(bank[u][:, 0:P], gs[:, u, :], ident[:, :]).then_inc(flipped, 1)

                @block.scalar
                def _(act):
                    steps_of(act, copied)
                    with act.Fori(0, NT // 2) as it:
                        for u in range(2):
                            done(act, flipped, it * 2 + (u + 1))
                            act.copy(flat(w1_sb[:, bass.ds(it * 2 + u, 1), :]), bank[u][:, 0:P]).then_inc(copied, 1)
                    act.wait_ge(ready, 1)
                    act.activation(flat(both[:, :, :]), flat(both[:, :, :]), ACT.Exp).then_inc(exp_ready, 1)

                @block.vector
                def _(dve):
                    link = chain(dve, v)
                    link(dve.tensor_tensor(al[:, :], a_s[:, :], a_d[:, :], ALU.add))
                    link(dve.tensor_tensor(al[:, :], al[:, :], ae_loop[:, :, l - 1], ALU.add))
                    link(dve.scalar_tensor_tensor(out=al[:, :], in0=al[:, :], scalar=SLOPE, in1=al[:, :], op0=ALU.mult, op1=ALU.max))
                    link(dve.tensor_scalar(M[:, :], has[:, :], -1.0, BIG, ALU.add, ALU.mult))
                    dve.wait_ge(turned, 1)
                    link(dve.tensor_tensor(m[:, :], M[:, :], aux_nodes(2)[:, :, 1], ALU.add))
                    link(dve.tensor_tensor(M[:, :], m[:, :], al[:, :], ALU.max))
                    link(dve.tensor_tensor(both[:, 0, :], m[:, :], M[:, :], ALU.subtract))
                    link(dve.tensor_tensor(both[:, 1, :], al[:, :], M[:, :], ALU.subtract))
                    dve.sem_inc(ready, 1)
                    dve.wait_ge(exp_ready, 1)
                    link(dve.tensor_tensor(den[:, :], aux_nodes(2)[:, :, 0], both[:, 0, :], ALU.mult))
                    link(dve.tensor_tensor(den[:, :], den[:, :], both[:, 1, :], ALU.add))
                    link(dve.reciprocal(den[:, :], den[:, :]))
                    for n in range(2):
                        link(dve.tensor_tensor(both[:, n, :], both[:, n, :], den[:, :], ALU.mult))
                    done(dve, copied, NT)
                    dve.wait_ge(loaded, 16)
                    link(dve.tensor_tensor(y_sb[:, :, :], w1_sb[:, :, :], over_features(both[:, 0, :]), ALU.mult))
                    link(dve.tensor_tensor(w1_sb[:, :, :], h_sb[:, :, :], over_features(both[:, 1, :]), ALU.mult))
                    link(dve.tensor_tensor(y_sb[:, :, :], y_sb[:, :, :], w1_sb[:, :, :], ALU.add))
                    link(dve.tensor_tensor(y_sb[:, :, :], y_sb[:, :, :], over_tiles(bias), ALU.add))
                    if l == 1:
                        link(dve.tensor_scalar(cur[:, :, :], y_sb[:, :, :], 0.0, None, ALU.max))

    prologue()
    node_loop("edge_tables", x_sb,
              [(wide_w[:, 0:P], a["L0_gnn_w1"][0:P, :]), (wide_w[:, P:2 * P], a["L0_gnn_wg"][0:P, :]),
               (wide_w[:, 2 * P:3 * P], a["L0_gnn_w1"][P:2 * P, :]), (wide_w[:, 3 * P:4 * P], a["L0_gnn_wg"][P:2 * P, :]),
               (wide_b[:, 0:P], row(a["L0_gnn_b1"])), (wide_b[:, P:2 * P], row(a["L0_gnn_bg"]))],
              4 * P, bias=True, stores=[(p_tab, 0), (q_tab, 2 * P)])
    gated_pass()
    degrees()
    node_loop("update0", x_sb, [(wide_w[:, 0:P], a["L0_gnn_wu"][0:P, :]), (wide_w[:, P:2 * P], a["L0_gnn_wu"][P:2 * P, :]),
                                (wide_b[:, 0:P], row(a["L0_gnn_bu"]))], P, bias=True, agg=True, dest=y_sb)
    finish_layer("norm0", gate=True, store=tables[0])

    edge_pass("mean1", tables[0], False)
    node_loop("update1", x_sb, [(wide_w[:, 0:P], a["L1_gnn_W_self"]), (wide_w[:, P:2 * P], a["L1_gnn_W_neigh"]),
                                (wide_b[:, 0:P], row(a["L1_gnn_b_self"]))], P, bias=True, agg=True, dest=y_sb)
    finish_layer("norm1")

    a_s, a_d = sb("a_s", [P, NT]), sb("a_d", [P, NT])
    for l in (1, 2):
        node_loop(f"hidden{l}", x_sb if l == 1 else cur, [(wide_w[:, 0:P], a[f"L2_gnn_W{l}"])], P, dest=h_sb)
        attend(l, tables[l], a_s, a_d)
        edge_pass(f"attention{l}", tables[l], True)
        settle_attention(l, a_s, a_d)
    finish_layer("norm2", store=tables[3])

    for l in range(2):
        edge_pass(f"mean3{l}", tables[3 + l], False)
        node_loop(f"update3{l}", x_sb if l == 0 else cur,
                  [(wide_w[:, 0:P], a[f"L3_gnn_W_r{l}"]), (wide_w[:, P:2 * P], a[f"L3_gnn_W_l{l}"]),
                   (wide_b[:, 0:P], row(a[f"L3_gnn_b_l{l}"]))], P, bias=True, turn=(0, 1), agg=True, dest=y_sb)
        finish_layer(f"norm3{l}", affine=(f"L3_gnn_gamma{l}", f"L3_gnn_beta{l}"), residual=l == 1, outer=l == 1,
                     store=tables[4] if l == 0 else None)
    ctx.close()


_INS = ["x", "src", "dst", "edge_attr_128", "edge_attr_64"] \
    + [f"L0_gnn_{n}" for n in ("w1", "b1", "w2", "b2", "wg", "bg", "wu", "bu")] \
    + [f"L1_gnn_{n}" for n in ("W_neigh", "W_self", "b_self")] \
    + [f"L2_gnn_{n}{l}" for l in (1, 2) for n in ("W", "We", "ae", "b")] + [f"L2_gnn_a{l}{s}" for l in (1, 2) for s in "sd"] \
    + [f"L3_gnn_{n}{l}" for l in range(2) for n in ("W_l", "b_l", "W_r", "gamma", "beta")]


def kernel(**inputs):
    import numpy as _np
    import concourse.bacc as _bacc
    from concourse import mybir as _mybir
    from concourse.bass_utils import run_bass_kernel_spmd as _run

    nc = _bacc.Bacc("TRN2", target_bir_lowering=False, num_devices=1)
    arrays, args = {}, {}
    for name in _INS:
        v = _np.ascontiguousarray(inputs[name])
        arrays[f"in_{name}_dram"] = v
        args[name] = nc.dram_tensor(f"in_{name}_dram", v.shape, _mybir.dt.from_np(v.dtype), kind="ExternalInput").ap()
    out = nc.dram_tensor("out_0_dram", args["x"].shape, _mybir.dt.float32, kind="ExternalOutput").ap()
    build_program(nc, args, out)
    r = _run(nc, [arrays], core_ids=[0])
    return r.results[0]["out_0_dram"]
```

```python
from contextlib import ExitStack, contextmanager

import concourse.bass as bass
from concourse import mybir

ALU = mybir.AluOpType
ACT = mybir.ActivationFunctionType
AX = mybir.AxisListType.X
F32 = mybir.dt.float32
BF16 = mybir.dt.bfloat16
I32 = mybir.dt.int32

P = 128
J = 8
BE = P * J
UN = 2
PAIRS = J // 2
TICKS = UN * PAIRS
CREDIT = 8
BIG = 1.0e38
EPS = 1e-5
SLOPE = 0.2


def build_program(nc, a, out):
    N, D = a["x"].shape
    E = a["src"].shape[0]
    DE = a["edge_attr_64"].shape[1]
    assert D == P and DE == P // 2
    NB = -(-E // BE)
    NB += NB % UN
    TAIL = E - (NB - 1) * BE
    TP, TR = TAIL // J, TAIL % J
    assert 0 < TAIL <= BE and TR > 0
    NT = -(-(N + P) // P)
    NODES = NT * P
    FT, FR = N // P, N % P
    ITERS = NB // UN
    STEPS = NB * PAIRS
    HI = NT

    ctx = ExitStack()

    def sb(name, shape, dt=F32):
        return ctx.enter_context(nc.sbuf_tensor(name, shape, dt))

    def sem(name):
        return ctx.enter_context(nc.semaphore(name))

    kept_sem = sem

    spent, clearing = [], []

    def clear_spent(sp):
        for s in clearing:
            sp.sem_clear(s)
        clearing[:] = []

    @contextmanager
    def phase(name):
        with ExitStack() as c:
            held = ExitStack()

            def local_sb(n, shape, dt=F32):
                return c.enter_context(nc.sbuf_tensor(f"{name}_{n}", shape, dt))

            def local_sem(n):
                s = held.enter_context(nc.semaphore(f"{name}_{n}"))
                used.append(s)
                return s
            used = []
            spent_now, spent[:] = list(spent), []
            clearing[:] = [s for _, ss in spent_now for s in ss]

            yield local_sb, local_sem
            assert not clearing, name
            for h, _ in spent_now:
                h.close()
            spent.append((held, used))

    def dram(name, shape, dt=F32):
        return nc.dram_tensor(name, shape, dt).ap()

    bank = [ctx.enter_context(nc.psum_tensor(f"bank{i}", [P, 512], F32)) for i in range(8)]
    ident = sb("ident", [P, P])
    ones = sb("ones", [1, P])
    iota0 = sb("iota0", [P, P])
    part0 = sb("part0", [P, 1])
    iota = sb("iota", [P, P])
    part = sb("part", [P, 1])
    base0 = sb("base0", [1, NB], I32)
    base = sb("base", [1, NB], I32)
    rounds = sb("rounds", [1, 1], I32)
    src_idx = sb("src_idx", [P, NB, J], I32)
    rel = sb("rel", [P, NB, J])
    x_sb = sb("x_sb", [P, NT, P])
    cur = sb("cur", [P, NT, P])
    h_sb = sb("h_sb", [P, NT, P])
    y_sb = sb("y_sb", [P, NT, P])
    w1_sb = sb("w1_sb", [P, NT, P])
    acc = sb("acc", [P, NODES])
    aux_acc = sb("aux_acc", [3, NODES])
    rdeg = sb("rdeg", [P, NT])
    has = sb("has", [P, NT])
    seg_start = sb("seg_start", [P, NT], I32)
    ae_tab = sb("ae_tab", [P, NB, J, 2])
    w_tab = sb("w_tab", [P, NB, J, 2])
    pen_f = sb("pen_f", [NB, BE])
    pen_b = sb("pen_b", [NB, BE])
    last = sb("last", [NB, BE])
    pass_f = sb("pass_f", [NB, 1])
    pass_b = sb("pass_b", [NB, 1])
    wide_w = sb("wide_w", [P, 4 * P])
    wide_b = sb("wide_b", [1, 4 * P])

    settled = sem("settled")
    p_tab = dram("p_tab", [NODES, 2 * P])
    q_tab = dram("q_tab", [NODES, 2 * P])
    rel_rows = dram("rel_rows", [NB, BE])
    id_rows = dram("id_rows", [NB, 2, BE], BF16)
    first_ad = dram("first_ad", [NB * BE + NODES, 1])
    tables = [dram(f"table{i}", [NODES, P]) for i in range(5)]

    def steps_of(engine, *sems):
        for s in sems:
            engine.sem_inc(s, CREDIT)

    def done(engine, s, n):
        engine.wait_ge(s, n + CREDIT)

    def settle(engine):
        engine.sem_inc(settled, 1)

    def row(v):
        return v.rearrange("(a n) -> a n", a=1)

    def spread(v, n=P):
        return row(v).broadcast_to([n, v.shape[0]])

    def by_tile(t):
        return t.rearrange("(t p) d -> p t d", p=P)

    def flat(t):
        return t.rearrange("p a b -> p (a b)")

    def prologue():
        with phase("pro") as (tmp, sem):
            dst_i = tmp("dst_i", [P, NB, J], I32)
            dst_f = tmp("dst_f", [P, NB, J])
            src_s = tmp("src_s", [NB, BE], I32)
            dst_s = tmp("dst_s", [NB, BE], I32)
            prev_s = tmp("prev_s", [NB, BE], I32)
            next_s = tmp("next_s", [NB, BE], I32)
            ids_i = tmp("ids_i", [NB, 2, BE], I32)
            ids_b = tmp("ids_b", [NB, 2, BE], BF16)
            none = tmp("none", [NB, BE])
            dst_sf = tmp("dst_sf", [NB, BE])
            rel_s = tmp("rel_s", [NB, BE])
            same = tmp("same", [NB, BE])
            base_b = tmp("base_b", [P, NB])
            mrel = tmp("mrel", [P, 1])
            mrel1 = tmp("mrel1", [1, 1])
            mrel_i = tmp("mrel_i", [1, 1], I32)
            mrel_q = tmp("mrel_q", [1, 1], I32)
            filled, loaded, consts = sem("filled"), sem("loaded"), sem("consts")
            v, t, stored = sem("v"), sem("t"), sem("stored")
            NL = 2 * 3 + 2 * 2 + 3 + 2 + 2

            with nc.Block() as block:
                @block.gpsimd
                def _(pool):
                    pool.memset(ident[:, :], 0.0).then_inc(consts, 1)
                    pool.memset(ones[:, :], 1.0).then_inc(consts, 1)
                    pool.wait_ge(consts, 2)
                    pool.affine_select(out=ident[:, :], in_=ident[:, :], compare_op=ALU.not_equal,
                                       fill=1.0, base=0, pattern=[[-1, P]],
                                       channel_multiplier=1).then_inc(consts, 1)
                    pool.iota(iota0[:, :], pattern=[[1, P]], base=0, channel_multiplier=0,
                              allow_small_or_imprecise_dtypes=True).then_inc(consts, 1)
                    pool.iota(part0[:, :], pattern=[[0, 1]], base=0, channel_multiplier=1,
                              allow_small_or_imprecise_dtypes=True).then_inc(consts, 1)
                    pool.memset(none[:, :], -BIG).then_inc(consts, 1)

                @block.sync
                def _(sp):
                    sp.wait_ge(filled, 7)
                    full = (NB - 1) * BE
                    for dst_t, name in ((src_idx, "src"), (dst_i, "dst")):
                        sp.dma_start(dst_t[:, 0:NB - 1, :],
                                     a[name][0:full].rearrange("(b p j) -> p b j", p=P, j=J)).then_inc(loaded, 16)
                        sp.dma_start(dst_t[0:TP, NB - 1, :],
                                     a[name][full:full + TP * J].rearrange("(p j) -> p j", j=J)).then_inc(loaded, 16)
                        sp.dma_start(dst_t[TP:TP + 1, NB - 1, 0:TR],
                                     a[name][full + TP * J:E].rearrange("(p j) -> p j", p=1)).then_inc(loaded, 16)
                    for dst_t, name in ((src_s, "src"), (dst_s, "dst")):
                        sp.dma_start(dst_t[0:NB - 1, :],
                                     a[name][0:full].rearrange("(b e) -> b e", e=BE)).then_inc(loaded, 16)
                        sp.dma_start(dst_t[NB - 1:NB, 0:TAIL],
                                     a[name][full:E].rearrange("(b e) -> b e", b=1)).then_inc(loaded, 16)
                    sp.dma_start(prev_s[0:1, 1:BE], a["dst"][0:BE - 1].rearrange("(b e) -> b e", b=1)).then_inc(loaded, 16)
                    sp.dma_start(prev_s[1:NB - 1, :],
                                 a["dst"][BE - 1:full - 1].rearrange("(b e) -> b e", e=BE)).then_inc(loaded, 16)
                    sp.dma_start(prev_s[NB - 1:NB, 0:TAIL + 1],
                                 a["dst"][full - 1:E].rearrange("(b e) -> b e", b=1)).then_inc(loaded, 16)
                    sp.dma_start(next_s[0:NB - 1, :],
                                 a["dst"][1:full + 1].rearrange("(b e) -> b e", e=BE)).then_inc(loaded, 16)
                    sp.dma_start(next_s[NB - 1:NB, 0:TAIL - 1],
                                 a["dst"][full + 1:E].rearrange("(b e) -> b e", b=1)).then_inc(loaded, 16)
                    sp.dma_start(x_sb[:, 0:FT, :], by_tile(a["x"][0:FT * P, :])).then_inc(loaded, 16)
                    sp.dma_start(x_sb[0:FR, FT, :], a["x"][FT * P:N, :]).then_inc(loaded, 16)
                    sp.wait_ge(v, 11)
                    sp.dma_start(rel_rows, rel_s[:, :]).then_inc(stored, 16)
                    sp.dma_start(id_rows, ids_b[:, :, :]).then_inc(stored, 16)
                    sp.wait_ge(consts, 6)
                    sp.dma_start(first_ad[0:NB * BE, :].rearrange("(b e) a -> b (e a)", e=BE), none[:, :]).then_inc(stored, 16)
                    sp.wait_ge(stored, 48)

                @block.vector
                def _(dve):
                    dve.memset(src_idx[:, NB - 1, :], 0).then_inc(filled, 1)
                    dve.memset(dst_i[:, NB - 1, :], N).then_inc(filled, 1)
                    dve.memset(src_s[:, :], 0).then_inc(filled, 1)
                    dve.memset(dst_s[:, :], N).then_inc(filled, 1)
                    dve.memset(prev_s[:, :], N).then_inc(filled, 1)
                    dve.memset(next_s[:, :], N).then_inc(filled, 1)
                    dve.memset(x_sb[:, FT:NT, :], 0.0).then_inc(filled, 1)
                    dve.wait_ge(loaded, 16 * NL)
                    dve.memset(prev_s[0:1, 0:1], -1).then_inc(v, 1)
                    dve.tensor_copy(dst_f[:, :, :], dst_i[:, :, :]).then_inc(v, 1)
                    dve.tensor_copy(dst_sf[:, :], dst_s[:, :]).then_inc(v, 1)
                    dve.wait_ge(v, 3)
                    dve.tensor_tensor(same[:, :], dst_s[:, :], prev_s[:, :], ALU.is_equal).then_inc(v, 1)
                    dve.wait_ge(v, 4)
                    dve.tensor_scalar(pen_f[:, :], same[:, :], -1.0, BIG, ALU.add, ALU.mult).then_inc(v, 1)
                    dve.tensor_tensor(last[:, :], dst_s[:, :], next_s[:, :], ALU.not_equal).then_inc(v, 1)
                    dve.wait_ge(v, 6)
                    dve.tensor_scalar(pen_b[:, :], last[:, :], -BIG, None, ALU.mult).then_inc(v, 1)
                    dve.tensor_tensor(rel_s[:, :], dst_sf[:, :], dst_sf[:, 0:1].broadcast_to([NB, BE]), ALU.subtract).then_inc(v, 1)
                    dve.tensor_scalar(ids_i[:, 0, :], src_s[:, :], P - 1, None, ALU.bitwise_and).then_inc(v, 1)
                    dve.tensor_scalar(ids_i[:, 1, :], src_s[:, :], 7, None, ALU.logical_shift_right).then_inc(v, 1)
                    dve.wait_ge(v, 10)
                    dve.tensor_copy(ids_b[:, :, :], ids_i[:, :, :]).then_inc(v, 1)
                    dve.tensor_reduce(pass_f[:, :], pen_f[:, :], AX, ALU.min).then_inc(v, 1)
                    dve.tensor_reduce(pass_b[:, :], pen_b[:, :], AX, ALU.min).then_inc(v, 1)
                    dve.wait_ge(t, 1)
                    dve.tensor_copy(base_b[:, :], bank[0][:, 0:NB]).then_inc(v, 1)
                    dve.tensor_copy(base0[:, :], dst_f[0:1, :, 0]).then_inc(v, 1)
                    dve.wait_ge(v, 15)
                    dve.tensor_tensor(rel[:, :, :], dst_f[:, :, :],
                                      base_b[:, :].rearrange("p (b j) -> p b j", j=1).broadcast_to([P, NB, J]),
                                      ALU.subtract).then_inc(v, 1)
                    dve.wait_ge(v, 16)
                    dve.tensor_reduce(mrel[:, :], flat(rel[:, :, :]), AX, ALU.max).then_inc(v, 1)
                    dve.wait_ge(t, 2)
                    dve.tensor_reduce(mrel1[:, :], bank[1][0:1, 0:P], AX, ALU.max).then_inc(v, 1)
                    dve.wait_ge(v, 18)
                    dve.tensor_copy(mrel_i[:, :], mrel1[:, :]).then_inc(v, 1)
                    dve.wait_ge(v, 19)
                    dve.tensor_scalar(mrel_q[:, :], mrel_i[:, :], 7, None, ALU.logical_shift_right).then_inc(v, 1)
                    dve.wait_ge(v, 20)
                    dve.tensor_scalar(rounds[:, :], mrel_q[:, :], 1, None, ALU.add).then_inc(v, 1)

                @block.tensor
                def _(pe):
                    pe.wait_ge(consts, 5)
                    pe.wait_ge(v, 2)
                    pe.matmul(bank[0][:, 0:NB], ones[0:1, :], dst_f[0:1, :, 0], start=True, stop=True).then_inc(t, 1)
                    pe.wait_ge(v, 17)
                    pe.transpose(bank[1][0:1, 0:P], mrel[:, :], ident[:, :]).then_inc(t, 1)

    def start_windows(dve, windows):
        dve.tensor_copy(iota[:, :], iota0[:, :]).then_inc(windows, 1)
        dve.tensor_copy(part[:, :], part0[:, :]).then_inc(windows, 1)
        dve.tensor_copy(base[:, :], base0[:, :]).then_inc(windows, 1)

    def next_windows(dve, windows):
        dve.tensor_scalar(iota[:, :], iota[:, :], float(P), None, ALU.add).then_inc(windows, 1)
        dve.tensor_scalar(part[:, :], part[:, :], float(P), None, ALU.add).then_inc(windows, 1)
        dve.tensor_scalar(base[:, :], base[:, :], P, N, ALU.add, ALU.min).then_inc(windows, 1)

    def lagged(i, lag, where, ticks=TICKS):
        j = i - lag
        if (where == "first" and j < 0) or (where == "tail" and j >= 0):
            return None
        return j % ticks, (-1 if j < 0 else 0)


    def node_loop(name, x_from, loads, width, bias=False, turn=(), agg=False, dest=None, stores=None):
        with phase(name) as (sb, sem):
            xs, gs = sb("xs", [P, 2, 2, P]), sb("gs", [P, 2, 2, P]) if agg else None
            xT = sb("xT", [P, 2, 2, P])
            zs = sb("zs", [P, 2, 2, width]) if (agg or stores) else None
            weights, turned_w = sem("weights"), sem("turned_w")
            staged, sums_staged, turned, xT_ready = sem("staged"), sem("sums_staged"), sem("turned"), sem("xT_ready")
            made, z_ready, y_ready = sem("made"), sem("z_ready"), sem("y_ready")
            stored = [sem(f"stored{u}") for u in range(2)] if stores else []
            NP = NT // 2
            assert NT % 2 == 0 and NP % 2 == 1

            def each_pair(engine, early, late=None):
                for u in range(2):
                    early(u, u)
                with engine.Fori(0, (NP - 3) // 2) as it:
                    for u in range(2):
                        if late:
                            late(it * 2 + u, u)
                        early(it * 2 + (u + 2), u)
                if late:
                    late(NP - 3, 0)
                early(NP - 1, 0)
                if late:
                    late(NP - 2, 1)
                    late(NP - 1, 0)

            def tiles(v, p):
                return v[:, bass.ds(p * 2, 2), :]

            with nc.Block() as block:
                @block.sync
                def _(sp):
                    clear_spent(sp)
                    for to, frm in loads:
                        sp.dma_start(to, frm).then_inc(weights, 16)

                    def store(p, u):
                        done(sp, z_ready, p + 1)
                        settle(sp)
                        for c in range(2):
                            for table, col in stores:
                                w = table.shape[1]
                                sp.dma_start(table[bass.ds(p * (2 * P) + c * P, P), :],
                                             zs[:, u, c, col:col + w]).then_inc(stored[u], 16)
                    if stores:
                        each_pair(sp, store)
                        for u in range(2):
                            sp.wait_ge(stored[u], 32 * len(stores) * (NP // 2 + 1 - u))

                if agg:
                    @block.gpsimd
                    def _(pool):
                        steps_of(pool, sums_staged)

                        def stage_sums(p, u):
                            done(pool, made, p - 1)
                            pool.tensor_copy(flat(gs[:, u, :, :]), acc[:, bass.ds(p * (2 * P), 2 * P)]).then_inc(sums_staged, 1)
                        each_pair(pool, stage_sums)

                @block.tensor
                def _(pe):
                    steps_of(pe, turned, made)
                    pe.wait_ge(weights, 16 * len(loads))
                    for n, k in enumerate(turn):
                        pe.transpose(bank[6 + n][:, 0:P], wide_w[:, k * P:(k + 1) * P], ident[:, :]).then_inc(turned_w, 1)
                    if turn:
                        pe.wait_ge(turned_w, 2 * len(turn))

                    def transpose(p, u):
                        done(pe, staged, p + 1)
                        done(pe, xT_ready, p - 1)
                        for c in range(2):
                            mm = pe.transpose(bank[u][:, c * P:(c + 1) * P], xs[:, u, c, :], ident[:, :])
                        mm.then_inc(turned, 1)

                    def product(p, u):
                        done(pe, xT_ready, p + 1)
                        done(pe, z_ready, p - 1)
                        for c in range(2):
                            z = bank[2 + 2 * u + c] if width > 2 * P else bank[2 + 2 * u][:, c * P:(c + 1) * P]
                            mm = pe.matmul(z[:, 0:width], xT[:, u, c, :], wide_w[:, 0:width], start=True, stop=not bias)
                            if bias:
                                nb = min(width, 2 * P)
                                mm = pe.matmul(z[:, 0:nb], ones[0:1, :], wide_b[0:1, 0:nb], start=False, stop=True)
                        if agg:
                            done(pe, sums_staged, p + 1)
                            done(pe, y_ready, p - 1)
                            for c in range(2):
                                mm = pe.matmul(bank[3 + 2 * u][:, c * P:(c + 1) * P], gs[:, u, c, :], wide_w[:, P:2 * P],
                                               start=True, stop=True)
                        mm.then_inc(made, 1)
                    each_pair(pe, transpose, product)

                @block.scalar
                def _(act):
                    steps_of(act, xT_ready, z_ready)

                    def copy_xT(p, u):
                        done(act, turned, p + 1)
                        done(act, made, p - 1)
                        act.copy(flat(xT[:, u, :, :]), bank[u][:, 0:2 * P]).then_inc(xT_ready, 1)

                    def copy_z(p, u):
                        done(act, made, p + 1)
                        if stores:
                            if not (isinstance(p, int) and p < 2):
                                act.wait_ge(stored[u], (p - u) * (16 * len(stores)))
                            for c in range(2):
                                ins = act.copy(zs[:, u, c, :], bank[2 + 2 * u + c][:, 0:width])
                        else:
                            if agg:
                                done(act, y_ready, p - 1)
                            to = flat(zs[:, u, :, :]) if agg else flat(tiles(dest, p))
                            ins = act.copy(to, bank[2 + 2 * u][:, 0:2 * P])
                        ins.then_inc(z_ready, 1)
                    if stores:
                        for u in range(2):
                            copy_xT(u, u)
                        for u in range(2):
                            copy_z(u, u)
                            copy_xT(u + 2, u)
                        with act.Fori(1, (NP - 3) // 2) as it:
                            for u in range(2):
                                copy_z(it * 2 + u, u)
                                copy_xT(it * 2 + (u + 2), u)
                        copy_z(NP - 3, 0)
                        copy_xT(NP - 1, 0)
                        copy_z(NP - 2, 1)
                        copy_z(NP - 1, 0)
                    else:
                        each_pair(act, copy_xT, copy_z)

                @block.vector
                def _(dve):
                    steps_of(dve, y_ready, staged)

                    def stage(p, u):
                        done(dve, turned, p - 1)
                        dve.tensor_copy(flat(xs[:, u, :, :]), flat(tiles(x_from, p))).then_inc(staged, 1)

                    def mean(p, u):
                        done(dve, z_ready, p + 1)
                        for c in range(2):
                            ins = dve.scalar_tensor_tensor(out=flat(dest[:, bass.ds(p * 2 + c, 1), :]),
                                                           in0=bank[3 + 2 * u][:, c * P:(c + 1) * P],
                                                           scalar=rdeg[:, bass.ds(p * 2 + c, 1)], in1=zs[:, u, c, :],
                                                           op0=ALU.mult, op1=ALU.add)
                        ins.then_inc(y_ready, 1)
                    for n, k in enumerate(turn):
                        dve.wait_ge(turned_w, len(turn))
                        dve.tensor_copy(wide_w[:, k * P:(k + 1) * P], bank[6 + n][:, 0:P]).then_inc(turned_w, 1)
                    each_pair(dve, stage, mean if agg else None)

    def chain(engine, s):
        count = [0]

        def link(ins):
            ins.then_inc(s, 1)
            count[0] += 1
            engine.wait_ge(s, count[0])
        return link

    def norm_steps(sb, sem):
        stats, mean, dif = sb("stats", [P, NT, 6]), sb("mean", [P, NT]), sb("dif", [P, NT])
        var, rstd = sb("var", [P, NT]), sb("rstd", [P, NT])
        counted, var_ready, rstd_ready = sem("counted"), sem("var_ready"), sem("rstd_ready")
        norms = [0]

        def wide(v):
            return v[:, :].rearrange("p (t d) -> p t d", d=1).broadcast_to([P, NT, P])

        def steps(dve, link, x, y):
            with dve.Fori(0, NT // 2) as it:
                for u in range(2):
                    dve.bn_stats(flat(stats[:, bass.ds(it * 2 + u, 1), :]), flat(x[:, bass.ds(it * 2 + u, 1), :])).then_inc(counted, 1)
            norms[0] += 1
            dve.wait_ge(counted, norms[0] * NT)
            link(dve.tensor_tensor(mean[:, :], stats[:, :, 1], stats[:, :, 4], ALU.add))
            link(dve.tensor_tensor(dif[:, :], stats[:, :, 1], stats[:, :, 4], ALU.subtract))
            link(dve.tensor_tensor(var[:, :], stats[:, :, 2], stats[:, :, 5], ALU.add))
            link(dve.tensor_scalar(mean[:, :], mean[:, :], 0.5, None, ALU.mult))
            link(dve.tensor_tensor(dif[:, :], dif[:, :], dif[:, :], ALU.mult))
            link(dve.tensor_scalar(dif[:, :], dif[:, :], 0.25, EPS, ALU.mult, ALU.add))
            link(dve.scalar_tensor_tensor(out=var[:, :], in0=var[:, :], scalar=1.0 / P, in1=dif[:, :],
                                          op0=ALU.mult, op1=ALU.add))
            dve.sem_inc(var_ready, 1)
            dve.wait_ge(rstd_ready, norms[0])
            link(dve.reciprocal(rstd[:, :], dif[:, :]))
            link(dve.tensor_tensor(dif[:, :], rstd[:, :], rstd[:, :], ALU.mult))
            link(dve.tensor_tensor(dif[:, :], dif[:, :], var[:, :], ALU.mult))
            link(dve.tensor_scalar(dif[:, :], dif[:, :], -0.5, 1.5, ALU.mult, ALU.add))
            link(dve.tensor_tensor(rstd[:, :], rstd[:, :], dif[:, :], ALU.mult))
            link(dve.tensor_tensor(x[:, :, :], x[:, :, :], wide(mean), ALU.subtract))
            link(dve.tensor_tensor(y[:, :, :], x[:, :, :], wide(rstd), ALU.mult))

        def root(act, n):
            act.wait_ge(var_ready, n + 1)
            act.activation(dif[:, :], var[:, :], ACT.Sqrt).then_inc(rstd_ready, 1)

        return steps, root

    def over_chunks(v):
        return v[:, :].rearrange("p (a n) -> p a n", a=1).broadcast_to([P, J, P])

    def over_nodes(b):
        return rel[:, bass.ds(b, 1), :].rearrange("p b (j n) -> p (b j) n", n=1).broadcast_to([P, J, P])

    def add_window(dve, seg, b, n, added, k):
        settle(dve)
        start = dve.value_load(base[0:1, bass.ds(b, 1)], min_val=0, max_val=N)
        to = acc[:, bass.ds(start, P)]
        done(dve, added, n)
        ins = dve.tensor_tensor(to, to, seg[:, 0:P], ALU.add)
        if k:
            to = aux_acc[0:k, bass.ds(start, P)]
            ins = dve.tensor_tensor(to, to, seg[0:k, P:2 * P], ALU.add)
        ins.then_inc(added, 1)

    def gated_pass():
        with phase("gated") as (sb, sem):
            we, w2 = sb("we", [P, 2, 2 * P]), sb("w2", [P, P])
            b2_part = sb("b2_part", [P, 3, P], BF16)
            b2_rows = sb("b2_rows", [P, 2, P], BF16)
            ones_b = sb("ones_b", [P, P], BF16)
            ae_row = sb("ae_row", [1, 2, P])
            ae_w = sb("ae_w", [P, 2, P])
            ae_c = sb("ae_c", [P, 2])
            idx = sb("idx", [P, UN, J], I32)
            ea64, ea128 = sb("ea64", [P, UN, J, DE]), sb("ea128", [P, UN, J, P])
            relr, qwin = sb("relr", [P, UN, BE]), sb("qwin", [P, UN, 2 * P])
            hotT, hot = sb("hotT", [P, UN, J, P]), sb("hot", [P, UN, J, P])
            hot_b = sb("hot_b", [P, UN, J, P], BF16)
            rows = sb("rows", [P, TICKS, 2, 2 * P])
            eaT = sb("eaT", [P, 2, P])
            pre, sig = sb("pre", [P, 2, 2, 2 * P]), sb("sig", [P, 4, 2, 2 * P])
            silu, siluT, msg = sb("silu", [P, 2, 2, P]), sb("siluT", [P, 2, 2, P]), sb("msg", [P, 2, 2, P])
            ae = sb("ae", [P, UN, J, 2])
            junk = w1_sb[:, 0:8, :].rearrange("p (m k) d -> p m k d", m=2)
            we_g, we_T = h_sb[:, 0:2, :], h_sb[:, 2:4, :]
            b2, b2_res = y_sb[:, 0, :], y_sb[:, 1, :]

            loaded, consts, ready = sem("loaded"), sem("consts"), sem("ready")
            idx_in = [sem(f"idx_in{u}") for u in range(UN)]
            ea64_in = [sem(f"ea64_in{u}") for u in range(UN)]
            ea128_in = [sem(f"ea128_in{u}") for u in range(UN)]
            relr_in = [sem(f"relr_in{u}") for u in range(UN)]
            qwin_in = [sem(f"qwin_in{u}") for u in range(UN)]
            rows_in = [kept_sem(f"gated_rows_in{i}") for i in range(TICKS)]
            windows = sem("windows")
            ea_turned, made, s_turned, m_made, summed = sem("ea_turned"), sem("pre_made"), sem("s_turned"), sem("m_made"), sem("summed")
            eaT_ready, sig_ready, sT_ready = sem("eaT_ready"), sem("sig_ready"), sem("sT_ready")
            hot_b_ready, split = sem("hot_b_ready"), sem("split")
            pre_ready, silu_ready, msg_ready = sem("pre_ready"), sem("silu_ready"), sem("msg_ready")
            ae_ready, hot_ready, hotT_ready, added, ae_kept = sem("ae_ready"), sem("hot_ready"), sem("hotT_ready"), sem("added"), sem("ae_kept")
            PRE = [bank[0], bank[1]]
            SEG = [bank[2], bank[3]]
            EAT, ST, M = bank[4], bank[5], bank[6]

            def q_of(rr, it, i):
                return rr * STEPS + it * TICKS + i

            def edges_in(engine, s, rr, it, u, where):
                if u < UN - 1:
                    engine.wait_ge(s[u], (rr * ITERS + it + 1) * 16)
                else:
                    engine.wait_ge(s[u], (rr * (ITERS + 1) + it + (2 if where == "last" else 1)) * 16)

            with nc.Block() as block:
                @block.sync
                def _(sp):
                    clear_spent(sp)
                    for half in range(2):
                        rows_h = slice(half * DE, (half + 1) * DE)
                        if half == 0:
                            sp.wait_ge(ready, 4)
                        sp.dma_start(we[rows_h, half, 0:P], a["L0_gnn_w1"][2 * P:2 * P + DE, :]).then_inc(loaded, 16)
                        sp.dma_start(we[rows_h, half, P:2 * P], a["L0_gnn_wg"][2 * P:2 * P + DE, :]).then_inc(loaded, 16)
                    sp.dma_start(w2[:, :], a["L0_gnn_w2"]).then_inc(loaded, 16)
                    sp.dma_start(b2[:, :], spread(a["L0_gnn_b2"])).then_inc(loaded, 16)
                    for k in range(2):
                        sp.dma_start(we_g[:, k, :], a[f"L2_gnn_We{k + 1}"]).then_inc(loaded, 16)
                        sp.dma_start(ae_c[:, k:k + 1], a[f"L2_gnn_ae{k + 1}"].rearrange("(p a) -> p a", a=1)).then_inc(loaded, 16)
                    R = sp.value_load(rounds[0:1, 0:1], min_val=1, max_val=NT)

                    def load_batch(rr, it, u, tail):
                        b = it * UN + u
                        n = rr * NB + b
                        q = n * PAIRS
                        done(sp, pre_ready, q - 4)
                        settle(sp)
                        sp.dma_start(idx[:, u, :], flat(src_idx[:, bass.ds(b, 1), :])).then_inc(idx_in[u], 16)
                        done(sp, ea_turned, q - 4)
                        settle(sp)
                        done(sp, ae_ready, q - 4)
                        settle(sp)
                        if not tail:
                            sp.dma_start(ea64[:, u, :, :], a["edge_attr_64"][bass.ds(b * BE, BE), :]
                                         .rearrange("(p j) d -> p j d", j=J)).then_inc(ea64_in[u], 16)
                            sp.dma_start(ea128[:, u, :, :], a["edge_attr_128"][bass.ds(b * BE, BE), :]
                                         .rearrange("(p j) d -> p j d", j=J)).then_inc(ea128_in[u], 16)
                        else:
                            for buf, name, s in ((ea64, "edge_attr_64", ea64_in), (ea128, "edge_attr_128", ea128_in)):
                                e0 = (NB - 1) * BE
                                sp.dma_start(buf[0:TP, u, :, :], a[name][e0:e0 + TP * J, :]
                                             .rearrange("(p j) d -> p j d", j=J)).then_inc(s[u], 16)
                                sp.dma_start(buf[TP:TP + 1, u, 0:TR, :], a[name][e0 + TP * J:E, :]
                                             .rearrange("(p j) d -> p j d", p=1)).then_inc(s[u], 16)
                        done(sp, hotT_ready, n - 1)
                        settle(sp)
                        sp.dma_start(relr[:, u, :], rel_rows[bass.ds(b, 1), :].broadcast_to([P, BE])).then_inc(relr_in[u], 16)
                        done(sp, made, q - 4)
                        settle(sp)
                        start = sp.value_load(base[0:1, bass.ds(b, 1)], min_val=0, max_val=N)
                        sp.dma_start(qwin[:, u, :], q_tab[bass.ds(start, P), :]).then_inc(qwin_in[u], 16)

                    with sp.Fori(0, R) as rr:
                        sp.wait_ge(windows, rr * 3 + 3)
                        settle(sp)
                        with sp.Fori(0, ITERS - 1) as it:
                            for u in range(UN):
                                load_batch(rr, it, u, False)
                        for u in range(UN):
                            load_batch(rr, ITERS - 1, u, u == UN - 1)

                @block.gpsimd
                def _(pool):
                    R = pool.value_load(rounds[0:1, 0:1], min_val=1, max_val=NT)
                    with pool.Fori(0, R) as rr:
                        with pool.Fori(0, ITERS) as it:
                            for u in range(UN):
                                pool.wait_ge(idx_in[u], (rr * ITERS + it + 1) * 16)
                                for k in range(PAIRS):
                                    i = u * PAIRS + k
                                    done(pool, pre_ready, q_of(rr, it, i) - TICKS + 1)
                                    settle(pool)
                                    for c in range(2):
                                        j = 2 * k + c
                                        pool.indirect_dma_start(out=rows[:, i, c, :], out_offset=None, in_=p_tab,
                                                                in_offset=bass.IndirectOffsetOnAxis(ap=idx[:, u, j:j + 1], axis=0)
                                                                ).then_inc(rows_in[i], 16)

                @block.tensor
                def _(pe):
                    steps_of(pe, ea_turned, made, s_turned, m_made, summed)
                    pe.wait_ge(loaded, 16 * 10)
                    for k in range(2):
                        pe.transpose(bank[k][:, 0:P], we_g[:, k, :], ident[:, :]).then_inc(consts, 1)
                    pe.wait_ge(consts, 4)
                    for k in range(2):
                        pe.matmul(bank[2][0:1, k * P:(k + 1) * P], ae_c[:, k:k + 1], we_T[:, k, :], start=True, stop=True).then_inc(consts, 1)
                    pe.wait_ge(consts, 7)
                    pe.matmul(bank[3][:, 0:2 * P], ones[0:1, :], flat(ae_row[0:1, :, :]), start=True, stop=True).then_inc(consts, 1)
                    pe.wait_ge(ready, 4)
                    pe.wait_ge(split, 5 + 6)
                    R = pe.value_load(rounds[0:1, 0:1], min_val=1, max_val=NT)

                    def tick(rr, it, i, where):
                        if (w := lagged(i, 0, where)):
                            m, back = w
                            q, u, k = q_of(rr, it + back, m), m // PAIRS, m % PAIRS
                            if k == 0:
                                edges_in(pe, ea64_in, rr, it, u, where)
                            done(pe, eaT_ready, q)
                            pe.transpose(EAT[:, 0:P], ea64[:, u, 2 * k:2 * k + 2, :].rearrange("p j d -> p (j d)"),
                                         ident[:, :]).then_inc(ea_turned, 1)
                        if (w := lagged(i, 2, where)):
                            m, back = w
                            q, u, k = q_of(rr, it + back, m), m // PAIRS, m % PAIRS
                            done(pe, eaT_ready, q + 1)
                            done(pe, hotT_ready, rr * NB + (it + back) * UN + u + 1)
                            pe.wait_ge(qwin_in[u], (rr * ITERS + it + back + 1) * 16)
                            done(pe, pre_ready, q - 1)
                            for c in range(2):
                                to = PRE[m % 2][:, c * 2 * P:(c + 1) * 2 * P]
                                pe.matmul(to, hotT[:, u, 2 * k + c, :], qwin[:, u, :], start=True, stop=False)
                                mm = pe.matmul(to, eaT[:, m % 2, :], we[:, c, :], start=False, stop=True)
                            mm.then_inc(made, 1)
                        if (w := lagged(i, 4, where)):
                            m, back = w
                            q = q_of(rr, it + back, m)
                            done(pe, silu_ready, q + 1)
                            done(pe, sT_ready, q)
                            for c in range(2):
                                mm = pe.transpose(ST[:, c * P:(c + 1) * P], silu[:, m % 2, c, :], ident[:, :])
                            mm.then_inc(s_turned, 1)
                        if (w := lagged(i, 5, where)):
                            m, back = w
                            q = q_of(rr, it + back, m)
                            done(pe, sT_ready, q + 1)
                            done(pe, msg_ready, q)
                            pe.matmul(M[:, 0:2 * P], ones_b[:, :], flat(b2_rows[:, :, :]), start=True, stop=False,
                                      skip_group_check=True)
                            for c in range(2):
                                mm = pe.matmul(M[:, c * P:(c + 1) * P], siluT[:, m % 2, c, :], w2[:, :], start=False,
                                               stop=True, skip_group_check=True)
                            mm.then_inc(m_made, 1)
                        if (w := lagged(i, 6, where)):
                            m, back = w
                            q, u, k = q_of(rr, it + back, m), m // PAIRS, m % PAIRS
                            b = rr * NB + (it + back) * UN + u
                            done(pe, msg_ready, q + 1)
                            if k == 0:
                                done(pe, hot_ready, b + 1)
                                done(pe, hot_b_ready, b + 1)
                                done(pe, added, b - 1)
                            for c in range(2):
                                j = 2 * k + c
                                pe.matmul(SEG[u][:, 0:P], msg[:, m % 2, c, :], hot[:, u, j, :],
                                          start=(j == 0), stop=(j == J - 1), skip_group_check=True)
                                mm = pe.matmul(SEG[u][0:1, P:2 * P], ones_b[:, 0:1], hot_b[:, u, j, :],
                                               start=False, stop=(j == J - 1), skip_group_check=True)
                            mm.then_inc(summed, 1)

                    with pe.Fori(0, R) as rr:
                        for i in range(TICKS):
                            tick(rr, 0, i, "first")
                        with pe.Fori(1, ITERS - 1) as it:
                            for i in range(TICKS):
                                tick(rr, it, i, "body")
                        for i in range(TICKS):
                            tick(rr, ITERS - 1, i, "last")
                        for i in range(6):
                            tick(rr, ITERS, i, "tail")

                @block.scalar
                def _(act):
                    steps_of(act, eaT_ready, sig_ready, sT_ready, hot_b_ready)
                    R = act.value_load(rounds[0:1, 0:1], min_val=1, max_val=NT)

                    def tick(rr, it, i, where):
                        if (w := lagged(i, 0, where)):
                            m, back = w
                            q = q_of(rr, it + back, m)
                            done(act, ea_turned, q + 1)
                            done(act, made, q - 1)
                            act.copy(eaT[:, m % 2, :], EAT[:, 0:P]).then_inc(eaT_ready, 1)
                        if (w := lagged(i, 2, where)):
                            m, back = w
                            q = q_of(rr, it + back, m)
                            done(act, pre_ready, q + 1)
                            done(act, msg_ready, q - 3)
                            act.activation(flat(sig[:, m % 4, :, :]), flat(pre[:, m % 2, :, :]), ACT.Sigmoid).then_inc(sig_ready, 1)
                        if (w := lagged(i, 4, where)):
                            m, back = w
                            q = q_of(rr, it + back, m)
                            done(act, s_turned, q + 1)
                            done(act, m_made, q - 1)
                            act.copy(flat(siluT[:, m % 2, :, :]), ST[:, 0:2 * P]).then_inc(sT_ready, 1)
                        if (w := lagged(i, 5, where)) and w[0] % PAIRS == 0:
                            m, back = w
                            q, u = q_of(rr, it + back, m), m // PAIRS
                            done(act, hot_ready, rr * NB + (it + back) * UN + u + 1)
                            done(act, summed, q - 4)
                            act.copy(hot_b[:, u, :, :], hot[:, u, :, :]).then_inc(hot_b_ready, 1)

                    with act.Fori(0, R) as rr:
                        for i in range(TICKS):
                            tick(rr, 0, i, "first")
                        with act.Fori(1, ITERS) as it:
                            for i in range(TICKS):
                                tick(rr, it, i, "body")
                        for i in range(5):
                            tick(rr, ITERS, i, "tail")

                @block.vector
                def _(dve):
                    steps_of(dve, pre_ready, silu_ready, msg_ready, ae_ready, hot_ready, hotT_ready, added, ae_kept)
                    dve.memset(we[:, :, :], 0.0).then_inc(ready, 1)
                    dve.memset(acc[:, :], 0.0).then_inc(ready, 1)
                    dve.memset(aux_acc[:, :], 0.0).then_inc(ready, 1)
                    dve.memset(ones_b[:, :], 1.0).then_inc(ready, 1)
                    dve.wait_ge(loaded, 16 * 10)
                    link = chain(dve, split)
                    link(dve.memset(b2_rows[:, :, :], 0.0))
                    link(dve.tensor_copy(b2_part[:, 0, :], b2[:, :]))
                    link(dve.tensor_tensor(b2_res[:, :], b2[:, :], b2_part[:, 0, :], ALU.subtract))
                    link(dve.tensor_copy(b2_part[:, 1, :], b2_res[:, :]))
                    link(dve.tensor_tensor(b2_part[:, 2, :], b2_res[:, :], b2_part[:, 1, :], ALU.subtract))
                    for n in range(3):
                        for c in range(2):
                            dve.tensor_copy(b2_rows[32 * n:32 * n + 1, c, :], b2_part[32 * n:32 * n + 1, n, :]).then_inc(split, 1)
                    dve.wait_ge(consts, 2)
                    dve.tensor_copy(we_T[:, 0, :], bank[0][:, 0:P]).then_inc(consts, 1)
                    dve.tensor_copy(we_T[:, 1, :], bank[1][:, 0:P]).then_inc(consts, 1)
                    dve.wait_ge(consts, 6)
                    dve.tensor_copy(flat(ae_row[0:1, :, :]), bank[2][0:1, 0:2 * P]).then_inc(consts, 1)
                    dve.wait_ge(consts, 8)
                    dve.tensor_copy(flat(ae_w[:, :, :]), bank[3][:, 0:2 * P]).then_inc(consts, 1)
                    start_windows(dve, windows)
                    dve.wait_ge(consts, 9)
                    dve.wait_ge(windows, 3)
                    R = dve.value_load(rounds[0:1, 0:1], min_val=1, max_val=NT)

                    def tick(rr, it, i, where):
                        if (w := lagged(i, 0, where)):
                            m, back = w
                            q, u, k = q_of(rr, it + back, m), m // PAIRS, m % PAIRS
                            b = it * UN + u
                            if k == 0:
                                dve.wait_ge(relr_in[u], (rr * ITERS + it + 1) * 16)
                                done(dve, made, q - 4)
                                dve.tensor_scalar(hotT[:, u, :, :], relr[:, u, :].rearrange("n (p j) -> n j p", j=J),
                                                  part[:, 0:1], None, ALU.is_equal).then_inc(hotT_ready, 1)
                                edges_in(dve, ea128_in, rr, it, u, where)
                                done(dve, ae_kept, rr * NB + b - 1)
                            done(dve, ae_ready, q - 1)
                            for c in range(2):
                                for l in range(2):
                                    j = 2 * k + c
                                    ins = dve.tensor_tensor_reduce(out=junk[:, m % 2, 2 * c + l, :], in0=ea128[:, u, j, :],
                                                                   in1=ae_w[:, l, :], scale=1.0, scalar=0.0,
                                                                   op0=ALU.mult, op1=ALU.add,
                                                                   accum_out=ae[:, u, j, l:l + 1])
                            ins.then_inc(ae_ready, 1)
                            if k == PAIRS - 1:
                                done(dve, ae_ready, q + 1)
                                dve.tensor_copy(ae_tab[:, bass.ds(b, 1), :, :].rearrange("p b j l -> p (b j) l"),
                                                ae[:, u, :, :]).then_inc(ae_kept, 1)
                        if (w := lagged(i, 2, where)):
                            m, back = w
                            q = q_of(rr, it + back, m)
                            done(dve, made, q + 1)
                            dve.wait_ge(rows_in[m], (rr * ITERS + it + back + 1) * 32)
                            done(dve, sig_ready, q - 1)
                            done(dve, silu_ready, q - 1)
                            dve.tensor_tensor(flat(pre[:, m % 2, :, :]), PRE[m % 2][:, :], flat(rows[:, m, :, :]),
                                              ALU.add).then_inc(pre_ready, 1)
                        if (w := lagged(i, 3, where)):
                            m, back = w
                            q = q_of(rr, it + back, m)
                            done(dve, sig_ready, q + 1)
                            done(dve, s_turned, q - 1)
                            dve.tensor_tensor(silu[:, m % 2, :, :], pre[:, m % 2, :, 0:P], sig[:, m % 4, :, 0:P],
                                              ALU.mult).then_inc(silu_ready, 1)
                        if (w := lagged(i, 4, where)) and w[0] % PAIRS == 0:
                            m, back = w
                            q, u = q_of(rr, it + back, m), m // PAIRS
                            b = (it + back) * UN + u
                            done(dve, summed, q - 4)
                            dve.tensor_tensor(hot[:, u, :, :], over_chunks(iota), over_nodes(b), ALU.is_equal).then_inc(hot_ready, 1)
                        if (w := lagged(i, 5, where)):
                            m, back = w
                            q = q_of(rr, it + back, m)
                            done(dve, m_made, q + 1)
                            done(dve, summed, q - 1)
                            dve.tensor_tensor(msg[:, m % 2, :, :], M[:, 0:2 * P].rearrange("p (c d) -> p c d", c=2),
                                              sig[:, m % 4, :, P:2 * P], ALU.mult).then_inc(msg_ready, 1)
                        if (w := lagged(i, 7, where)) and w[0] % PAIRS == PAIRS - 1:
                            m, back = w
                            q, u = q_of(rr, it + back, m), m // PAIRS
                            b = (it + back) * UN + u
                            done(dve, summed, q + 1)
                            add_window(dve, SEG[u], b, rr * NB + b, added, 1)

                    with dve.Fori(0, R) as rr:
                        dve.wait_ge(windows, rr * 3 + 3)
                        for i in range(TICKS):
                            tick(rr, 0, i, "first")
                        with dve.Fori(1, ITERS - 1) as it:
                            for i in range(TICKS):
                                tick(rr, it, i, "body")
                        for i in range(TICKS):
                            tick(rr, ITERS - 1, i, "last")
                        for i in range(7):
                            tick(rr, ITERS, i, "tail")
                        done(dve, hot_ready, (rr + 1) * NB)
                        next_windows(dve, windows)

    def edge_pass(name, table, weighted=0):
        with phase(name) as (sb, sem):
            idx, hot = sb("idx", [P, UN, J], I32), sb("hot", [P, UN, J, P])
            rows = sb("rows", [P, TICKS, 2, P])
            aux = sb("aux", [P, UN, J, 3])
            scaled = sb("scaled", [P, 4, 2, P])
            idx_in = [sem(f"idx_in{u}") for u in range(UN)]
            rows_in = [kept_sem(f"{name}_rows_in{i}") for i in range(TICKS)]
            windows, ready = sem("windows"), sem("ready")
            hot_ready, added, summed, scaled_ready, aux_ready = sem("hot_ready"), sem("added"), sem("summed"), sem("scaled_ready"), sem("aux_ready")
            used = scaled_ready if weighted else summed
            SEG = [bank[0], bank[1]]

            with nc.Block() as block:
                @block.sync
                def _(sp):
                    clear_spent(sp)
                    R = sp.value_load(rounds[0:1, 0:1], min_val=1, max_val=NT)
                    with sp.Fori(0, R) as rr:
                        with sp.Fori(0, ITERS) as it:
                            for u in range(UN):
                                done(sp, used, rr * STEPS + it * TICKS + u * PAIRS - PAIRS)
                                settle(sp)
                                sp.dma_start(idx[:, u, :], flat(src_idx[:, bass.ds(it * UN + u, 1), :])).then_inc(idx_in[u], 16)

                @block.gpsimd
                def _(pool):
                    R = pool.value_load(rounds[0:1, 0:1], min_val=1, max_val=NT)
                    with pool.Fori(0, R) as rr:
                        with pool.Fori(0, ITERS) as it:
                            for u in range(UN):
                                pool.wait_ge(idx_in[u], (rr * ITERS + it + 1) * 16)
                                for k in range(PAIRS):
                                    i = u * PAIRS + k
                                    done(pool, used, rr * STEPS + it * TICKS + i - TICKS + 1)
                                    settle(pool)
                                    for c in range(2):
                                        j = 2 * k + c
                                        pool.indirect_dma_start(out=rows[:, i, c, :], out_offset=None, in_=table,
                                                                in_offset=bass.IndirectOffsetOnAxis(ap=idx[:, u, j:j + 1], axis=0)
                                                                ).then_inc(rows_in[i], 16)

                if weighted:
                    @block.scalar
                    def _(act):
                        steps_of(act, scaled_ready)
                        R = act.value_load(rounds[0:1, 0:1], min_val=1, max_val=NT)
                        with act.Fori(0, R) as rr:
                            with act.Fori(0, ITERS) as it:
                                for i in range(TICKS):
                                    u, k = i // PAIRS, i % PAIRS
                                    q = rr * STEPS + it * TICKS + i
                                    if k == 0:
                                        done(act, aux_ready, (rr * NB + it * UN + u + 1) * 2)
                                    act.wait_ge(rows_in[i], (rr * ITERS + it + 1) * 32)
                                    done(act, summed, q - 3)
                                    for c in range(2):
                                        ins = act.activation(scaled[:, i % 4, c, :], rows[:, i, c, :], ACT.Copy,
                                                             scale=aux[:, u, 2 * k + c, 0:1])
                                    ins.then_inc(scaled_ready, 1)

                @block.tensor
                def _(pe):
                    steps_of(pe, summed)
                    R = pe.value_load(rounds[0:1, 0:1], min_val=1, max_val=NT)
                    with pe.Fori(0, R) as rr:
                        with pe.Fori(0, ITERS) as it:
                            for i in range(TICKS):
                                u, k = i // PAIRS, i % PAIRS
                                q = rr * STEPS + it * TICKS + i
                                n = rr * NB + it * UN + u
                                if k == 0:
                                    done(pe, hot_ready, n + 1)
                                    done(pe, added, n - 1)
                                    if weighted:
                                        done(pe, aux_ready, n * 2 + 2)
                                if weighted:
                                    done(pe, scaled_ready, q + 1)
                                else:
                                    pe.wait_ge(rows_in[i], (rr * ITERS + it + 1) * 32)
                                for c in range(2):
                                    j = 2 * k + c
                                    lhsT = scaled[:, i % 4, c, :] if weighted else rows[:, i, c, :]
                                    mm = pe.matmul(SEG[u][:, 0:P], lhsT, hot[:, u, j, :], start=(j == 0),
                                                   stop=(j == J - 1), skip_group_check=True)
                                    if weighted:
                                        mm = pe.matmul(SEG[u][0:3, P:2 * P], aux[:, u, j, :], hot[:, u, j, :],
                                                       start=False, stop=(j == J - 1), skip_group_check=True)
                                mm.then_inc(summed, 1)

                @block.vector
                def _(dve):
                    steps_of(dve, hot_ready, added, aux_ready)
                    dve.memset(acc[:, :], 0.0).then_inc(ready, 1)
                    dve.memset(aux_acc[:, :], 0.0).then_inc(ready, 1)
                    start_windows(dve, windows)
                    dve.wait_ge(ready, 2)
                    R = dve.value_load(rounds[0:1, 0:1], min_val=1, max_val=NT)

                    def onehots(rr, it, u):
                        b, n = it * UN + u, rr * NB + it * UN + u
                        done(dve, summed, n * PAIRS - PAIRS)
                        if weighted:
                            dve.tensor_copy(aux[:, u, :, 0:2], w_tab[:, bass.ds(b, 1), :, :].rearrange("p b j l -> p (b j) l")).then_inc(aux_ready, 1)
                            dve.tensor_copy(aux[:, u, :, 2:3], ae_tab[:, bass.ds(b, 1), :, weighted - 1:weighted]
                                            .rearrange("p b j l -> p (b j) l")).then_inc(aux_ready, 1)
                        dve.tensor_tensor(hot[:, u, :, :], over_chunks(iota), over_nodes(b), ALU.is_equal).then_inc(hot_ready, 1)

                    def add(rr, b, u):
                        n = rr * NB + b
                        done(dve, summed, n * PAIRS + PAIRS)
                        add_window(dve, SEG[u], b, n, added, 3 if weighted else 0)

                    with dve.Fori(0, R) as rr:
                        dve.wait_ge(windows, rr * 3 + 3)
                        onehots(rr, 0, 0)
                        onehots(rr, 0, 1)
                        with dve.Fori(1, ITERS) as it:
                            for u in range(UN):
                                add(rr, it * UN - UN + u, u)
                                onehots(rr, it, u)
                        for u in range(UN):
                            add(rr, NB - UN + u, u)
                        done(dve, hot_ready, rr * NB + NB)
                        next_windows(dve, windows)

    def turn_aux(pe, k, s):
        for t in range(NT):
            mm = pe.transpose(bank[7][:, t * k:(t + 1) * k], aux_acc[0:k, t * P:(t + 1) * P], ident[0:k, 0:k])
        mm.then_inc(s, 1)

    def aux_nodes(k):
        return bank[7][:, 0:NT * k].rearrange("p (t k) -> p t k", k=k)

    def degrees():
        with phase("degrees") as (sb, sem):
            turned, v, numbered = sem("turned"), sem("v"), sem("numbered")
            cnt, start, spare = sb("cnt", [P, NT]), sb("start", [P, NT]), sb("spare", [P, NT])
            zero_row, ends_row = flat(h_sb[:, :, :])[0:1, :], flat(w1_sb[:, :, :])[0:1, :]
            with nc.Block() as block:
                @block.sync
                def _(sp):
                    clear_spent(sp)

                @block.gpsimd
                def _(pool):
                    pool.iota(spare[:, :], pattern=[[P, NT]], base=NB * BE, channel_multiplier=1,
                              allow_small_or_imprecise_dtypes=True).then_inc(numbered, 1)

                @block.tensor
                def _(pe):
                    turn_aux(pe, 1, turned)
                    pe.wait_ge(v, 2)
                    for t in range(NT):
                        mm = pe.transpose(bank[6][:, t:t + 1], ends_row[:, t * P:(t + 1) * P], ident[0:1, 0:1])
                    mm.then_inc(turned, 1)

                @block.vector
                def _(dve):
                    link = chain(dve, v)
                    link(dve.memset(zero_row, 0.0))
                    link(dve.tensor_tensor_scan(ends_row, aux_acc[0:1, :], zero_row, 0.0, ALU.add, ALU.add))
                    dve.wait_ge(turned, 1)
                    link(dve.tensor_scalar(cnt[:, :], aux_nodes(1)[:, :, 0], 1.0, None, ALU.max))
                    link(dve.tensor_scalar(has[:, :], aux_nodes(1)[:, :, 0], 1.0, None, ALU.min))
                    link(dve.reciprocal(rdeg[:, :], cnt[:, :]))
                    dve.wait_ge(turned, 2)
                    dve.wait_ge(numbered, 1)
                    link(dve.tensor_copy(start[:, :], bank[6][:, 0:NT]))
                    link(dve.tensor_tensor(start[:, :], start[:, :], aux_nodes(1)[:, :, 0], ALU.subtract))
                    link(dve.tensor_tensor(start[:, :], start[:, :], spare[:, :], ALU.subtract))
                    link(dve.tensor_tensor(start[:, :], start[:, :], has[:, :], ALU.mult))
                    link(dve.tensor_tensor(start[:, :], start[:, :], spare[:, :], ALU.add))
                    link(dve.tensor_copy(seg_start[:, :], start[:, :]))

    def over_tiles(v):
        return v[:, :].rearrange("p (a d) -> p a d", a=1).broadcast_to([P, NT, P])

    def over_features(v):
        return v[:, :].rearrange("p (t d) -> p t d", d=1).broadcast_to([P, NT, P])

    def finish_layer(name, gate=False, affine=None, residual=True, outer=False, store=None):
        with phase(name) as (sb, sem):
            norm, root = norm_steps(sb, sem)
            gb = sb("gb", [P, 2, P])
            loaded, v, sig, fin, stored = sem("loaded"), sem("v"), sem("sig"), sem("fin"), sem("stored")
            result = x_sb if residual else cur
            with nc.Block() as block:
                @block.sync
                def _(sp):
                    clear_spent(sp)
                    if affine:
                        for k in range(2):
                            sp.dma_start(gb[:, k, :], spread(a[affine[k]])).then_inc(loaded, 16)
                    sp.wait_ge(fin, 1)
                    if outer:
                        sp.dma_start(by_tile(out[0:FT * P, :]), result[:, 0:FT, :]).then_inc(stored, 16)
                        sp.dma_start(out[FT * P:N, :], result[0:FR, FT, :]).then_inc(stored, 16)
                        sp.wait_ge(stored, 32)
                    else:
                        if store is not None:
                            sp.dma_start(by_tile(store), result[:, :, :]).then_inc(stored, 16)
                            sp.wait_ge(stored, 16)

                @block.scalar
                def _(act):
                    if gate:
                        act.activation(flat(w1_sb[:, :, :]), flat(y_sb[:, :, :]), ACT.Sigmoid).then_inc(sig, 1)
                    for n in range((affine is not None) + residual):
                        root(act, n)

                @block.vector
                def _(dve):
                    link = chain(dve, v)
                    if gate:
                        dve.wait_ge(sig, 1)
                        link(dve.tensor_tensor(y_sb[:, :, :], y_sb[:, :, :], w1_sb[:, :, :], ALU.mult))
                    if affine:
                        norm(dve, link, y_sb, y_sb)
                        dve.wait_ge(loaded, 32)
                        link(dve.tensor_tensor(y_sb[:, :, :], y_sb[:, :, :], over_tiles(gb[:, 0, :]), ALU.mult))
                        link(dve.tensor_tensor(y_sb[:, :, :], y_sb[:, :, :], over_tiles(gb[:, 1, :]), ALU.add))
                        link(dve.tensor_scalar((y_sb if residual else cur)[:, :, :], y_sb[:, :, :], 0.0, None, ALU.max))
                    if residual:
                        link(dve.tensor_tensor(y_sb[:, :, :], y_sb[:, :, :], x_sb[:, :, :], ALU.add))
                        norm(dve, link, y_sb, x_sb)
                    dve.sem_inc(fin, 1)

    def attend(l, table, a_s, a_d):
        ROWS = 4
        with phase(f"attend{l}") as (sb, sem):
            att = sb("att", [P, 2, P])
            res = sb("res", [P, NT])
            tab = sb("tab", [P, P], BF16)
            hik, hi_off = sb("hik", [P, 1]), sb("hi_off", [P, 2])
            pick = sb("pick", [P, 2 * P - 1], BF16)
            ids = sb("ids", [P, ROWS, 2, BE], BF16)
            hot_lo, found = sb("hot_lo", [P, 2, BE], BF16), sb("found", [P, 2, BE], BF16)
            ae_s, alpha, ad_in = sb("ae_s", [NB, BE]), sb("alpha", [NB, BE]), sb("ad_in", [NB, BE])
            run, seg_max, ex, ml = sb("run", [NB, BE]), sb("seg_max", [NB, BE]), sb("ex", [NB, BE]), sb("ml", [NB, BE])
            pass_row, end_row, carry_row = sb("pass_row", [1, NB]), sb("end_row", [1, NB]), sb("carry_row", [1, NB + 1])
            carry = sb("carry", [NB, 1])
            loaded, stored, v, t, consts = sem("loaded"), sem("stored"), sem("v"), sem("t"), sem("consts")
            scanned, carried, shifted, weighed = sem("scanned"), sem("carried"), sem("shifted"), sem("weighed")
            max_ready = sem("max_ready")
            times_ad, ad_ready, ad_loaded = sem("times_ad"), sem("ad_ready"), sem("ad_loaded")
            scattered = kept_sem(f"attend{l}_scattered")
            ids_in = [sem(f"ids_in{i}") for i in range(ROWS)]
            hot_ready, found_ready, looked, picked = sem("hot_ready"), sem("found_ready"), sem("looked"), sem("picked")
            TURNS = NB // ROWS
            assert NB % ROWS == 0
            OUT = [bank[4], bank[5]]
            HALF = BE // 2

            with nc.Block() as block:
                @block.sync
                def _(sp):
                    clear_spent(sp)
                    for k, side in enumerate("sd"):
                        sp.dma_start(att[:, k, :], spread(a[f"L2_gnn_a{l}{side}"])).then_inc(loaded, 16)
                    sp.dma_start(by_tile(table), h_sb[:, :, :]).then_inc(stored, 16)
                    with sp.Fori(0, TURNS) as it:
                        for r in range(ROWS):
                            done(sp, found_ready, it * ROWS + r - ROWS + 1)
                            settle(sp)
                            sp.dma_start(ids[:, r, :, :], id_rows[bass.ds(it * ROWS + r, 1), :, :]
                                         .rearrange("b k e -> b (k e)").broadcast_to([P, 2 * BE])).then_inc(ids_in[r], 16)
                    sp.wait_ge(scattered, 16 * NT)
                    sp.dma_start(ad_in[:, :], first_ad[0:NB * BE, :].rearrange("(b e) a -> b (e a)", e=BE)).then_inc(ad_loaded, 16)
                    sp.wait_ge(stored, 16)

                @block.gpsimd
                def _(pool):
                    pool.wait_ge(loaded, 32)
                    pool.tensor_tensor(y_sb[:, :, :], h_sb[:, :, :], over_tiles(att[:, 1, :]), ALU.mult).then_inc(times_ad, 1)
                    pool.wait_ge(ad_ready, 1)
                    for n in range(NT):
                        pool.indirect_dma_start(out=first_ad,
                                                out_offset=bass.IndirectOffsetOnAxis(ap=seg_start[:, n:n + 1], axis=0),
                                                in_=a_d[:, n:n + 1], in_offset=None).then_inc(scattered, 16)

                @block.tensor
                def _(pe):
                    steps_of(pe, looked, picked)
                    for j in range(J):
                        to = bank[6 + j // PAIRS][0:NB, (j % PAIRS) * P:(j % PAIRS + 1) * P]
                        mm = pe.transpose(to, ae_tab[:, :, j, l - 1], ident[:, :])
                    mm.then_inc(t, 1)
                    pe.wait_ge(consts, 1)
                    pe.matmul(OUT[0][:, :], pick[:, 0:P], found[:, 0, 0:HALF], start=True, stop=False, skip_group_check=True)
                    pe.matmul(OUT[1][:, :], pick[:, 0:P], found[:, 0, 0:HALF], start=True, stop=False, skip_group_check=True)

                    def tick(it, i, where):
                        if (w := lagged(i, 0, where, ROWS)):
                            m, back = w
                            b = (it + back) * ROWS + m
                            done(pe, hot_ready, b + 1)
                            done(pe, found_ready, b - 1)
                            for h in range(2):
                                mm = pe.matmul(bank[2 * (m % 2) + h][:, :], tab[:, :],
                                               hot_lo[:, m % 2, h * HALF:(h + 1) * HALF], start=True, stop=True)
                            mm.then_inc(looked, 1)
                        if (w := lagged(i, 1, where, ROWS)):
                            m, back = w
                            b = (it + back) * ROWS + m
                            done(pe, found_ready, b + 1)
                            for h in range(2):
                                mm = pe.matmul(OUT[h][:, :], pick[:, bass.ds(b * (-1) + (P - 1), P)],
                                               found[:, m % 2, h * HALF:(h + 1) * HALF], start=False, stop=where == "tail",
                                               skip_group_check=True)
                            mm.then_inc(picked, 1)

                    for i in range(ROWS):
                        tick(0, i, "first")
                    with pe.Fori(1, TURNS) as it:
                        for i in range(ROWS):
                            tick(it, i, "body")
                    tick(TURNS, 0, "tail")
                    for n, (end, through) in enumerate(((run[:, BE - 1:BE], pass_f), (run[:, BE - 1:BE], pass_f),
                                                        (seg_max[:, 0:1], pass_b))):
                        at = n // 2
                        pe.wait_ge(scanned, n + 1)
                        pe.transpose(bank[0][0:1, 0:NB], end, ident[0:NB, 0:NB])
                        pe.transpose(bank[0][0:1, P:P + NB], through[:, :], ident[0:NB, 0:NB]).then_inc(t, 1)
                        pe.wait_ge(carried, n + 1)
                        pe.transpose(bank[0][0:NB, 2 * P:2 * P + 1], carry_row[0:1, at:at + NB], ident[0:1, 0:1]).then_inc(t, 1)
                    for n, (frm, s) in enumerate(((ml, max_ready), (ex, weighed))):
                        pe.wait_ge(s, 1)
                        for j in range(J):
                            mm = pe.transpose(bank[2 + n][:, j * NB:(j + 1) * NB], frm[:, j:BE:J], ident[0:NB, 0:NB])
                        mm.then_inc(t, 1)

                @block.scalar
                def _(act):
                    act.wait_ge(shifted, 1)
                    act.activation(ex[:, :], run[:, :], ACT.Exp).then_inc(weighed, 1)

                @block.vector
                def _(dve):
                    steps_of(dve, hot_ready, found_ready)
                    link = chain(dve, v)
                    link(dve.memset(tab[:, :], 0.0))
                    link(dve.memset(found[:, :, :], 0.0))
                    link(dve.memset(pick[:, :], 0.0))
                    link(dve.memset(pick[:, P - 1:P], 1.0))
                    for n in range(2):
                        link(dve.tensor_scalar(hi_off[:, n:n + 1], part0[:, :], float((n + 1) * NT), -float(NT), ALU.is_ge, ALU.mult))
                    link(dve.tensor_tensor(hik[:, :], part0[:, :], hi_off[:, 0:1], ALU.add))
                    link(dve.tensor_tensor(hik[:, :], hik[:, :], hi_off[:, 1:2], ALU.add))
                    dve.wait_ge(loaded, 32)
                    link(dve.tensor_tensor(w1_sb[:, :, :], h_sb[:, :, :], over_tiles(att[:, 0, :]), ALU.mult))
                    link(dve.tensor_reduce(a_s[:, :], w1_sb[:, :, :], AX, ALU.add))
                    link(dve.tensor_copy(tab[:, 0:NT], a_s[:, :]))
                    link(dve.tensor_tensor(res[:, :], a_s[:, :], tab[:, 0:NT], ALU.subtract))
                    link(dve.tensor_copy(tab[:, NT:2 * NT], res[:, :]))
                    link(dve.tensor_tensor(res[:, :], res[:, :], tab[:, NT:2 * NT], ALU.subtract))
                    link(dve.tensor_copy(tab[:, 2 * NT:3 * NT], res[:, :]))
                    dve.sem_inc(consts, 1)

                    def tick(it, i, where):
                        if (w := lagged(i, 0, where, ROWS)):
                            m, back = w
                            b = (it + back) * ROWS + m
                            dve.wait_ge(ids_in[m], (it + back + 1) * 16)
                            done(dve, looked, b - 1)
                            dve.tensor_scalar(hot_lo[:, m % 2, :], ids[:, m, 0, :], part0[:, 0:1], None,
                                              ALU.is_equal).then_inc(hot_ready, 1)
                        if (w := lagged(i, 1, where, ROWS)):
                            m, back = w
                            b = (it + back) * ROWS + m
                            done(dve, looked, b + 1)
                            done(dve, picked, b - 1)
                            for h in range(2):
                                ins = dve.scalar_tensor_tensor(out=found[:, m % 2, h * HALF:(h + 1) * HALF],
                                                               in0=ids[:, m, 1, h * HALF:(h + 1) * HALF],
                                                               scalar=hik[:, 0:1], in1=bank[2 * (m % 2) + h][:, :],
                                                               op0=ALU.is_equal, op1=ALU.mult)
                            ins.then_inc(found_ready, 1)

                    for i in range(ROWS):
                        tick(0, i, "first")
                    dve.wait_ge(times_ad, 1)
                    link(dve.tensor_reduce(a_d[:, :], y_sb[:, :, :], AX, ALU.add))
                    dve.sem_inc(ad_ready, 1)
                    dve.wait_ge(t, 1)
                    for h in range(2):
                        link(dve.tensor_copy(ae_s[:, :].rearrange("b (p j) -> b j p", j=J)[:, h * PAIRS:(h + 1) * PAIRS, :],
                                             bank[6 + h][0:NB, :].rearrange("b (j p) -> b j p", p=P)))
                    with dve.Fori(1, TURNS) as it:
                        for i in range(ROWS):
                            tick(it, i, "body")
                    tick(TURNS, 0, "tail")

                    rev = slice(None, None, -1)
                    fwd = slice(None)

                    def spread_max(n, to, pen, frm, way):
                        link(dve.tensor_tensor_scan(to[:, way], pen[:, way], frm[:, way], -BIG, ALU.add, ALU.max))
                        dve.sem_inc(scanned, 1)
                        dve.wait_ge(t, 2 + 2 * n)
                        link(dve.tensor_copy(end_row[:, :], bank[0][0:1, 0:NB]))
                        link(dve.tensor_copy(pass_row[:, :], bank[0][0:1, P:P + NB]))
                        link(dve.memset(carry_row[:, :], -BIG))
                        carries = carry_row[:, 1:NB + 1] if way is fwd else carry_row[:, 0:NB]
                        link(dve.tensor_tensor_scan(carries[:, way], pass_row[:, way], end_row[:, way], -BIG, ALU.add, ALU.max))
                        dve.sem_inc(carried, 1)
                        dve.wait_ge(t, 3 + 2 * n)
                        link(dve.tensor_copy(carry[:, :], bank[0][0:NB, 2 * P:2 * P + 1]))
                        link(dve.tensor_tensor_scan(to[:, way], pen[:, way], frm[:, way], carry[:, 0:1], ALU.add, ALU.max))

                    dve.wait_ge(ad_loaded, 16)
                    spread_max(0, run, pen_f, ad_in, fwd)
                    link(dve.tensor_tensor(ae_s[:, :], ae_s[:, :], run[:, :], ALU.add))
                    done(dve, picked, NB)
                    for h in range(2):
                        cols = slice(h * HALF, (h + 1) * HALF)
                        link(dve.tensor_tensor(alpha[:, cols], ae_s[:, cols], OUT[h][0:NB, :], ALU.add))
                    link(dve.scalar_tensor_tensor(out=alpha[:, :], in0=alpha[:, :], scalar=SLOPE, in1=alpha[:, :], op0=ALU.mult, op1=ALU.max))
                    spread_max(1, run, pen_f, alpha, fwd)
                    spread_max(2, seg_max, pen_b, run, rev)
                    link(dve.tensor_tensor(run[:, :], alpha[:, :], seg_max[:, :], ALU.subtract))
                    dve.sem_inc(shifted, 1)
                    link(dve.tensor_tensor(ml[:, :], seg_max[:, :], last[:, :], ALU.mult))
                    dve.sem_inc(max_ready, 1)
                    for n in range(2):
                        dve.wait_ge(t, 8 + n)
                        dve.tensor_copy(w_tab[:, :, :, 1 - n], bank[2 + n][:, 0:NB * J].rearrange("p (j b) -> p b j", b=NB)).then_inc(consts, 1)

    def settle_attention(l, a_s, a_d):
        with phase(f"gat{l}") as (sb, sem):
            m, al, M = sb("m", [P, NT]), sb("al", [P, NT]), sb("M", [P, NT])
            both = sb("both", [P, 2, NT])
            den, bias = sb("den", [P, NT]), sb("bias", [P, P])
            gs = sb("gs", [P, 2, P])
            loaded, v, turned, exp_ready, ready = sem("loaded"), sem("v"), sem("turned"), sem("exp_ready"), sem("ready")
            staged, flipped, copied = sem("staged"), sem("flipped"), sem("copied")
            with nc.Block() as block:
                @block.sync
                def _(sp):
                    clear_spent(sp)
                    sp.dma_start(bias[:, :], spread(a[f"L2_gnn_b{l}"])).then_inc(loaded, 16)

                @block.gpsimd
                def _(pool):
                    steps_of(pool, staged)
                    with pool.Fori(0, NT // 2) as it:
                        for u in range(2):
                            done(pool, flipped, it * 2 + (u - 1))
                            pool.tensor_copy(gs[:, u, :], acc[:, bass.ds(it * (2 * P) + u * P, P)]).then_inc(staged, 1)

                @block.tensor
                def _(pe):
                    steps_of(pe, flipped)
                    turn_aux(pe, 3, turned)
                    with pe.Fori(0, NT // 2) as it:
                        for u in range(2):
                            done(pe, staged, it * 2 + (u + 1))
                            done(pe, copied, it * 2 + (u - 1))
                            pe.transpose(bank[u][:, 0:P], gs[:, u, :], ident[:, :]).then_inc(flipped, 1)

                @block.scalar
                def _(act):
                    steps_of(act, copied)
                    with act.Fori(0, NT // 2) as it:
                        for u in range(2):
                            done(act, flipped, it * 2 + (u + 1))
                            act.copy(flat(w1_sb[:, bass.ds(it * 2 + u, 1), :]), bank[u][:, 0:P]).then_inc(copied, 1)
                    act.wait_ge(ready, 1)
                    act.activation(flat(both[:, :, :]), flat(both[:, :, :]), ACT.Exp).then_inc(exp_ready, 1)

                @block.vector
                def _(dve):
                    link = chain(dve, v)
                    link(dve.tensor_tensor(al[:, :], a_s[:, :], a_d[:, :], ALU.add))
                    dve.wait_ge(turned, 1)
                    link(dve.tensor_tensor(M[:, :], aux_nodes(3)[:, :, 2], rdeg[:, :], ALU.mult))
                    link(dve.tensor_tensor(al[:, :], al[:, :], M[:, :], ALU.add))
                    link(dve.scalar_tensor_tensor(out=al[:, :], in0=al[:, :], scalar=SLOPE, in1=al[:, :], op0=ALU.mult, op1=ALU.max))
                    link(dve.tensor_scalar(M[:, :], has[:, :], -1.0, BIG, ALU.add, ALU.mult))
                    link(dve.tensor_tensor(m[:, :], M[:, :], aux_nodes(3)[:, :, 1], ALU.add))
                    link(dve.tensor_tensor(M[:, :], m[:, :], al[:, :], ALU.max))
                    link(dve.tensor_tensor(both[:, 0, :], m[:, :], M[:, :], ALU.subtract))
                    link(dve.tensor_tensor(both[:, 1, :], al[:, :], M[:, :], ALU.subtract))
                    dve.sem_inc(ready, 1)
                    dve.wait_ge(exp_ready, 1)
                    link(dve.tensor_tensor(den[:, :], aux_nodes(3)[:, :, 0], both[:, 0, :], ALU.mult))
                    link(dve.tensor_tensor(den[:, :], den[:, :], both[:, 1, :], ALU.add))
                    link(dve.reciprocal(den[:, :], den[:, :]))
                    for n in range(2):
                        link(dve.tensor_tensor(both[:, n, :], both[:, n, :], den[:, :], ALU.mult))
                    done(dve, copied, NT)
                    dve.wait_ge(loaded, 16)
                    link(dve.tensor_tensor(y_sb[:, :, :], w1_sb[:, :, :], over_features(both[:, 0, :]), ALU.mult))
                    link(dve.tensor_tensor(w1_sb[:, :, :], h_sb[:, :, :], over_features(both[:, 1, :]), ALU.mult))
                    link(dve.tensor_tensor(y_sb[:, :, :], y_sb[:, :, :], w1_sb[:, :, :], ALU.add))
                    link(dve.tensor_tensor(y_sb[:, :, :], y_sb[:, :, :], over_tiles(bias), ALU.add))
                    if l == 1:
                        link(dve.tensor_scalar(cur[:, :, :], y_sb[:, :, :], 0.0, None, ALU.max))

    prologue()
    node_loop("edge_tables", x_sb,
              [(wide_w[:, 0:P], a["L0_gnn_w1"][0:P, :]), (wide_w[:, P:2 * P], a["L0_gnn_wg"][0:P, :]),
               (wide_w[:, 2 * P:3 * P], a["L0_gnn_w1"][P:2 * P, :]), (wide_w[:, 3 * P:4 * P], a["L0_gnn_wg"][P:2 * P, :]),
               (wide_b[:, 0:P], row(a["L0_gnn_b1"])), (wide_b[:, P:2 * P], row(a["L0_gnn_bg"]))],
              4 * P, bias=True, stores=[(p_tab, 0), (q_tab, 2 * P)])
    gated_pass()
    degrees()
    node_loop("update0", x_sb, [(wide_w[:, 0:P], a["L0_gnn_wu"][0:P, :]), (wide_w[:, P:2 * P], a["L0_gnn_wu"][P:2 * P, :]),
                                (wide_b[:, 0:P], row(a["L0_gnn_bu"]))], P, bias=True, agg=True, dest=y_sb)
    finish_layer("norm0", gate=True, store=tables[0])

    edge_pass("mean1", tables[0])
    node_loop("update1", x_sb, [(wide_w[:, 0:P], a["L1_gnn_W_self"]), (wide_w[:, P:2 * P], a["L1_gnn_W_neigh"]),
                                (wide_b[:, 0:P], row(a["L1_gnn_b_self"]))], P, bias=True, agg=True, dest=y_sb)
    finish_layer("norm1")

    a_s, a_d = sb("a_s", [P, NT]), sb("a_d", [P, NT])
    for l in (1, 2):
        node_loop(f"hidden{l}", x_sb if l == 1 else cur, [(wide_w[:, 0:P], a[f"L2_gnn_W{l}"])], P, dest=h_sb)
        attend(l, tables[l], a_s, a_d)
        edge_pass(f"attention{l}", tables[l], weighted=l)
        settle_attention(l, a_s, a_d)
    finish_layer("norm2", store=tables[3])

    for l in range(2):
        edge_pass(f"mean3{l}", tables[3 + l])
        node_loop(f"update3{l}", x_sb if l == 0 else cur,
                  [(wide_w[:, 0:P], a[f"L3_gnn_W_r{l}"]), (wide_w[:, P:2 * P], a[f"L3_gnn_W_l{l}"]),
                   (wide_b[:, 0:P], row(a[f"L3_gnn_b_l{l}"]))], P, bias=True, turn=(0, 1), agg=True, dest=y_sb)
        finish_layer(f"norm3{l}", affine=(f"L3_gnn_gamma{l}", f"L3_gnn_beta{l}"), residual=l == 1, outer=l == 1,
                     store=tables[4] if l == 0 else None)
    ctx.close()


_INS = ["x", "src", "dst", "edge_attr_128", "edge_attr_64"] \
    + [f"L0_gnn_{n}" for n in ("w1", "b1", "w2", "b2", "wg", "bg", "wu", "bu")] \
    + [f"L1_gnn_{n}" for n in ("W_neigh", "W_self", "b_self")] \
    + [f"L2_gnn_{n}{l}" for l in (1, 2) for n in ("W", "We", "ae", "b")] + [f"L2_gnn_a{l}{s}" for l in (1, 2) for s in "sd"] \
    + [f"L3_gnn_{n}{l}" for l in range(2) for n in ("W_l", "b_l", "W_r", "gamma", "beta")]


def kernel(**inputs):
    import numpy as _np
    import concourse.bacc as _bacc
    from concourse import mybir as _mybir
    from concourse.bass_utils import run_bass_kernel_spmd as _run

    nc = _bacc.Bacc("TRN2", target_bir_lowering=False, num_devices=1)
    arrays, args = {}, {}
    for name in _INS:
        v = _np.ascontiguousarray(inputs[name])
        arrays[f"in_{name}_dram"] = v
        args[name] = nc.dram_tensor(f"in_{name}_dram", v.shape, _mybir.dt.from_np(v.dtype), kind="ExternalInput").ap()
    out = nc.dram_tensor("out_0_dram", args["x"].shape, _mybir.dt.float32, kind="ExternalOutput").ap()
    build_program(nc, args, out)
    r = _run(nc, [arrays], core_ids=[0])
    return r.results[0]["out_0_dram"]
```

```python
from contextlib import ExitStack, contextmanager, nullcontext

import concourse.bass as bass
from concourse import mybir

ALU = mybir.AluOpType
ACT = mybir.ActivationFunctionType
AX = mybir.AxisListType.X
F32 = mybir.dt.float32
BF16 = mybir.dt.bfloat16
F16 = mybir.dt.float16
I32 = mybir.dt.int32

P = 128
J = 4
BE = P * J
W = P // 2
LB = 2
UN = 2 * LB
PAIRS = J // 2
DENSE_BODY, DENSE = 8, 4
TICKS = UN * PAIRS
CREDIT = 16
BIG = 1.0e38
EPS = 1e-5
SLOPE = 0.2


def build_program(nc, a, out):
    N, D = a["x"].shape
    E = a["src"].shape[0]
    DE = a["edge_attr_64"].shape[1]
    assert D == P and DE == P // 2
    NB = -(-E // BE)
    assert NB % UN == 0 and NB <= P
    TAIL = E - (NB - 1) * BE
    TP, TR = TAIL // J, TAIL % J
    assert 0 < TAIL <= BE and TR > 0
    NT = -(-(N + P) // P)
    NODES = NT * P
    FT, FR = N // P, N % P
    ITERS = NB // UN
    STEPS = NB * PAIRS
    CB = 4
    COLS = NT * W // CB
    assert COLS <= 512 and CB * COLS == NT * W and NT % 2 == 0
    assert BE <= 2048 and NT * W <= 2048
    assert J * P <= 512 and J * NB <= 512 and DE == W
    MAX_ROUNDS = NODES // W

    ctx = ExitStack()

    def sb(name, shape, dt=F32):
        return ctx.enter_context(nc.sbuf_tensor(name, shape, dt))

    def sem(name):
        return ctx.enter_context(nc.semaphore(name))

    kept_sem = sem

    spent, clearing = [], []

    def clear_spent(sp):
        for s in clearing:
            sp.sem_clear(s)
        clearing[:] = []

    @contextmanager
    def phase(name):
        with ExitStack() as c:
            held = ExitStack()

            def local_sb(n, shape, dt=F32):
                return c.enter_context(nc.sbuf_tensor(f"{name}_{n}", shape, dt))

            def local_sem(n):
                s = held.enter_context(nc.semaphore(f"{name}_{n}"))
                used.append(s)
                return s
            used = []
            spent_now, spent[:] = list(spent), []
            clearing[:] = [s for _, ss in spent_now for s in ss]

            yield local_sb, local_sem
            assert not clearing, name
            for h, _ in spent_now:
                h.close()
            spent.append((held, used))

    def dram(name, shape, dt=F32):
        return nc.dram_tensor(name, shape, dt).ap()

    bank = [ctx.enter_context(nc.psum_tensor(f"bank{i}", [P, 512], F32)) for i in range(8)]
    ident = sb("ident", [P, P])
    ones = sb("ones", [1, P])
    iota0 = sb("iota0", [P, W])
    part0 = sb("part0", [P, 1])
    node0 = sb("node0", [P, 1])
    iota = sb("iota", [P, W])
    node = sb("node", [P, 1])
    base0 = sb("base0", [1, NB], I32)
    base = sb("base", [1, NB], I32)
    rounds = sb("rounds", [1, 1], I32)
    src_idx = sb("src_idx", [P, NB, J], I32)
    rel = sb("rel", [P, NB, J])
    x_sb = sb("x_sb", [P, NT, P])
    cur = sb("cur", [P, NT, P])
    h_sb = sb("h_sb", [P, NT, P])
    y_sb = sb("y_sb", [P, NT, P])
    w1_sb = sb("w1_sb", [P, NT, P])
    acc = sb("acc", [P, NODES])
    aux_acc = sb("aux_acc", [3, NODES])
    rdeg = sb("rdeg", [P, NT])
    has = sb("has", [P, NT])
    seg_start = sb("seg_start", [P, NT], I32)
    lo_iota = sb("lo_iota", [P, P], BF16)
    code_iota = sb("code_iota", [P, NT * W], F16)
    src_lo = sb("src_lo", [P, NB, J], BF16)
    code = sb("code", [P, NB, J])
    ae_w = sb("ae_w", [P, 2, P])
    ae_tab = sb("ae_tab", [P, NB, J, 2])
    w_tab = sb("w_tab", [P, NB, J, 2])
    pen_f = sb("pen_f", [NB, BE])
    pen_b = sb("pen_b", [NB, BE])
    last = sb("last", [NB, BE])
    pass_f = sb("pass_f", [NB, 1])
    pass_b = sb("pass_b", [NB, 1])
    wide_w = sb("wide_w", [P, 4 * P])
    wide_b = sb("wide_b", [1, 4 * P])

    settled = sem("settled")
    p_tab = dram("p_tab", [NODES, 2 * P])
    q_tab = dram("q_tab", [NODES, 2 * P])
    rel_rows = dram("rel_rows", [2, NB, BE // 2])
    id_rows = dram("id_rows", [NB, 2, BE], BF16)
    first_ad = dram("first_ad", [NB * BE + NODES, 1])
    count_tabs = dram("count_tabs", [NB // DENSE_BODY, DENSE, P, NT * W], F16)
    tables = [dram(f"table{i}", [NODES, P]) for i in range(5)]

    def steps_of(engine, *sems):
        for s in sems:
            engine.sem_inc(s, CREDIT)

    def done(engine, s, n):
        engine.wait_ge(s, n + CREDIT)

    def settle(engine):
        engine.sem_inc(settled, 1)

    def row(v):
        return v.rearrange("(a n) -> a n", a=1)

    def spread(v, n=P):
        return row(v).broadcast_to([n, v.shape[0]])

    def by_tile(t):
        return t.rearrange("(t p) d -> p t d", p=P)

    def flat(t):
        return t.rearrange("p a b -> p (a b)")

    def prologue():
        with phase("pro") as (tmp, sem):
            src_s = tmp("src_s", [NB, BE], I32)
            dst_s = tmp("dst_s", [NB, BE], I32)
            prev_s = tmp("prev_s", [NB, BE], I32)
            next_s = tmp("next_s", [NB, BE], I32)
            ids_i = tmp("ids_i", [NB, 2, BE], I32)
            ids_b = tmp("ids_b", [NB, 2, BE], BF16)
            none = tmp("none", [NB, BE])
            src_sf, dst_sf = tmp("src_sf", [NB, BE]), tmp("dst_sf", [NB, BE])
            rel_s = tmp("rel_s", [NB, BE])
            rel_p = tmp("rel_p", [NB, 2, PAIRS, P])
            same = tmp("same", [NB, BE])
            high = tmp("high", [P, 1])
            mrel = tmp("mrel", [NB, 1])
            mrel1 = tmp("mrel1", [1, 1])
            mrel_i = tmp("mrel_i", [1, 1], I32)
            mrel_q = tmp("mrel_q", [1, 1], I32)
            filled, loaded, consts = sem("filled"), sem("loaded"), sem("consts")
            v, t, stored = sem("v"), sem("t"), sem("stored")
            NL = 2 * 2 + 3 + 2 + 2

            with nc.Block() as block:
                @block.gpsimd
                def _(pool):
                    pool.memset(ident[:, :], 0.0).then_inc(consts, 1)
                    pool.memset(ones[:, :], 1.0).then_inc(consts, 1)
                    pool.wait_ge(consts, 2)
                    pool.affine_select(out=ident[:, :], in_=ident[:, :], compare_op=ALU.not_equal,
                                       fill=1.0, base=0, pattern=[[-1, P]],
                                       channel_multiplier=1).then_inc(consts, 1)
                    pool.iota(iota0[:, :], pattern=[[1, W]], base=0, channel_multiplier=0,
                              allow_small_or_imprecise_dtypes=True).then_inc(consts, 1)
                    pool.iota(part0[:, :], pattern=[[0, 1]], base=0, channel_multiplier=1,
                              allow_small_or_imprecise_dtypes=True).then_inc(consts, 1)
                    pool.memset(none[:, :], -BIG).then_inc(consts, 1)

                @block.sync
                def _(sp):
                    sp.wait_ge(filled, 5)
                    full = (NB - 1) * BE
                    for dst_t, name in ((src_s, "src"), (dst_s, "dst")):
                        sp.dma_start(dst_t[0:NB - 1, :],
                                     a[name][0:full].rearrange("(b e) -> b e", e=BE)).then_inc(loaded, 16)
                        sp.dma_start(dst_t[NB - 1:NB, 0:TAIL],
                                     a[name][full:E].rearrange("(b e) -> b e", b=1)).then_inc(loaded, 16)
                    sp.dma_start(prev_s[0:1, 1:BE], a["dst"][0:BE - 1].rearrange("(b e) -> b e", b=1)).then_inc(loaded, 16)
                    sp.dma_start(prev_s[1:NB - 1, :],
                                 a["dst"][BE - 1:full - 1].rearrange("(b e) -> b e", e=BE)).then_inc(loaded, 16)
                    sp.dma_start(prev_s[NB - 1:NB, 0:TAIL + 1],
                                 a["dst"][full - 1:E].rearrange("(b e) -> b e", b=1)).then_inc(loaded, 16)
                    sp.dma_start(next_s[0:NB - 1, :],
                                 a["dst"][1:full + 1].rearrange("(b e) -> b e", e=BE)).then_inc(loaded, 16)
                    sp.dma_start(next_s[NB - 1:NB, 0:TAIL - 1],
                                 a["dst"][full + 1:E].rearrange("(b e) -> b e", b=1)).then_inc(loaded, 16)
                    sp.dma_start(x_sb[:, 0:FT, :], by_tile(a["x"][0:FT * P, :])).then_inc(loaded, 16)
                    sp.dma_start(x_sb[0:FR, FT, :], a["x"][FT * P:N, :]).then_inc(loaded, 16)
                    sp.wait_ge(v, 9)
                    for c in range(2):
                        sp.dma_start(rel_rows[c, :, :], rel_p[:, c, :, :].rearrange("b k p -> b (k p)")).then_inc(stored, 16)
                    sp.wait_ge(v, 13)
                    sp.dma_start(id_rows, ids_b[:, :, :]).then_inc(stored, 16)
                    sp.wait_ge(consts, 6)
                    sp.dma_start(first_ad[0:NB * BE, :].rearrange("(b e) a -> b (e a)", e=BE), none[:, :]).then_inc(stored, 16)
                    sp.wait_ge(stored, 64)

                @block.vector
                def _(dve):
                    dve.memset(src_s[:, :], 0).then_inc(filled, 1)
                    dve.memset(dst_s[:, :], N).then_inc(filled, 1)
                    dve.memset(prev_s[:, :], N).then_inc(filled, 1)
                    dve.memset(next_s[:, :], N).then_inc(filled, 1)
                    dve.memset(x_sb[:, FT:NT, :], 0.0).then_inc(filled, 1)
                    dve.wait_ge(loaded, 16 * NL)
                    dve.memset(prev_s[0:1, 0:1], -1).then_inc(v, 1)
                    dve.tensor_copy(dst_sf[:, :], dst_s[:, :]).then_inc(v, 1)
                    dve.tensor_copy(src_sf[:, :], src_s[:, :]).then_inc(v, 1)
                    dve.wait_ge(v, 3)
                    dve.tensor_tensor(same[:, :], dst_s[:, :], prev_s[:, :], ALU.is_equal).then_inc(v, 1)
                    dve.wait_ge(v, 4)
                    dve.tensor_scalar(pen_f[:, :], same[:, :], -1.0, BIG, ALU.add, ALU.mult).then_inc(v, 1)
                    dve.tensor_tensor(last[:, :], dst_s[:, :], next_s[:, :], ALU.not_equal).then_inc(v, 1)
                    dve.wait_ge(v, 6)
                    dve.tensor_scalar(pen_b[:, :], last[:, :], -BIG, None, ALU.mult).then_inc(v, 1)
                    dve.tensor_tensor(rel_s[:, :], dst_sf[:, :], dst_sf[:, 0:1].broadcast_to([NB, BE]), ALU.subtract).then_inc(v, 1)
                    dve.wait_ge(v, 8)
                    dve.tensor_copy(rel_p[:, :, :, :], rel_s[:, :].rearrange("b (p k c) -> b c k p", k=PAIRS, c=2)).then_inc(v, 1)
                    dve.tensor_reduce(mrel[:, :], rel_s[:, :], AX, ALU.max).then_inc(v, 1)
                    dve.tensor_scalar(ids_i[:, 0, :], src_s[:, :], P - 1, None, ALU.bitwise_and).then_inc(v, 1)
                    dve.tensor_scalar(ids_i[:, 1, :], src_s[:, :], 7, None, ALU.logical_shift_right).then_inc(v, 1)
                    dve.wait_ge(v, 12)
                    dve.tensor_copy(ids_b[:, :, :], ids_i[:, :, :]).then_inc(v, 1)
                    dve.tensor_reduce(pass_f[:, :], pen_f[:, :], AX, ALU.min).then_inc(v, 1)
                    dve.tensor_reduce(pass_b[:, :], pen_b[:, :], AX, ALU.min).then_inc(v, 1)
                    dve.wait_ge(t, 1)
                    dve.tensor_copy(src_idx[:, :, :], bank[0][:, 0:NB * J].rearrange("p (j b) -> p b j", b=NB)).then_inc(v, 1)
                    dve.wait_ge(t, 2)
                    dve.tensor_copy(rel[:, :, :], bank[1][:, 0:NB * J].rearrange("p (j b) -> p b j", b=NB)).then_inc(v, 1)
                    dve.tensor_copy(base0[:, :], bank[2][0:1, 0:NB]).then_inc(v, 1)
                    dve.wait_ge(t, 3)
                    dve.tensor_reduce(mrel1[:, :], bank[3][0:1, 0:NB], AX, ALU.max).then_inc(v, 1)
                    dve.wait_ge(v, 19)
                    dve.tensor_copy(mrel_i[:, :], mrel1[:, :]).then_inc(v, 1)
                    dve.wait_ge(v, 20)
                    dve.tensor_scalar(mrel_q[:, :], mrel_i[:, :], W.bit_length() - 1, None, ALU.logical_shift_right).then_inc(v, 1)
                    dve.wait_ge(v, 21)
                    dve.tensor_scalar(rounds[:, :], mrel_q[:, :], 1, None, ALU.add).then_inc(v, 1)
                    dve.wait_ge(consts, 5)
                    dve.tensor_scalar(high[:, :], part0[:, :], float(W), -float(W), ALU.is_ge, ALU.mult).then_inc(v, 1)
                    dve.wait_ge(v, 23)
                    dve.tensor_tensor(node0[:, :], part0[:, :], high[:, :], ALU.add).then_inc(v, 1)

                @block.tensor
                def _(pe):
                    pe.wait_ge(consts, 5)
                    for n, (frm, steps) in enumerate(((src_sf, 3), (rel_s, 8))):
                        pe.wait_ge(v, steps)
                        if n == 1:
                            pe.transpose(bank[2][0:1, 0:NB], dst_sf[:, 0:1], ident[0:NB, 0:NB])
                        for j in range(J):
                            mm = pe.transpose(bank[n][:, j * NB:(j + 1) * NB], frm[:, j:BE:J], ident[0:NB, 0:NB])
                        mm.then_inc(t, 1)
                    pe.wait_ge(v, 10)
                    pe.transpose(bank[3][0:1, 0:NB], mrel[:, :], ident[0:NB, 0:NB]).then_inc(t, 1)

    def start_windows(dve, windows):
        dve.tensor_copy(iota[:, :], iota0[:, :]).then_inc(windows, 1)
        dve.tensor_copy(node[:, :], node0[:, :]).then_inc(windows, 1)
        dve.tensor_copy(base[:, :], base0[:, :]).then_inc(windows, 1)

    def next_windows(dve, windows):
        dve.tensor_scalar(iota[:, :], iota[:, :], float(W), None, ALU.add).then_inc(windows, 1)
        dve.tensor_scalar(node[:, :], node[:, :], float(W), None, ALU.add).then_inc(windows, 1)
        dve.tensor_scalar(base[:, :], base[:, :], W, N, ALU.add, ALU.min).then_inc(windows, 1)

    def lagged(i, lag, where, ticks=TICKS):
        j = i - lag
        if (where == "first" and j < 0) or (where == "tail" and j >= 0):
            return None
        return j % ticks, (-1 if j < 0 else 0)


    def node_loop(name, x_from, loads, width, bias=False, turn=(), agg=False, dest=None, stores=None):
        with phase(name) as (sb, sem):
            xs, gs = sb("xs", [P, 2, 2, P]), sb("gs", [P, 2, 2, P]) if agg else None
            xT = sb("xT", [P, 2, 2, P])
            zs = sb("zs", [P, 2, 2, width]) if (agg or stores) else None
            weights, turned_w = sem("weights"), sem("turned_w")
            staged, sums_staged, turned, xT_ready = sem("staged"), sem("sums_staged"), sem("turned"), sem("xT_ready")
            made, z_ready, y_ready = sem("made"), sem("z_ready"), sem("y_ready")
            stored = [sem(f"stored{u}") for u in range(2)] if stores else []
            NP = NT // 2
            assert NT % 2 == 0 and NP % 2 == 1

            def each_pair(engine, early, late=None):
                for u in range(2):
                    early(u, u)
                with engine.Fori(0, (NP - 3) // 2) as it:
                    for u in range(2):
                        if late:
                            late(it * 2 + u, u)
                        early(it * 2 + (u + 2), u)
                if late:
                    late(NP - 3, 0)
                early(NP - 1, 0)
                if late:
                    late(NP - 2, 1)
                    late(NP - 1, 0)

            def tiles(v, p):
                return v[:, bass.ds(p * 2, 2), :]

            with nc.Block() as block:
                @block.sync
                def _(sp):
                    clear_spent(sp)
                    for to, frm in loads:
                        sp.dma_start(to, frm).then_inc(weights, 16)

                    def store(p, u):
                        done(sp, z_ready, p + 1)
                        settle(sp)
                        for c in range(2):
                            for table, col in stores:
                                w = table.shape[1]
                                sp.dma_start(table[bass.ds(p * (2 * P) + c * P, P), :],
                                             zs[:, u, c, col:col + w]).then_inc(stored[u], 16)
                    if stores:
                        each_pair(sp, store)
                        for u in range(2):
                            sp.wait_ge(stored[u], 32 * len(stores) * (NP // 2 + 1 - u))

                if agg:
                    @block.gpsimd
                    def _(pool):
                        steps_of(pool, sums_staged)

                        def stage_sums(p, u):
                            done(pool, made, p - 1)
                            pool.tensor_copy(flat(gs[:, u, :, :]), acc[:, bass.ds(p * (2 * P), 2 * P)]).then_inc(sums_staged, 1)
                        each_pair(pool, stage_sums)

                @block.tensor
                def _(pe):
                    steps_of(pe, turned, made)
                    pe.wait_ge(weights, 16 * len(loads))
                    for n, k in enumerate(turn):
                        pe.transpose(bank[6 + n][:, 0:P], wide_w[:, k * P:(k + 1) * P], ident[:, :]).then_inc(turned_w, 1)
                    if turn:
                        pe.wait_ge(turned_w, 2 * len(turn))

                    def transpose(p, u):
                        done(pe, staged, p + 1)
                        done(pe, xT_ready, p - 1)
                        for c in range(2):
                            mm = pe.transpose(bank[u][:, c * P:(c + 1) * P], xs[:, u, c, :], ident[:, :])
                        mm.then_inc(turned, 1)

                    def product(p, u):
                        done(pe, xT_ready, p + 1)
                        done(pe, z_ready, p - 1)
                        for c in range(2):
                            z = bank[2 + 2 * u + c] if width > 2 * P else bank[2 + 2 * u][:, c * P:(c + 1) * P]
                            mm = pe.matmul(z[:, 0:width], xT[:, u, c, :], wide_w[:, 0:width], start=True, stop=not bias)
                            if bias:
                                nb = min(width, 2 * P)
                                mm = pe.matmul(z[:, 0:nb], ones[0:1, :], wide_b[0:1, 0:nb], start=False, stop=True)
                        if agg:
                            done(pe, sums_staged, p + 1)
                            done(pe, y_ready, p - 1)
                            for c in range(2):
                                mm = pe.matmul(bank[3 + 2 * u][:, c * P:(c + 1) * P], gs[:, u, c, :], wide_w[:, P:2 * P],
                                               start=True, stop=True)
                        mm.then_inc(made, 1)
                    each_pair(pe, transpose, product)

                @block.scalar
                def _(act):
                    steps_of(act, xT_ready, z_ready)

                    def copy_xT(p, u):
                        done(act, turned, p + 1)
                        done(act, made, p - 1)
                        act.copy(flat(xT[:, u, :, :]), bank[u][:, 0:2 * P]).then_inc(xT_ready, 1)

                    def copy_z(p, u):
                        done(act, made, p + 1)
                        if stores:
                            if not (isinstance(p, int) and p < 2):
                                act.wait_ge(stored[u], (p - u) * (16 * len(stores)))
                            for c in range(2):
                                ins = act.copy(zs[:, u, c, :], bank[2 + 2 * u + c][:, 0:width])
                        else:
                            if agg:
                                done(act, y_ready, p - 1)
                            to = flat(zs[:, u, :, :]) if agg else flat(tiles(dest, p))
                            ins = act.copy(to, bank[2 + 2 * u][:, 0:2 * P])
                        ins.then_inc(z_ready, 1)
                    if stores:
                        for u in range(2):
                            copy_xT(u, u)
                        for u in range(2):
                            copy_z(u, u)
                            copy_xT(u + 2, u)
                        with act.Fori(1, (NP - 3) // 2) as it:
                            for u in range(2):
                                copy_z(it * 2 + u, u)
                                copy_xT(it * 2 + (u + 2), u)
                        copy_z(NP - 3, 0)
                        copy_xT(NP - 1, 0)
                        copy_z(NP - 2, 1)
                        copy_z(NP - 1, 0)
                    else:
                        each_pair(act, copy_xT, copy_z)

                @block.vector
                def _(dve):
                    steps_of(dve, y_ready, staged)

                    def stage(p, u):
                        done(dve, turned, p - 1)
                        dve.tensor_copy(flat(xs[:, u, :, :]), flat(tiles(x_from, p))).then_inc(staged, 1)

                    def mean(p, u):
                        done(dve, z_ready, p + 1)
                        for c in range(2):
                            ins = dve.scalar_tensor_tensor(out=flat(dest[:, bass.ds(p * 2 + c, 1), :]),
                                                           in0=bank[3 + 2 * u][:, c * P:(c + 1) * P],
                                                           scalar=rdeg[:, bass.ds(p * 2 + c, 1)], in1=zs[:, u, c, :],
                                                           op0=ALU.mult, op1=ALU.add)
                        ins.then_inc(y_ready, 1)
                    for n, k in enumerate(turn):
                        dve.wait_ge(turned_w, len(turn))
                        dve.tensor_copy(wide_w[:, k * P:(k + 1) * P], bank[6 + n][:, 0:P]).then_inc(turned_w, 1)
                    each_pair(dve, stage, mean if agg else None)

    def chain(engine, s):
        count = [0]

        def link(ins):
            ins.then_inc(s, 1)
            count[0] += 1
            engine.wait_ge(s, count[0])
        return link

    halves = (slice(0, NT // 2), slice(NT // 2, NT))

    def norm_steps(sb, sem):
        stats, mean, dif = sb("stats", [P, NT, 6]), sb("mean", [P, NT]), sb("dif", [P, NT])
        var, rstd = sb("var", [P, NT]), sb("rstd", [P, NT])
        counted, var_ready, rstd_ready = sem("counted"), sem("var_ready"), sem("rstd_ready")
        norms = [0]

        def wide(v):
            return v[:, :].rearrange("p (t d) -> p t d", d=1).broadcast_to([P, NT, P])

        def steps(dve, link, x, y, fin=None):
            with dve.Fori(0, NT // 2) as it:
                for u in range(2):
                    dve.bn_stats(flat(stats[:, bass.ds(it * 2 + u, 1), :]), flat(x[:, bass.ds(it * 2 + u, 1), :])).then_inc(counted, 1)
            norms[0] += 1
            dve.wait_ge(counted, norms[0] * NT)
            link(dve.tensor_tensor(mean[:, :], stats[:, :, 1], stats[:, :, 4], ALU.add))
            link(dve.tensor_tensor(dif[:, :], stats[:, :, 1], stats[:, :, 4], ALU.subtract))
            link(dve.tensor_tensor(var[:, :], stats[:, :, 2], stats[:, :, 5], ALU.add))
            link(dve.tensor_scalar(mean[:, :], mean[:, :], 0.5, None, ALU.mult))
            link(dve.tensor_tensor(dif[:, :], dif[:, :], dif[:, :], ALU.mult))
            link(dve.tensor_scalar(dif[:, :], dif[:, :], 0.25, EPS, ALU.mult, ALU.add))
            link(dve.scalar_tensor_tensor(out=var[:, :], in0=var[:, :], scalar=1.0 / P, in1=dif[:, :],
                                          op0=ALU.mult, op1=ALU.add))
            dve.sem_inc(var_ready, 1)
            dve.wait_ge(rstd_ready, norms[0])
            link(dve.reciprocal(rstd[:, :], dif[:, :]))
            link(dve.tensor_tensor(dif[:, :], rstd[:, :], rstd[:, :], ALU.mult))
            link(dve.tensor_tensor(dif[:, :], dif[:, :], var[:, :], ALU.mult))
            link(dve.tensor_scalar(dif[:, :], dif[:, :], -0.5, 1.5, ALU.mult, ALU.add))
            link(dve.tensor_tensor(rstd[:, :], rstd[:, :], dif[:, :], ALU.mult))
            link(dve.tensor_tensor(x[:, :, :], x[:, :, :], wide(mean), ALU.subtract))
            for h in halves:
                link(dve.tensor_tensor(y[:, h, :], x[:, h, :], wide(rstd)[:, h, :], ALU.mult))
                if fin is not None:
                    dve.sem_inc(fin, 1)

        def root(act, n):
            act.wait_ge(var_ready, n + 1)
            act.activation(dif[:, :], var[:, :], ACT.Sqrt).then_inc(rstd_ready, 1)

        return steps, root

    def over_chunks(v):
        return v[:, :].rearrange("p (a n) -> p a n", a=1).broadcast_to([P, J, W])

    def over_nodes(b):
        return rel[:, bass.ds(b, 1), :].rearrange("p b (j n) -> p (b j) n", n=1).broadcast_to([P, J, W])

    def add_window(dve, seg, seg_aux, b, n, added, k):
        settle(dve)
        start = dve.value_load(base[0:1, bass.ds(b, 1)], min_val=0, max_val=N)
        to = acc[:, bass.ds(start, W)]
        done(dve, added, n)
        ins = dve.tensor_tensor(to, to, seg, ALU.add)
        if k:
            to = aux_acc[0:k, bass.ds(start, W)]
            ins = dve.tensor_tensor(to, to, seg_aux[0:k, :], ALU.add)
        ins.then_inc(added, 1)

    def load_indices(sp, idx, b, u, idx_in):
        sp.dma_start(idx[:, u * LB:(u + 1) * LB, :], src_idx[:, bass.ds(b, LB), :]).then_inc(idx_in[u], 16)

    def load_edges(sp, name, buf, b, u, s, tail):
        if not tail:
            sp.dma_start(buf[:, u * LB:(u + 1) * LB, :, :], a[name][bass.ds(b * BE, LB * BE), :]
                         .rearrange("(b p j) d -> p b j d", p=P, j=J)).then_inc(s[u], 16)
        else:
            e0, at = (NB - 1) * BE, (u + 1) * LB - 1
            sp.dma_start(buf[:, u * LB:at, :, :], a[name][e0 - (LB - 1) * BE:e0, :]
                         .rearrange("(b p j) d -> p b j d", p=P, j=J)).then_inc(s[u], 16)
            sp.dma_start(buf[0:TP, at, :, :], a[name][e0:e0 + TP * J, :]
                         .rearrange("(p j) d -> p j d", j=J)).then_inc(s[u], 16)
            sp.dma_start(buf[TP:TP + 1, at, 0:TR, :], a[name][e0 + TP * J:E, :]
                         .rearrange("(p j) d -> p j d", p=1)).then_inc(s[u], 16)

    def edges_in(engine, s, rr, it, u, where):
        if u < UN // LB - 1:
            engine.wait_ge(s[u], (rr * ITERS + it + 1) * 16)
        else:
            engine.wait_ge(s[u], (rr * (ITERS + 2) + it + (3 if where == "last" else 1)) * 16)

    def gated_pass():
        with phase("gated") as (sb, sem):
            we, w2 = sb("we", [P, 2 * P]), sb("w2", [P, P])
            b2, b2_res = sb("b2", [P, P]), sb("b2_res", [P, P])
            b2_part = sb("b2_part", [P, 3, P], BF16)
            b2_rows = sb("b2_rows", [P, 2, P], BF16)
            ones_b = sb("ones_b", [P, P], BF16)
            idx = sb("idx", [P, UN, J], I32)
            ea64 = sb("ea64", [P, UN, J, DE])
            relr = sb("relr", [P, UN, BE // 2])
            comb, wide_q = sb("comb", [P, UN, PAIRS, 2, P]), sb("wide_q", [P, UN, 2, 2 * P])
            hot, hot_b = sb("hot", [P, UN, J, W]), sb("hot_b", [P, UN, J, W], BF16)
            rows = sb("rows", [P, TICKS, 2, 2 * P])
            pre, sig = sb("pre", [P, 2, 2, 2 * P]), sb("sig", [P, 4, 2, 2 * P])
            silu, siluT, msg = sb("silu", [P, 2, 2, P]), sb("siluT", [P, 2, 2, P]), sb("msg", [P, 2, 2, P])

            loaded, ready = sem("loaded"), sem("ready")
            idx_in = [sem(f"idx_in{u}") for u in range(UN // LB)]
            ea64_in = [sem(f"ea64_in{u}") for u in range(UN // LB)]
            relr_in = [sem(f"relr_in{u}") for u in range(UN // LB)]
            q_in = [sem(f"q_in{u}") for u in range(UN)]
            rows_in = [kept_sem(f"gated_rows_in{i}") for i in range(TICKS)]
            windows = sem("windows")
            ea_turned, made, s_turned, m_made, summed = sem("ea_turned"), sem("pre_made"), sem("s_turned"), sem("m_made"), sem("summed")
            eaT_ready, sig_ready, sT_ready = sem("eaT_ready"), sem("sig_ready"), sem("sT_ready")
            hot_b_ready, split, we_placed = sem("hot_b_ready"), sem("split"), sem("we_placed")
            pre_ready, silu_ready, msg_ready = sem("pre_ready"), sem("silu_ready"), sem("msg_ready")
            hot_ready, hotT_ready, added = sem("hot_ready"), sem("hotT_ready"), sem("added")
            PRE = [bank[0], bank[1]]
            SEG = [bank[2], bank[3]]
            EAT, ST, M = bank[4], bank[5], bank[6]
            low, high = slice(0, W), slice(W, P)
            BACK = (UN - 1) * PAIRS

            def q_of(rr, it, i):
                return rr * STEPS + it * TICKS + i

            with nc.Block() as block:
                @block.sync
                def _(sp):
                    clear_spent(sp)
                    for half in (low, high):
                        sp.dma_start(we[half, 0:P], a["L0_gnn_w1"][2 * P:2 * P + DE, :]).then_inc(loaded, 16)
                        sp.dma_start(we[half, P:2 * P], a["L0_gnn_wg"][2 * P:2 * P + DE, :]).then_inc(loaded, 16)
                    sp.dma_start(w2[:, :], a["L0_gnn_w2"]).then_inc(loaded, 16)
                    sp.dma_start(b2[:, :], spread(a["L0_gnn_b2"])).then_inc(loaded, 16)
                    R = sp.value_load(rounds[0:1, 0:1], min_val=1, max_val=MAX_ROUNDS)

                    def load_batches(rr, it, u, tail):
                        b = it * UN + u * LB
                        n = rr * NB + b
                        q = (n + LB - UN) * PAIRS
                        done(sp, pre_ready, q)
                        settle(sp)
                        load_indices(sp, idx, b, u, idx_in)
                        done(sp, ea_turned, q)
                        settle(sp)
                        load_edges(sp, "edge_attr_64", ea64, b, u, ea64_in, tail)
                        done(sp, hotT_ready, n + LB - UN)
                        settle(sp)
                        for c, half in ((0, high), (1, low)):
                            sp.dma_start(relr[half, u * LB:(u + 1) * LB, :].rearrange("p b e -> p (b e)"),
                                         rel_rows[c:c + 1, bass.ds(b, LB), :].rearrange("c b e -> c (b e)")
                                         .broadcast_to([W, LB * BE // 2])).then_inc(relr_in[u], 16)
                        for g in range(LB):
                            done(sp, made, q + g * PAIRS - (LB - 1) * PAIRS)
                            settle(sp)
                            start = sp.value_load(base[0:1, bass.ds(b + g, 1)], min_val=0, max_val=N)
                            for c, half in ((0, high), (1, low)):
                                sp.dma_start(wide_q[half, u * LB + g, c, :], q_tab[bass.ds(start, W), :]).then_inc(q_in[u * LB + g], 16)

                    with sp.Fori(0, R) as rr:
                        sp.wait_ge(windows, rr * 3 + 3)
                        settle(sp)
                        with sp.Fori(0, ITERS - 1) as it:
                            for u in range(UN // LB):
                                load_batches(rr, it, u, False)
                        for u in range(UN // LB):
                            load_batches(rr, ITERS - 1, u, u == UN // LB - 1)

                @block.gpsimd
                def _(pool):
                    R = pool.value_load(rounds[0:1, 0:1], min_val=1, max_val=MAX_ROUNDS)
                    with pool.Fori(0, R) as rr:
                        with pool.Fori(0, ITERS) as it:
                            for i in range(TICKS):
                                u, k = i // PAIRS, i % PAIRS
                                if u % LB == 0 and k == 0:
                                    pool.wait_ge(idx_in[u // LB], (rr * ITERS + it + 1) * 16)
                                done(pool, pre_ready, q_of(rr, it, i) - TICKS + 1)
                                settle(pool)
                                for c in range(2):
                                    j = 2 * k + c
                                    pool.indirect_dma_start(out=rows[:, i, c, :], out_offset=None, in_=p_tab,
                                                            in_offset=bass.IndirectOffsetOnAxis(ap=idx[:, u, j:j + 1], axis=0)
                                                            ).then_inc(rows_in[i], 16)

                @block.tensor
                def _(pe):
                    steps_of(pe, ea_turned, made, s_turned, m_made, summed)
                    pe.wait_ge(loaded, 16 * 6)
                    pe.wait_ge(ready, 3)
                    pe.wait_ge(split, 5 + 6)
                    pe.wait_ge(we_placed, 2)
                    R = pe.value_load(rounds[0:1, 0:1], min_val=1, max_val=MAX_ROUNDS)

                    def tick(rr, it, i, where):
                        if (w := lagged(i, 0, where)):
                            m, back = w
                            q, u, k = q_of(rr, it + back, m), m // PAIRS, m % PAIRS
                            if k == 0:
                                edges_in(pe, ea64_in, rr, it, u // LB, where)
                            done(pe, eaT_ready, q)
                            pe.transpose(EAT[:, 0:P], ea64[:, u, 2 * k:2 * k + 2, :].rearrange("p j d -> p (j d)"),
                                         ident[:, :]).then_inc(ea_turned, 1)
                        if (w := lagged(i, 2, where)):
                            m, back = w
                            q, u, k = q_of(rr, it + back, m), m // PAIRS, m % PAIRS
                            done(pe, eaT_ready, q + 1)
                            done(pe, hotT_ready, rr * NB + (it + back) * UN + u + 1)
                            pe.wait_ge(q_in[u], (rr * ITERS + it + back + 1) * 32)
                            done(pe, pre_ready, q - 1)
                            for c in range(2):
                                mm = pe.matmul(PRE[m % 2][:, c * 2 * P:(c + 1) * 2 * P], comb[:, u, k, c, :],
                                               wide_q[:, u, c, :], start=True, stop=True)
                            mm.then_inc(made, 1)
                        if (w := lagged(i, 4, where)):
                            m, back = w
                            q = q_of(rr, it + back, m)
                            done(pe, silu_ready, q + 1)
                            done(pe, sT_ready, q)
                            for c in range(2):
                                mm = pe.transpose(ST[:, c * P:(c + 1) * P], silu[:, m % 2, c, :], ident[:, :])
                            mm.then_inc(s_turned, 1)
                        if (w := lagged(i, 5, where)):
                            m, back = w
                            q = q_of(rr, it + back, m)
                            done(pe, sT_ready, q + 1)
                            done(pe, msg_ready, q)
                            pe.matmul(M[:, 0:2 * P], ones_b[:, :], flat(b2_rows[:, :, :]), start=True, stop=False,
                                      skip_group_check=True)
                            for c in range(2):
                                mm = pe.matmul(M[:, c * P:(c + 1) * P], siluT[:, m % 2, c, :], w2[:, :], start=False,
                                               stop=True, skip_group_check=True)
                            mm.then_inc(m_made, 1)
                        if (w := lagged(i, 6, where)):
                            m, back = w
                            q, u, k = q_of(rr, it + back, m), m // PAIRS, m % PAIRS
                            b = rr * NB + (it + back) * UN + u
                            done(pe, msg_ready, q + 1)
                            if k == 0:
                                done(pe, hot_ready, b + 1)
                                done(pe, hot_b_ready, b + 1)
                                done(pe, added, b - 1)
                            for c in range(2):
                                j = 2 * k + c
                                pe.matmul(SEG[u % 2][:, 0:W], msg[:, m % 2, c, :], hot[:, u, j, :],
                                          start=(j == 0), stop=(j == J - 1), skip_group_check=True)
                                mm = pe.matmul(SEG[u % 2][0:1, W:2 * W], ones_b[:, 0:1], hot_b[:, u, j, :],
                                               start=False, stop=(j == J - 1), skip_group_check=True)
                            mm.then_inc(summed, 1)

                    with pe.Fori(0, R) as rr:
                        for i in range(TICKS):
                            tick(rr, 0, i, "first")
                        with pe.Fori(1, ITERS - 1) as it:
                            for i in range(TICKS):
                                tick(rr, it, i, "body")
                        for i in range(TICKS):
                            tick(rr, ITERS - 1, i, "last")
                        for i in range(6):
                            tick(rr, ITERS, i, "tail")

                @block.scalar
                def _(act):
                    steps_of(act, eaT_ready, sig_ready, sT_ready, hot_b_ready)
                    R = act.value_load(rounds[0:1, 0:1], min_val=1, max_val=MAX_ROUNDS)

                    def tick(rr, it, i, where):
                        if (w := lagged(i, 0, where)):
                            m, back = w
                            q, u, k = q_of(rr, it + back, m), m // PAIRS, m % PAIRS
                            done(act, ea_turned, q + 1)
                            done(act, made, q - TICKS + 1)
                            act.copy(comb[low, u, k, 0, :], EAT[low, 0:P])
                            act.copy(comb[high, u, k, 1, :], EAT[high, 0:P]).then_inc(eaT_ready, 1)
                        if (w := lagged(i, 2, where)):
                            m, back = w
                            q = q_of(rr, it + back, m)
                            done(act, pre_ready, q + 1)
                            done(act, msg_ready, q - 3)
                            act.activation(flat(sig[:, m % 4, :, :]), flat(pre[:, m % 2, :, :]), ACT.Sigmoid).then_inc(sig_ready, 1)
                        if (w := lagged(i, 4, where)):
                            m, back = w
                            q = q_of(rr, it + back, m)
                            done(act, s_turned, q + 1)
                            done(act, m_made, q - 1)
                            act.copy(flat(siluT[:, m % 2, :, :]), ST[:, 0:2 * P]).then_inc(sT_ready, 1)
                        if (w := lagged(i, 5, where)) and w[0] % PAIRS == 0:
                            m, back = w
                            q, u = q_of(rr, it + back, m), m // PAIRS
                            done(act, hot_ready, rr * NB + (it + back) * UN + u + 1)
                            done(act, summed, q - BACK)
                            act.copy(hot_b[:, u, :, :], hot[:, u, :, :]).then_inc(hot_b_ready, 1)

                    with act.Fori(0, R) as rr:
                        for i in range(TICKS):
                            tick(rr, 0, i, "first")
                        with act.Fori(1, ITERS) as it:
                            for i in range(TICKS):
                                tick(rr, it, i, "body")
                        for i in range(5):
                            tick(rr, ITERS, i, "tail")

                @block.vector
                def _(dve):
                    steps_of(dve, pre_ready, silu_ready, msg_ready, hot_ready, hotT_ready, added)
                    start_windows(dve, windows)
                    dve.memset(acc[:, :], 0.0).then_inc(ready, 1)
                    dve.memset(aux_acc[:, :], 0.0).then_inc(ready, 1)
                    dve.memset(ones_b[:, :], 1.0).then_inc(ready, 1)
                    dve.wait_ge(loaded, 16 * 6)
                    for c, half in ((0, low), (1, high)):
                        dve.tensor_copy(wide_q[half, :, c, :], we[half, :].rearrange("p (a d) -> p a d", a=1)
                                        .broadcast_to([W, UN, 2 * P])).then_inc(we_placed, 1)
                    link = chain(dve, split)
                    link(dve.memset(b2_rows[:, :, :], 0.0))
                    link(dve.tensor_copy(b2_part[:, 0, :], b2[:, :]))
                    link(dve.tensor_tensor(b2_res[:, :], b2[:, :], b2_part[:, 0, :], ALU.subtract))
                    link(dve.tensor_copy(b2_part[:, 1, :], b2_res[:, :]))
                    link(dve.tensor_tensor(b2_part[:, 2, :], b2_res[:, :], b2_part[:, 1, :], ALU.subtract))
                    for n in range(3):
                        for c in range(2):
                            dve.tensor_copy(b2_rows[32 * n:32 * n + 1, c, :], b2_part[32 * n:32 * n + 1, n, :]).then_inc(split, 1)
                    dve.wait_ge(windows, 3)
                    R = dve.value_load(rounds[0:1, 0:1], min_val=1, max_val=MAX_ROUNDS)

                    def tick(rr, it, i, where):
                        if (w := lagged(i, 0, where)) and w[0] % PAIRS == 0:
                            m, back = w
                            q, u = q_of(rr, it + back, m), m // PAIRS
                            dve.wait_ge(relr_in[u // LB], (rr * ITERS + it + 1) * 32)
                            done(dve, made, q - BACK)
                            for c, half in ((0, high), (1, low)):
                                ins = dve.tensor_scalar(comb[half, u, :, c, :], relr[half, u, :].rearrange("n (k p) -> n k p", p=P),
                                                        node[half, 0:1], None, ALU.is_equal)
                            ins.then_inc(hotT_ready, 1)
                        if (w := lagged(i, 2, where)):
                            m, back = w
                            q = q_of(rr, it + back, m)
                            done(dve, made, q + 1)
                            dve.wait_ge(rows_in[m], (rr * ITERS + it + back + 1) * 32)
                            done(dve, sig_ready, q - 1)
                            done(dve, silu_ready, q - 1)
                            dve.tensor_tensor(flat(pre[:, m % 2, :, :]), PRE[m % 2][:, :], flat(rows[:, m, :, :]),
                                              ALU.add).then_inc(pre_ready, 1)
                        if (w := lagged(i, 3, where)):
                            m, back = w
                            q = q_of(rr, it + back, m)
                            done(dve, sig_ready, q + 1)
                            done(dve, s_turned, q - 1)
                            dve.tensor_tensor(silu[:, m % 2, :, :], pre[:, m % 2, :, 0:P], sig[:, m % 4, :, 0:P],
                                              ALU.mult).then_inc(silu_ready, 1)
                        if (w := lagged(i, 4, where)) and w[0] % PAIRS == 0:
                            m, back = w
                            q, u = q_of(rr, it + back, m), m // PAIRS
                            b = (it + back) * UN + u
                            done(dve, summed, q - BACK)
                            dve.tensor_tensor(hot[:, u, :, :], over_chunks(iota), over_nodes(b), ALU.is_equal).then_inc(hot_ready, 1)
                        if (w := lagged(i, 5, where)):
                            m, back = w
                            q = q_of(rr, it + back, m)
                            done(dve, m_made, q + 1)
                            done(dve, summed, q - 1)
                            dve.tensor_tensor(msg[:, m % 2, :, :], M[:, 0:2 * P].rearrange("p (c d) -> p c d", c=2),
                                              sig[:, m % 4, :, P:2 * P], ALU.mult).then_inc(msg_ready, 1)
                        if (w := lagged(i, 7, where)) and w[0] % PAIRS == PAIRS - 1:
                            m, back = w
                            q, u = q_of(rr, it + back, m), m // PAIRS
                            b = (it + back) * UN + u
                            done(dve, summed, q + 1)
                            add_window(dve, SEG[u % 2][:, 0:W], SEG[u % 2][:, W:2 * W], b, rr * NB + b, added, 1)

                    with dve.Fori(0, R) as rr:
                        dve.wait_ge(windows, rr * 3 + 3)
                        for i in range(TICKS):
                            tick(rr, 0, i, "first")
                        with dve.Fori(1, ITERS) as it:
                            for i in range(TICKS):
                                tick(rr, it, i, "body")
                        for i in range(7):
                            tick(rr, ITERS, i, "tail")
                        done(dve, hot_ready, (rr + 1) * NB)
                        next_windows(dve, windows)

    def edge_pass(name, table, body, dense=0, x_from=None, when=None, build=(), prepare_at=(), count_at=(),
                  weighted=0, edge_terms=False):
        with phase(name) as (sb, sem):
            ITERS = NB // body
            GB = body - dense
            S = GB + (dense > 0)
            GT = GB * PAIRS
            HR = 4
            NG = len(build)
            assert NB % body == 0 and GB % LB == 0 and GB % HR == 0 and dense * W <= 512
            assert all(p < c < GB for p, c in zip(prepare_at, count_at)) and len(prepare_at) == len(count_at) == NG
            assert all(p >= c for p, c in zip(prepare_at[1:], count_at))
            assert not (build or dense) or body == DENSE_BODY
            idx, hot = sb("idx", [P, GB, J], I32), sb("hot", [P, HR, J, W])
            rows = sb("rows", [P, GT, 2, P])
            if build:
                lo = sb("lo", [P, J, P], BF16)
                wide = sb("wide", [P, J, NT * W], BF16)
                code_s = sb("code_s", [P, J])
                built = sb("built", [P, NG, NT * W], F16)
                table_stored = [sem(f"table_stored{g}") for g in range(NG)]
            if dense:
                assert dense == DENSE
                packed = sb("packed", [P, 2, dense, NT // 2 * W], F16)
                counts = sb("counts", [P, NT, dense, W])
                packed_in = [sem(f"packed_in{h}") for h in range(2)]
            idx_in = [sem(f"idx_in{u}") for u in range(GB // LB)]
            rows_in = [kept_sem(f"{name}_rows_in{i}") for i in range(GT)]
            windows, ready, staged = sem("windows"), sem("ready"), sem("staged")
            hot_ready, added, summed, used = sem("hot_ready"), sem("added"), sem("summed"), sem("rows_used")
            prepared, counted, copied, half_used = sem("prepared"), sem("counted"), sem("copied"), sem("half_used")
            SEG, SEG_D, CNT = [bank[0], bank[1]], bank[2], bank[3:3 + CB]
            if weighted:
                SR = GT // 2
                aux, scaled = sb("aux", [P, HR, J, 3]), sb("scaled", [P, SR, 2, P])
                aux_ready, scaled_used = sem("aux_ready"), sem("scaled_used")
            if edge_terms:
                ea128, junk, ae = sb("ea128", [P, UN, J, P]), sb("junk", [P, 2, 2 * J, P]), sb("ae", [P, 2, J, 2])
                ea128_in = [sem(f"ea128_in{u}") for u in range(UN // LB)]
                ae_ready, ae_kept = sem("ae_ready"), sem("ae_kept")
                assert body % UN == 0

            def body_of(rr, it):
                return rr * ITERS + it

            def step_of(rr, it, i):
                return body_of(rr, it) * S + i

            def step_back(rr, it, i, n):
                return step_of(rr, it, i) - n + 1 - (S - GB if i < n else 0)

            def pair_of(rr, it, u, k):
                return body_of(rr, it) * GT + u * PAIRS + k

            def table_of(rr, it, g):
                return body_of(rr, it) * NG + g

            def only_when(engine, R):
                return engine.If(R < 2) if when == "one" else engine.If(R >= 2) if when == "more" else nullcontext()

            with nc.Block() as block:
                @block.sync
                def _(sp):
                    clear_spent(sp)
                    R = sp.value_load(rounds[0:1, 0:1], min_val=1, max_val=MAX_ROUNDS)

                    def load_batches(rr, it, u, tail):
                        b = it * body + u * LB
                        if u * LB < GB:
                            g = (u + 1) * LB * PAIRS
                            done(sp, used, body_of(rr, it) * GT + (g - GT))
                            settle(sp)
                            load_indices(sp, idx, b, u, idx_in)
                        if edge_terms:
                            done(sp, ae_ready, rr * NB + b + LB - UN)
                            settle(sp)
                            load_edges(sp, "edge_attr_128", ea128, b, u % 2, ea128_in, tail)

                    def tables(rr, it):
                        for g, u in enumerate(build):
                            done(sp, copied, (table_of(rr, it, g) + 1) * CB)
                            settle(sp)
                            sp.dma_start(count_tabs[bass.ds(it, 1), u - (body - DENSE), :, :].rearrange("i p c -> p (i c)"),
                                         built[:, g, :]).then_inc(table_stored[g], 16)
                        for h in range(2) if dense else ():
                            done(sp, copied, (body_of(rr, it) - 1) * 2 + (h + 1))
                            settle(sp)
                            cols = slice(h * (NT // 2) * W, (h + 1) * (NT // 2) * W)
                            sp.dma_start(packed[:, h, :, :], count_tabs[bass.ds(it, 1), :, :, cols]
                                         .rearrange("i g p c -> p (i g) c")).then_inc(packed_in[h], 16)

                    with only_when(sp, R), sp.Fori(0, R) as rr:
                        with sp.Fori(0, ITERS - 1) as it:
                            for u in range(body // LB):
                                load_batches(rr, it, u, False)
                            tables(rr, it)
                        for u in range(body // LB):
                            load_batches(rr, ITERS - 1, u, u == body // LB - 1)
                        tables(rr, ITERS - 1)
                        for s in table_stored if build else ():
                            sp.wait_ge(s, (rr + 1) * (16 * ITERS))
                            settle(sp)

                @block.gpsimd
                def _(pool):
                    R = pool.value_load(rounds[0:1, 0:1], min_val=1, max_val=MAX_ROUNDS)
                    with only_when(pool, R), pool.Fori(0, R) as rr:
                        with pool.Fori(0, ITERS) as it:
                            for u in range(GB):
                                pool.wait_ge(idx_in[u // LB], (rr * ITERS + it + 1) * 16)
                                for k in range(PAIRS):
                                    done(pool, used, pair_of(rr, it, u, k) - GT + 1)
                                    settle(pool)
                                    for c in range(2):
                                        j = 2 * k + c
                                        pool.indirect_dma_start(out=rows[:, u * PAIRS + k, c, :], out_offset=None, in_=table,
                                                                in_offset=bass.IndirectOffsetOnAxis(ap=idx[:, u, j:j + 1], axis=0)
                                                                ).then_inc(rows_in[u * PAIRS + k], 16)

                @block.scalar
                def _(act):
                    if not (weighted or dense):
                        return
                    steps_of(act, copied)
                    if weighted:
                        steps_of(act, used)
                    R = act.value_load(rounds[0:1, 0:1], min_val=1, max_val=MAX_ROUNDS)

                    def scale(rr, it, u):
                        done(act, aux_ready, (body_of(rr, it) * GB + u + 1) * 2)
                        for k in range(PAIRS):
                            i = u * PAIRS + k
                            q = pair_of(rr, it, u, k)
                            act.wait_ge(rows_in[i], (body_of(rr, it) + 1) * 32)
                            done(act, scaled_used, q + 1 - SR)
                            for c in range(2):
                                ins = act.activation(scaled[:, i % SR, c, :], rows[:, i, c, :], ACT.Copy,
                                                     scale=aux[:, u % HR, 2 * k + c, 0:1])
                            ins.then_inc(used, 1)

                    def copy_counts(rr, it, g):
                        d = table_of(rr, it, g)
                        act.wait_ge(table_stored[g], body_of(rr, it) * 16)
                        for h in range(CB):
                            done(act, counted, d * CB + (h + 1))
                            act.copy(built[:, g, h * COLS:(h + 1) * COLS], CNT[h][:, 0:COLS]).then_inc(copied, 1)

                    def unpack_counts(rr, it, h):
                        act.wait_ge(packed_in[h], (body_of(rr, it) + 1) * 16)
                        if h == 0:
                            done(act, half_used, body_of(rr, it))
                        else:
                            done(act, summed, step_of(rr, it, 0))
                        for g in range(dense):
                            ins = act.copy(counts[:, h * (NT // 2):(h + 1) * (NT // 2), g, :],
                                           packed[:, h, g, :].rearrange("p (t w) -> p t w", w=W))
                        ins.then_inc(copied, 1)

                    with only_when(act, R), act.Fori(0, R) as rr:
                        with act.Fori(0, ITERS) as it:
                            for i in range(GB):
                                if weighted:
                                    scale(rr, it, i)
                                if i in count_at:
                                    copy_counts(rr, it, count_at.index(i))
                            for h in range(2) if dense else ():
                                unpack_counts(rr, it, h)

                @block.tensor
                def _(pe):
                    steps_of(pe, summed, counted, half_used, scaled_used if weighted else used)
                    R = pe.value_load(rounds[0:1, 0:1], min_val=1, max_val=MAX_ROUNDS)

                    def count(rr, it, g):
                        d = table_of(rr, it, g)
                        done(pe, prepared, d + 1)
                        for h in range(CB):
                            done(pe, copied, (d - 1) * CB + (h + 1))
                            for j in range(J):
                                mm = pe.matmul(CNT[h][:, 0:COLS], lo[:, j, :], wide[:, j, h * COLS:(h + 1) * COLS],
                                               start=(j == 0), stop=(j == J - 1))
                            mm.then_inc(counted, 1)

                    def sum_gathered(rr, it, i):
                        done(pe, added, body_of(rr, it) * body + i - 1 - (dense if i < 2 else 0))
                        done(pe, hot_ready, body_of(rr, it) * GB + i + 1)
                        if weighted:
                            done(pe, aux_ready, (body_of(rr, it) * GB + i + 1) * 2)
                        for k in range(PAIRS):
                            if weighted:
                                done(pe, used, pair_of(rr, it, i, k) + 1)
                            else:
                                pe.wait_ge(rows_in[i * PAIRS + k], (body_of(rr, it) + 1) * 32)
                            for c in range(2):
                                j, at = 2 * k + c, i * PAIRS + k
                                lhsT = scaled[:, at % SR, c, :] if weighted else rows[:, at, c, :]
                                mm = pe.matmul(SEG[i % 2][:, 0:W], lhsT, hot[:, i % HR, j, :], start=(j == 0),
                                               stop=(j == J - 1), skip_group_check=True)
                            mm.then_inc(scaled_used if weighted else used, 1)
                            if weighted:
                                for c in range(2):
                                    j = 2 * k + c
                                    mm = pe.matmul(SEG[i % 2][0:3, W:2 * W], aux[:, i % HR, j, :], hot[:, i % HR, j, :],
                                                   start=False, stop=(j == J - 1), skip_group_check=True)
                        if weighted:
                            mm.then_inc(summed, 1)
                        else:
                            done(pe, used, pair_of(rr, it, i, PAIRS))
                            pe.sem_inc(summed, 1)

                    def sum_dense(rr, it, i):
                        if i == 1:
                            done(pe, added, body_of(rr, it) * body)
                        for t in range((i - 1) * NT // (GB - 1), i * NT // (GB - 1)):
                            if t % (NT // 2) == 0:
                                done(pe, copied, body_of(rr, it) * 2 + t // (NT // 2) + 1)
                            mm = pe.matmul(SEG_D[:, 0:dense * W], x_from[:, t, :], flat(counts[:, t, :, :]),
                                           start=(t == 0), stop=(t == NT - 1), skip_group_check=True)
                            if t == NT // 2 - 1:
                                mm.then_inc(half_used, 1)
                        if i == GB - 1:
                            mm.then_inc(summed, 1)

                    with only_when(pe, R), pe.Fori(0, R) as rr:
                        with pe.Fori(0, ITERS) as it:
                            for i in range(GB):
                                if i in count_at:
                                    count(rr, it, count_at.index(i))
                                sum_gathered(rr, it, i)
                                if dense and i > 0:
                                    sum_dense(rr, it, i)

                @block.vector
                def _(dve):
                    steps_of(dve, hot_ready, added)
                    if build:
                        steps_of(dve, prepared)
                    if weighted:
                        steps_of(dve, aux_ready)
                    if edge_terms:
                        steps_of(dve, ae_ready, ae_kept)
                    R = dve.value_load(rounds[0:1, 0:1], min_val=1, max_val=MAX_ROUNDS)
                    with only_when(dve, R):
                        dve.memset(acc[:, :], 0.0).then_inc(ready, 1)
                        dve.memset(aux_acc[:, :], 0.0).then_inc(ready, 1)
                        start_windows(dve, windows)
                        dve.wait_ge(ready, 2)

                    def prepare(rr, it, g):
                        d = table_of(rr, it, g)
                        at = bass.ds(it * body + build[g], 1)
                        done(dve, prepared, d)
                        dve.tensor_copy(code_s[:, :], flat(code[:, at, :])).then_inc(staged, 1)
                        done(dve, counted, d * CB)
                        dve.tensor_tensor(lo[:, :, :], lo_iota[:, :].rearrange("p (a n) -> p a n", a=1).broadcast_to([P, J, P]),
                                          src_lo[:, at, :].rearrange("p b (j n) -> p (b j) n", n=1).broadcast_to([P, J, P]),
                                          ALU.is_equal).then_inc(staged, 1)
                        dve.wait_ge(staged, d * 2 + 2)
                        for j in range(J):
                            ins = dve.tensor_scalar(wide[:, j, :], code_iota[:, :], code_s[:, j:j + 1], None, ALU.is_equal)
                        ins.then_inc(prepared, 1)

                    def onehots(rr, it, i):
                        b = it * body + i
                        done(dve, summed, step_back(rr, it, i, HR))
                        if weighted:
                            dve.tensor_copy(aux[:, i % HR, :, 0:2], w_tab[:, bass.ds(b, 1), :, :].rearrange("p b j l -> p (b j) l")).then_inc(aux_ready, 1)
                            dve.tensor_copy(aux[:, i % HR, :, 2:3], ae_tab[:, bass.ds(b, 1), :, weighted - 1:weighted]
                                            .rearrange("p b j l -> p (b j) l")).then_inc(aux_ready, 1)
                        dve.tensor_tensor(hot[:, i % HR, :, :], over_chunks(iota), over_nodes(b), ALU.is_equal).then_inc(hot_ready, 1)

                    def add(rr, it, i):
                        done(dve, summed, step_of(rr, it, i) + 1)
                        if i < GB:
                            b = it * body + i
                            add_window(dve, SEG[i % 2][:, 0:W], SEG[i % 2][:, W:2 * W], b, rr * NB + b, added,
                                       3 if weighted else 0)
                        else:
                            for g in range(dense):
                                b = it * body + GB + g
                                add_window(dve, SEG_D[:, g * W:(g + 1) * W], None, b, rr * NB + b, added, 0)

                    def a_e(rr, it, u, where):
                        b = it * body + u
                        n = rr * NB + b
                        edges_in(dve, ea128_in, rr, it * (body // UN) + u // UN, u // LB % 2,
                                 "last" if where == "last" and u // LB == body // LB - 1 else "body")
                        done(dve, ae_kept, n - 1)
                        done(dve, ae_ready, n - 1)
                        for j in range(J):
                            for l in range(2):
                                ins = dve.tensor_tensor_reduce(out=junk[:, u % 2, 2 * j + l, :], in0=ea128[:, u % UN, j, :],
                                                               in1=ae_w[:, l, :], scale=1.0, scalar=0.0,
                                                               op0=ALU.mult, op1=ALU.add, accum_out=ae[:, u % 2, j, l:l + 1])
                        ins.then_inc(ae_ready, 1)
                        done(dve, ae_ready, n + 1)
                        dve.tensor_copy(ae_tab[:, bass.ds(b, 1), :, :].rearrange("p b j l -> p (b j) l"),
                                        ae[:, u % 2, :, :]).then_inc(ae_kept, 1)

                    def steps(rr, it, where):
                        for i in range(S):
                            if i < GB:
                                onehots(rr, it, i)
                            if i in prepare_at:
                                prepare(rr, it, prepare_at.index(i))
                            if where != "first" or i >= 2:
                                add(rr, it + (-1 if i < 2 else 0), (i - 2) % S)
                            if edge_terms:
                                for u in ([i] if i < GB else range(GB, body)):
                                    a_e(rr, it, u, where)

                    with only_when(dve, R), dve.Fori(0, R) as rr:
                        dve.wait_ge(windows, rr * 3 + 3)
                        steps(rr, 0, "first")
                        with dve.Fori(1, ITERS - 1) as it:
                            steps(rr, it, "body")
                        steps(rr, ITERS - 1, "last")
                        for i in range(S - 2, S):
                            add(rr, ITERS - 1, i)
                        done(dve, hot_ready, (rr + 1) * (GB * ITERS))
                        if build:
                            done(dve, prepared, (rr + 1) * (NG * ITERS))
                        next_windows(dve, windows)

    def turn_aux(pe, k, s):
        for t in range(NT):
            mm = pe.transpose(bank[7][:, t * k:(t + 1) * k], aux_acc[0:k, t * P:(t + 1) * P], ident[0:k, 0:k])
        mm.then_inc(s, 1)

    def aux_nodes(k):
        return bank[7][:, 0:NT * k].rearrange("p (t k) -> p t k", k=k)

    def degrees():
        with phase("degrees") as (sb, sem):
            turned, v, numbered = sem("turned"), sem("v"), sem("numbered")
            loaded, ae_steps = sem("loaded"), sem("ae_steps")
            we_g, we_T, ae_c, ae_row = sb("we_g", [P, 2, P]), sb("we_T", [P, 2, P]), sb("ae_c", [P, 2]), sb("ae_row", [1, 2 * P])
            cnt, start, spare = sb("cnt", [P, NT]), sb("start", [P, NT]), sb("spare", [P, NT])
            columns = flat(y_sb[:, :, :])[:, 0:NT * W]
            src_part = sb("src_part", [P, 2, NB, J], I32)
            src_hi, inside = sb("src_hi", [P, NB, J]), sb("inside", [P, NB, J])
            zero_row, ends_row = flat(h_sb[:, :, :])[0:1, :], flat(w1_sb[:, :, :])[0:1, :]
            with nc.Block() as block:
                @block.sync
                def _(sp):
                    clear_spent(sp)
                    for k in range(2):
                        sp.dma_start(we_g[:, k, :], a[f"L2_gnn_We{k + 1}"]).then_inc(loaded, 16)
                        sp.dma_start(ae_c[:, k:k + 1], a[f"L2_gnn_ae{k + 1}"].rearrange("(p a) -> p a", a=1)).then_inc(loaded, 16)

                @block.gpsimd
                def _(pool):
                    pool.iota(columns, pattern=[[1, NT * W]], base=0, channel_multiplier=0,
                              allow_small_or_imprecise_dtypes=True).then_inc(numbered, 1)
                    pool.iota(spare[:, :], pattern=[[P, NT]], base=NB * BE, channel_multiplier=1,
                              allow_small_or_imprecise_dtypes=True).then_inc(numbered, 1)

                @block.tensor
                def _(pe):
                    turn_aux(pe, 1, turned)
                    pe.wait_ge(v, 2)
                    for t in range(NT):
                        mm = pe.transpose(bank[6][:, t:t + 1], ends_row[:, t * P:(t + 1) * P], ident[0:1, 0:1])
                    mm.then_inc(turned, 1)
                    pe.wait_ge(loaded, 16 * 4)
                    for k in range(2):
                        pe.transpose(bank[k][:, 0:P], we_g[:, k, :], ident[:, :]).then_inc(ae_steps, 1)
                    pe.wait_ge(ae_steps, 4)
                    for k in range(2):
                        pe.matmul(bank[2][0:1, k * P:(k + 1) * P], ae_c[:, k:k + 1], we_T[:, k, :], start=True, stop=True).then_inc(ae_steps, 1)
                    pe.wait_ge(ae_steps, 7)
                    pe.matmul(bank[3][:, 0:2 * P], ones[0:1, :], ae_row[0:1, :], start=True, stop=True).then_inc(ae_steps, 1)

                @block.vector
                def _(dve):
                    link = chain(dve, v)
                    link(dve.memset(zero_row, 0.0))
                    link(dve.tensor_tensor_scan(ends_row, aux_acc[0:1, :], zero_row, 0.0, ALU.add, ALU.add))
                    dve.wait_ge(turned, 1)
                    link(dve.tensor_scalar(cnt[:, :], aux_nodes(1)[:, :, 0], 1.0, None, ALU.max))
                    link(dve.tensor_scalar(has[:, :], aux_nodes(1)[:, :, 0], 1.0, None, ALU.min))
                    link(dve.reciprocal(rdeg[:, :], cnt[:, :]))
                    dve.wait_ge(turned, 2)
                    dve.wait_ge(numbered, 2)
                    link(dve.tensor_copy(start[:, :], bank[6][:, 0:NT]))
                    link(dve.tensor_tensor(start[:, :], start[:, :], aux_nodes(1)[:, :, 0], ALU.subtract))
                    link(dve.tensor_tensor(start[:, :], start[:, :], spare[:, :], ALU.subtract))
                    link(dve.tensor_tensor(start[:, :], start[:, :], has[:, :], ALU.mult))
                    link(dve.tensor_tensor(start[:, :], start[:, :], spare[:, :], ALU.add))
                    link(dve.tensor_copy(seg_start[:, :], start[:, :]))
                    link(dve.tensor_copy(code_iota[:, :], columns))
                    link(dve.tensor_copy(lo_iota[:, :], columns[:, 0:P]))
                    link(dve.tensor_scalar(src_part[:, 0, :, :], src_idx[:, :, :], P - 1, None, ALU.bitwise_and))
                    link(dve.tensor_scalar(src_part[:, 1, :, :], src_idx[:, :, :], 7, None, ALU.logical_shift_right))
                    link(dve.tensor_copy(src_lo[:, :, :], src_part[:, 0, :, :]))
                    link(dve.tensor_copy(src_hi[:, :, :], src_part[:, 1, :, :]))
                    link(dve.scalar_tensor_tensor(out=code[:, :, :], in0=src_hi[:, :, :], scalar=float(W), in1=rel[:, :, :],
                                                  op0=ALU.mult, op1=ALU.add))
                    link(dve.tensor_scalar(inside[:, :, :], rel[:, :, :], float(W), None, ALU.is_lt))
                    link(dve.scalar_tensor_tensor(out=code[:, :, :], in0=code[:, :, :], scalar=1.0, in1=inside[:, :, :],
                                                  op0=ALU.add, op1=ALU.mult))
                    link(dve.tensor_scalar(code[:, :, :], code[:, :, :], -1.0, None, ALU.add))
                    dve.wait_ge(ae_steps, 2)
                    dve.tensor_copy(we_T[:, 0, :], bank[0][:, 0:P]).then_inc(ae_steps, 1)
                    dve.tensor_copy(we_T[:, 1, :], bank[1][:, 0:P]).then_inc(ae_steps, 1)
                    dve.wait_ge(ae_steps, 6)
                    dve.tensor_copy(ae_row[0:1, :], bank[2][0:1, 0:2 * P]).then_inc(ae_steps, 1)
                    dve.wait_ge(ae_steps, 8)
                    link(dve.tensor_copy(flat(ae_w[:, :, :]), bank[3][:, 0:2 * P]))

    def over_tiles(v):
        return v[:, :].rearrange("p (a d) -> p a d", a=1).broadcast_to([P, NT, P])

    def over_features(v):
        return v[:, :].rearrange("p (t d) -> p t d", d=1).broadcast_to([P, NT, P])

    def finish_layer(name, gate=False, affine=None, residual=True, outer=False, store=None):
        with phase(name) as (sb, sem):
            norm, root = norm_steps(sb, sem)
            gb = sb("gb", [P, 2, P])
            loaded, v, sig, fin, stored = sem("loaded"), sem("v"), sem("sig"), sem("fin"), sem("stored")
            result = x_sb if residual else cur
            with nc.Block() as block:
                @block.sync
                def _(sp):
                    clear_spent(sp)
                    if affine:
                        for k in range(2):
                            sp.dma_start(gb[:, k, :], spread(a[affine[k]])).then_inc(loaded, 16)
                    for n, h in enumerate(halves):
                        sp.wait_ge(fin, n + 1)
                        if outer:
                            full = slice(h.start, min(h.stop, FT))
                            sp.dma_start(by_tile(out[full.start * P:full.stop * P, :]), result[:, full, :]).then_inc(stored, 16)
                        elif store is not None:
                            sp.dma_start(by_tile(store[h.start * P:h.stop * P, :]), result[:, h, :]).then_inc(stored, 16)
                    if outer:
                        sp.dma_start(out[FT * P:N, :], result[0:FR, FT, :]).then_inc(stored, 16)
                        sp.wait_ge(stored, 48)
                    elif store is not None:
                        sp.wait_ge(stored, 32)

                @block.scalar
                def _(act):
                    if gate:
                        act.activation(flat(w1_sb[:, :, :]), flat(y_sb[:, :, :]), ACT.Sigmoid).then_inc(sig, 1)
                    for n in range((affine is not None) + residual):
                        root(act, n)

                @block.vector
                def _(dve):
                    link = chain(dve, v)
                    if gate:
                        dve.wait_ge(sig, 1)
                        link(dve.tensor_tensor(y_sb[:, :, :], y_sb[:, :, :], w1_sb[:, :, :], ALU.mult))
                    if affine:
                        norm(dve, link, y_sb, y_sb)
                        dve.wait_ge(loaded, 32)
                        link(dve.tensor_tensor(y_sb[:, :, :], y_sb[:, :, :], over_tiles(gb[:, 0, :]), ALU.mult))
                        link(dve.tensor_tensor(y_sb[:, :, :], y_sb[:, :, :], over_tiles(gb[:, 1, :]), ALU.add))
                        for h in halves:
                            link(dve.tensor_scalar((y_sb if residual else cur)[:, h, :], y_sb[:, h, :], 0.0, None, ALU.max))
                            if not residual:
                                dve.sem_inc(fin, 1)
                    if residual:
                        link(dve.tensor_tensor(y_sb[:, :, :], y_sb[:, :, :], x_sb[:, :, :], ALU.add))
                        norm(dve, link, y_sb, x_sb, fin)

    def attend(l, table, a_s, a_d):
        ROWS = 4
        with phase(f"attend{l}") as (sb, sem):
            att = sb("att", [P, 2, P])
            res = sb("res", [P, NT])
            tab = sb("tab", [P, P], BF16)
            hik, hi_off = sb("hik", [P, 1]), sb("hi_off", [P, 2])
            pick = sb("pick", [P, 2 * P - 1], BF16)
            ids = sb("ids", [P, ROWS, LB, 2, BE], BF16)
            hot_lo, found = sb("hot_lo", [P, 2, LB, BE], BF16), sb("found", [P, 2, LB, BE], BF16)
            ae_s, alpha, ad_in = sb("ae_s", [NB, BE]), sb("alpha", [NB, BE]), sb("ad_in", [NB, BE])
            run, seg_max, ex, ml = sb("run", [NB, BE]), sb("seg_max", [NB, BE]), sb("ex", [NB, BE]), sb("ml", [NB, BE])
            pass_row, end_row, carry_row = sb("pass_row", [1, NB]), sb("end_row", [1, NB]), sb("carry_row", [1, NB + 1])
            carry = sb("carry", [NB, 1])
            loaded, stored, v, t, consts = sem("loaded"), sem("stored"), sem("v"), sem("t"), sem("consts")
            scanned, carried, shifted, weighed = sem("scanned"), sem("carried"), sem("shifted"), sem("weighed")
            max_ready = sem("max_ready")
            times_ad, ad_ready, ad_loaded = sem("times_ad"), sem("ad_ready"), sem("ad_loaded")
            scattered = kept_sem(f"attend{l}_scattered")
            ids_in = [sem(f"ids_in{i}") for i in range(ROWS)]
            hot_ready, found_ready, looked, picked = sem("hot_ready"), sem("found_ready"), sem("looked"), sem("picked")
            NL = NB // LB
            TURNS = NL // ROWS
            assert NL % ROWS == 0 and LB == 2 and BE <= 512
            OUT = bank[4]

            with nc.Block() as block:
                @block.sync
                def _(sp):
                    clear_spent(sp)
                    for k, side in enumerate("sd"):
                        sp.dma_start(att[:, k, :], spread(a[f"L2_gnn_a{l}{side}"])).then_inc(loaded, 16)
                    sp.dma_start(by_tile(table), h_sb[:, :, :]).then_inc(stored, 16)
                    with sp.Fori(0, TURNS) as it:
                        for r in range(ROWS):
                            done(sp, found_ready, it * ROWS + r - ROWS + 1)
                            settle(sp)
                            sp.dma_start(ids[:, r, :, :, :].rearrange("p b k e -> p (b k e)"),
                                         id_rows[bass.ds((it * ROWS + r) * LB, LB), :, :]
                                         .rearrange("b k e -> (b k e)").rearrange("(a n) -> a n", a=1)
                                         .broadcast_to([P, LB * 2 * BE])).then_inc(ids_in[r], 16)
                    sp.wait_ge(scattered, 16 * NT)
                    sp.dma_start(ad_in[:, :], first_ad[0:NB * BE, :].rearrange("(b e) a -> b (e a)", e=BE)).then_inc(ad_loaded, 16)
                    sp.wait_ge(stored, 16)

                @block.gpsimd
                def _(pool):
                    pool.wait_ge(loaded, 32)
                    pool.tensor_tensor(y_sb[:, :, :], h_sb[:, :, :], over_tiles(att[:, 1, :]), ALU.mult).then_inc(times_ad, 1)
                    pool.wait_ge(ad_ready, 1)
                    for n in range(NT):
                        pool.indirect_dma_start(out=first_ad,
                                                out_offset=bass.IndirectOffsetOnAxis(ap=seg_start[:, n:n + 1], axis=0),
                                                in_=a_d[:, n:n + 1], in_offset=None).then_inc(scattered, 16)

                @block.tensor
                def _(pe):
                    steps_of(pe, looked, picked)
                    for j in range(J):
                        mm = pe.transpose(bank[6][0:NB, j * P:(j + 1) * P], ae_tab[:, :, j, l - 1], ident[:, :])
                    mm.then_inc(t, 1)
                    pe.wait_ge(consts, 1)
                    pe.matmul(OUT[:, :], pick[:, 0:P], found[:, 0, 0, :], start=True, stop=False, skip_group_check=True)

                    def tick(it, i, where):
                        if (w := lagged(i, 0, where, ROWS)):
                            m, back = w
                            b = (it + back) * ROWS + m
                            done(pe, hot_ready, b + 1)
                            done(pe, found_ready, b - 1)
                            for h in range(LB):
                                mm = pe.matmul(bank[2 * (m % 2) + h][:, :], tab[:, :], hot_lo[:, m % 2, h, :],
                                               start=True, stop=True)
                            mm.then_inc(looked, 1)
                        if (w := lagged(i, 1, where, ROWS)):
                            m, back = w
                            b = (it + back) * ROWS + m
                            done(pe, found_ready, b + 1)
                            for h in range(LB):
                                mm = pe.matmul(OUT[:, :], pick[:, bass.ds(b * (-LB) + (P - 1 - h), P)],
                                               found[:, m % 2, h, :], start=False, stop=where == "tail" and h == LB - 1,
                                               skip_group_check=True)
                            mm.then_inc(picked, 1)

                    for i in range(ROWS):
                        tick(0, i, "first")
                    with pe.Fori(1, TURNS) as it:
                        for i in range(ROWS):
                            tick(it, i, "body")
                    tick(TURNS, 0, "tail")
                    for n, (end, through) in enumerate(((run[:, BE - 1:BE], pass_f), (run[:, BE - 1:BE], pass_f),
                                                        (seg_max[:, 0:1], pass_b))):
                        at = n // 2
                        pe.wait_ge(scanned, n + 1)
                        pe.transpose(bank[0][0:1, 0:NB], end, ident[0:NB, 0:NB])
                        pe.transpose(bank[0][0:1, P:P + NB], through[:, :], ident[0:NB, 0:NB]).then_inc(t, 1)
                        pe.wait_ge(carried, n + 1)
                        pe.transpose(bank[0][0:NB, 2 * P:2 * P + 1], carry_row[0:1, at:at + NB], ident[0:1, 0:1]).then_inc(t, 1)
                    for n, (frm, s) in enumerate(((ml, max_ready), (ex, weighed))):
                        pe.wait_ge(s, 1)
                        for j in range(J):
                            mm = pe.transpose(bank[2 + n][:, j * NB:(j + 1) * NB], frm[:, j:BE:J], ident[0:NB, 0:NB])
                        mm.then_inc(t, 1)

                @block.scalar
                def _(act):
                    act.wait_ge(shifted, 1)
                    act.activation(ex[:, :], run[:, :], ACT.Exp).then_inc(weighed, 1)

                @block.vector
                def _(dve):
                    steps_of(dve, hot_ready, found_ready)
                    link = chain(dve, v)
                    link(dve.memset(tab[:, :], 0.0))
                    link(dve.memset(found[:, :, :, :], 0.0))
                    link(dve.memset(pick[:, :], 0.0))
                    link(dve.memset(pick[:, P - 1:P], 1.0))
                    for n in range(2):
                        link(dve.tensor_scalar(hi_off[:, n:n + 1], part0[:, :], float((n + 1) * NT), -float(NT), ALU.is_ge, ALU.mult))
                    link(dve.tensor_tensor(hik[:, :], part0[:, :], hi_off[:, 0:1], ALU.add))
                    link(dve.tensor_tensor(hik[:, :], hik[:, :], hi_off[:, 1:2], ALU.add))
                    dve.wait_ge(loaded, 32)
                    link(dve.tensor_tensor(w1_sb[:, :, :], h_sb[:, :, :], over_tiles(att[:, 0, :]), ALU.mult))
                    link(dve.tensor_reduce(a_s[:, :], w1_sb[:, :, :], AX, ALU.add))
                    link(dve.tensor_copy(tab[:, 0:NT], a_s[:, :]))
                    link(dve.tensor_tensor(res[:, :], a_s[:, :], tab[:, 0:NT], ALU.subtract))
                    link(dve.tensor_copy(tab[:, NT:2 * NT], res[:, :]))
                    link(dve.tensor_tensor(res[:, :], res[:, :], tab[:, NT:2 * NT], ALU.subtract))
                    link(dve.tensor_copy(tab[:, 2 * NT:3 * NT], res[:, :]))
                    dve.sem_inc(consts, 1)

                    def tick(it, i, where):
                        if (w := lagged(i, 0, where, ROWS)):
                            m, back = w
                            b = (it + back) * ROWS + m
                            dve.wait_ge(ids_in[m], (it + back + 1) * 16)
                            done(dve, looked, b - 1)
                            dve.tensor_scalar(hot_lo[:, m % 2, :, :], ids[:, m, :, 0, :], part0[:, 0:1], None,
                                              ALU.is_equal).then_inc(hot_ready, 1)
                        if (w := lagged(i, 1, where, ROWS)):
                            m, back = w
                            b = (it + back) * ROWS + m
                            done(dve, looked, b + 1)
                            done(dve, picked, b - 1)
                            for h in range(LB):
                                ins = dve.scalar_tensor_tensor(out=found[:, m % 2, h, :], in0=ids[:, m, h, 1, :],
                                                               scalar=hik[:, 0:1], in1=bank[2 * (m % 2) + h][:, :],
                                                               op0=ALU.is_equal, op1=ALU.mult)
                            ins.then_inc(found_ready, 1)

                    for i in range(ROWS):
                        tick(0, i, "first")
                    dve.wait_ge(times_ad, 1)
                    link(dve.tensor_reduce(a_d[:, :], y_sb[:, :, :], AX, ALU.add))
                    dve.sem_inc(ad_ready, 1)
                    dve.wait_ge(t, 1)
                    link(dve.tensor_copy(ae_s[:, :].rearrange("b (p j) -> b j p", j=J),
                                         bank[6][0:NB, :].rearrange("b (j p) -> b j p", p=P)))
                    with dve.Fori(1, TURNS) as it:
                        for i in range(ROWS):
                            tick(it, i, "body")
                    tick(TURNS, 0, "tail")

                    rev = slice(None, None, -1)
                    fwd = slice(None)

                    def spread_max(n, to, pen, frm, way):
                        link(dve.tensor_tensor_scan(to[:, way], pen[:, way], frm[:, way], -BIG, ALU.add, ALU.max))
                        dve.sem_inc(scanned, 1)
                        dve.wait_ge(t, 2 + 2 * n)
                        link(dve.tensor_copy(end_row[:, :], bank[0][0:1, 0:NB]))
                        link(dve.tensor_copy(pass_row[:, :], bank[0][0:1, P:P + NB]))
                        link(dve.memset(carry_row[:, :], -BIG))
                        carries = carry_row[:, 1:NB + 1] if way is fwd else carry_row[:, 0:NB]
                        link(dve.tensor_tensor_scan(carries[:, way], pass_row[:, way], end_row[:, way], -BIG, ALU.add, ALU.max))
                        dve.sem_inc(carried, 1)
                        dve.wait_ge(t, 3 + 2 * n)
                        link(dve.tensor_copy(carry[:, :], bank[0][0:NB, 2 * P:2 * P + 1]))
                        link(dve.tensor_tensor_scan(to[:, way], pen[:, way], frm[:, way], carry[:, 0:1], ALU.add, ALU.max))

                    dve.wait_ge(ad_loaded, 16)
                    spread_max(0, run, pen_f, ad_in, fwd)
                    link(dve.tensor_tensor(ae_s[:, :], ae_s[:, :], run[:, :], ALU.add))
                    done(dve, picked, NL)
                    link(dve.tensor_tensor(alpha[:, :], ae_s[:, :], OUT[0:NB, :], ALU.add))
                    link(dve.scalar_tensor_tensor(out=alpha[:, :], in0=alpha[:, :], scalar=SLOPE, in1=alpha[:, :], op0=ALU.mult, op1=ALU.max))
                    spread_max(1, run, pen_f, alpha, fwd)
                    spread_max(2, seg_max, pen_b, run, rev)
                    link(dve.tensor_tensor(run[:, :], alpha[:, :], seg_max[:, :], ALU.subtract))
                    dve.sem_inc(shifted, 1)
                    link(dve.tensor_tensor(ml[:, :], seg_max[:, :], last[:, :], ALU.mult))
                    dve.sem_inc(max_ready, 1)
                    for n in range(2):
                        dve.wait_ge(t, 8 + n)
                        dve.tensor_copy(w_tab[:, :, :, 1 - n], bank[2 + n][:, 0:NB * J].rearrange("p (j b) -> p b j", b=NB)).then_inc(consts, 1)

    def settle_attention(l, a_s, a_d):
        with phase(f"gat{l}") as (sb, sem):
            m, al, M = sb("m", [P, NT]), sb("al", [P, NT]), sb("M", [P, NT])
            both = sb("both", [P, 2, NT])
            den, bias = sb("den", [P, NT]), sb("bias", [P, P])
            gs = sb("gs", [P, 2, P])
            loaded, v, turned, exp_ready, ready = sem("loaded"), sem("v"), sem("turned"), sem("exp_ready"), sem("ready")
            staged, flipped, copied = sem("staged"), sem("flipped"), sem("copied")
            with nc.Block() as block:
                @block.sync
                def _(sp):
                    clear_spent(sp)
                    sp.dma_start(bias[:, :], spread(a[f"L2_gnn_b{l}"])).then_inc(loaded, 16)

                @block.gpsimd
                def _(pool):
                    steps_of(pool, staged)
                    with pool.Fori(0, NT // 2) as it:
                        for u in range(2):
                            done(pool, flipped, it * 2 + (u - 1))
                            pool.tensor_copy(gs[:, u, :], acc[:, bass.ds(it * (2 * P) + u * P, P)]).then_inc(staged, 1)

                @block.tensor
                def _(pe):
                    steps_of(pe, flipped)
                    turn_aux(pe, 3, turned)
                    with pe.Fori(0, NT // 2) as it:
                        for u in range(2):
                            done(pe, staged, it * 2 + (u + 1))
                            done(pe, copied, it * 2 + (u - 1))
                            pe.transpose(bank[u][:, 0:P], gs[:, u, :], ident[:, :]).then_inc(flipped, 1)

                @block.scalar
                def _(act):
                    steps_of(act, copied)
                    with act.Fori(0, NT // 2) as it:
                        for u in range(2):
                            done(act, flipped, it * 2 + (u + 1))
                            act.copy(flat(w1_sb[:, bass.ds(it * 2 + u, 1), :]), bank[u][:, 0:P]).then_inc(copied, 1)
                    act.wait_ge(ready, 1)
                    act.activation(flat(both[:, :, :]), flat(both[:, :, :]), ACT.Exp).then_inc(exp_ready, 1)

                @block.vector
                def _(dve):
                    link = chain(dve, v)
                    link(dve.tensor_tensor(al[:, :], a_s[:, :], a_d[:, :], ALU.add))
                    dve.wait_ge(turned, 1)
                    link(dve.tensor_tensor(M[:, :], aux_nodes(3)[:, :, 2], rdeg[:, :], ALU.mult))
                    link(dve.tensor_tensor(al[:, :], al[:, :], M[:, :], ALU.add))
                    link(dve.scalar_tensor_tensor(out=al[:, :], in0=al[:, :], scalar=SLOPE, in1=al[:, :], op0=ALU.mult, op1=ALU.max))
                    link(dve.tensor_scalar(M[:, :], has[:, :], -1.0, BIG, ALU.add, ALU.mult))
                    link(dve.tensor_tensor(m[:, :], M[:, :], aux_nodes(3)[:, :, 1], ALU.add))
                    link(dve.tensor_tensor(M[:, :], m[:, :], al[:, :], ALU.max))
                    link(dve.tensor_tensor(both[:, 0, :], m[:, :], M[:, :], ALU.subtract))
                    link(dve.tensor_tensor(both[:, 1, :], al[:, :], M[:, :], ALU.subtract))
                    dve.sem_inc(ready, 1)
                    dve.wait_ge(exp_ready, 1)
                    link(dve.tensor_tensor(den[:, :], aux_nodes(3)[:, :, 0], both[:, 0, :], ALU.mult))
                    link(dve.tensor_tensor(den[:, :], den[:, :], both[:, 1, :], ALU.add))
                    link(dve.reciprocal(den[:, :], den[:, :]))
                    for n in range(2):
                        link(dve.tensor_tensor(both[:, n, :], both[:, n, :], den[:, :], ALU.mult))
                    done(dve, copied, NT)
                    dve.wait_ge(loaded, 16)
                    link(dve.tensor_tensor(y_sb[:, :, :], w1_sb[:, :, :], over_features(both[:, 0, :]), ALU.mult))
                    link(dve.tensor_tensor(w1_sb[:, :, :], h_sb[:, :, :], over_features(both[:, 1, :]), ALU.mult))
                    link(dve.tensor_tensor(y_sb[:, :, :], y_sb[:, :, :], w1_sb[:, :, :], ALU.add))
                    link(dve.tensor_tensor(y_sb[:, :, :], y_sb[:, :, :], over_tiles(bias), ALU.add))
                    if l == 1:
                        link(dve.tensor_scalar(cur[:, :, :], y_sb[:, :, :], 0.0, None, ALU.max))

    prologue()
    node_loop("edge_tables", x_sb,
              [(wide_w[:, 0:P], a["L0_gnn_w1"][0:P, :]), (wide_w[:, P:2 * P], a["L0_gnn_wg"][0:P, :]),
               (wide_w[:, 2 * P:3 * P], a["L0_gnn_w1"][P:2 * P, :]), (wide_w[:, 3 * P:4 * P], a["L0_gnn_wg"][P:2 * P, :]),
               (wide_b[:, 0:P], row(a["L0_gnn_b1"])), (wide_b[:, P:2 * P], row(a["L0_gnn_bg"]))],
              4 * P, bias=True, stores=[(p_tab, 0), (q_tab, 2 * P)])
    gated_pass()
    degrees()
    node_loop("update0", x_sb, [(wide_w[:, 0:P], a["L0_gnn_wu"][0:P, :]), (wide_w[:, P:2 * P], a["L0_gnn_wu"][P:2 * P, :]),
                                (wide_b[:, 0:P], row(a["L0_gnn_bu"]))], P, bias=True, agg=True, dest=y_sb)
    finish_layer("norm0", gate=True, store=tables[0])

    edge_pass("mean1", tables[0], body=UN, edge_terms=True)
    node_loop("update1", x_sb, [(wide_w[:, 0:P], a["L1_gnn_W_self"]), (wide_w[:, P:2 * P], a["L1_gnn_W_neigh"]),
                                (wide_b[:, 0:P], row(a["L1_gnn_b_self"]))], P, bias=True, agg=True, dest=y_sb)
    finish_layer("norm1")

    a_s, a_d = sb("a_s", [P, NT]), sb("a_d", [P, NT])
    for l in (1, 2):
        node_loop(f"hidden{l}", x_sb if l == 1 else cur, [(wide_w[:, 0:P], a[f"L2_gnn_W{l}"])], P, dest=h_sb)
        attend(l, tables[l], a_s, a_d)
        edge_pass(f"attention{l}", tables[l], body=DENSE_BODY, weighted=l,
                  build=(4, 5) if l == 1 else (6, 7), prepare_at=(0, 2), count_at=(1, 4))
        settle_attention(l, a_s, a_d)
    finish_layer("norm2", store=tables[3])

    for l in range(2):
        edge_pass(f"mean3{l}", tables[3 + l], body=DENSE_BODY, dense=DENSE, x_from=x_sb if l == 0 else cur, when="one")
        edge_pass(f"mean3{l}r", tables[3 + l], body=UN, when="more")
        node_loop(f"update3{l}", x_sb if l == 0 else cur,
                  [(wide_w[:, 0:P], a[f"L3_gnn_W_r{l}"]), (wide_w[:, P:2 * P], a[f"L3_gnn_W_l{l}"]),
                   (wide_b[:, 0:P], row(a[f"L3_gnn_b_l{l}"]))], P, bias=True, turn=(0, 1), agg=True, dest=y_sb)
        finish_layer(f"norm3{l}", affine=(f"L3_gnn_gamma{l}", f"L3_gnn_beta{l}"), residual=l == 1, outer=l == 1,
                     store=tables[4] if l == 0 else None)
    ctx.close()


_INS = ["x", "src", "dst", "edge_attr_128", "edge_attr_64"] \
    + [f"L0_gnn_{n}" for n in ("w1", "b1", "w2", "b2", "wg", "bg", "wu", "bu")] \
    + [f"L1_gnn_{n}" for n in ("W_neigh", "W_self", "b_self")] \
    + [f"L2_gnn_{n}{l}" for l in (1, 2) for n in ("W", "We", "ae", "b")] + [f"L2_gnn_a{l}{s}" for l in (1, 2) for s in "sd"] \
    + [f"L3_gnn_{n}{l}" for l in range(2) for n in ("W_l", "b_l", "W_r", "gamma", "beta")]


def kernel(**inputs):
    import numpy as _np
    import concourse.bacc as _bacc
    from concourse import mybir as _mybir
    from concourse.bass_utils import run_bass_kernel_spmd as _run

    nc = _bacc.Bacc("TRN2", target_bir_lowering=False, num_devices=1)
    arrays, args = {}, {}
    for name in _INS:
        v = _np.ascontiguousarray(inputs[name])
        arrays[f"in_{name}_dram"] = v
        args[name] = nc.dram_tensor(f"in_{name}_dram", v.shape, _mybir.dt.from_np(v.dtype), kind="ExternalInput").ap()
    out = nc.dram_tensor("out_0_dram", args["x"].shape, _mybir.dt.float32, kind="ExternalOutput").ap()
    build_program(nc, args, out)
    r = _run(nc, [arrays], core_ids=[0])
    return r.results[0]["out_0_dram"]
```
